# Optimizing a Trainium2 kernel written in Bass

```python
import numpy as np
import jax
import jax.numpy as jnp

def _softmax(x, axis=-1):
    return jax.nn.softmax(x, axis=axis)

def _gelu(x):
    return jax.nn.gelu(x, approximate=True)

def _silu(x):
    return jax.nn.silu(x)

def _sigmoid(x):
    return jax.nn.sigmoid(x)

def _layernorm(x, axis=-1, eps=1e-05):
    m = jnp.mean(x, axis=axis, keepdims=True)
    v = jnp.var(x, axis=axis, keepdims=True)
    return (x - m) / jnp.sqrt(v + eps)

def _scatter_add(tgt, idx, src, axis=0):
    return tgt.at[idx].add(src)

def _segment_sum(src, seg, n):
    return jax.ops.segment_sum(src, seg, n)
kernel_name = 'mk_vit_tower_d2_tok_img256_r4_139c4f'

def setup_inputs(seed: int=0):
    np.random.seed(seed)
    _w = jnp.asarray

    def _rec_inputs():
        import jax
        import jax.numpy as jnp
        _rk = jax.random.key(seed)
        x = -7.10856e-05 + 0.999911 * jax.random.normal(jax.random.fold_in(_rk, 1), (4, 64, 128, 64), jnp.float32)
        return x
    x = _rec_inputs()

    def _L0_tok_setup():
        import jax, jax.numpy as jnp
        import numpy as np
        PATCH_LEN = 16
        STRIDE = 8
        PAD = 8
        key = jax.random.key(seed)
        k1, k2 = jax.random.split(key)
        x = jax.random.normal(k1, (32, 64, 128, 64), dtype=jnp.float32)
        in_feat = 64 * (PATCH_LEN // 2 + 1) * 2
        W = jax.random.normal(k2, (64, in_feat), dtype=jnp.float32) * 0.02
        return {'x': x, 'W': W}
    _L0_tok_all = _L0_tok_setup()
    _L0_tok_in = {k: v for k, v in _L0_tok_all.items() if k in ('W',)}
    del _L0_tok_all

    def _L0_attn_setup():
        import jax, jax.numpy as jnp
        import numpy as np
        key = jax.random.key(seed)
        k1, k2 = jax.random.split(key)
        B, N, D = (4, 1024, 64)
        inp = jax.random.normal(k1, (B, N, D), dtype=jnp.float32)
        q_weight = jax.random.normal(k2, (D, D), dtype=jnp.float32)
        return {'input': inp, 'q_weight': q_weight}
    _L0_attn_all = _L0_attn_setup()
    _L0_attn_in = {k: v for k, v in _L0_attn_all.items() if k in ('q_weight',)}
    del _L0_attn_all

    def _L0_ffn_setup():
        import jax, jax.numpy as jnp
        import numpy as np
        B, T, IN_DIM = (64, 64, 64)
        HID, OUT_DIM = (128, 64)
        N_LAYERS, N_EXPERTS, N_SHARED = (2, 16, 1)
        key = jax.random.key(seed)
        ks = jax.random.split(key, 10)
        s = 0.02
        x = jax.random.normal(ks[0], (B, T, IN_DIM), dtype=jnp.float32)
        route_id = jax.random.randint(ks[1], (B,), 0, N_EXPERTS)
        Wi = jax.random.normal(ks[2], (HID, IN_DIM), dtype=jnp.float32) * s
        bi = jnp.zeros((HID,), dtype=jnp.float32)
        Wr = jax.random.normal(ks[3], (N_LAYERS, N_EXPERTS, HID, HID), dtype=jnp.float32) * s
        br = jax.random.normal(ks[4], (N_LAYERS, N_EXPERTS, HID), dtype=jnp.float32) * s
        Ws = jax.random.normal(ks[5], (N_LAYERS, N_SHARED, HID, HID), dtype=jnp.float32) * s
        bs = jax.random.normal(ks[6], (N_LAYERS, N_SHARED, HID), dtype=jnp.float32) * s
        Wo = jax.random.normal(ks[7], (OUT_DIM, HID), dtype=jnp.float32) * s
        bo = jnp.zeros((OUT_DIM,), dtype=jnp.float32)
        return {'x': x, 'route_id': route_id, 'Wi': Wi, 'bi': bi, 'Wr': Wr, 'br': br, 'Ws': Ws, 'bs': bs, 'Wo': Wo, 'bo': bo}
    _L0_ffn_all = _L0_ffn_setup()
    _L0_ffn_in = {k: v for k, v in _L0_ffn_all.items() if k in ('route_id', 'Wi', 'bi', 'Wr', 'br', 'Ws', 'bs', 'Wo', 'bo')}
    del _L0_ffn_all

    def _L1_attn_setup():
        import math
        import jax
        import jax.numpy as jnp
        import numpy as np
        from jax import lax
        D_MODEL = 64
        N = 64
        L = 512
        BATCH = 8
        DT = 0.1
        key = jax.random.key(seed)
        k1, k2, k3, k4 = jax.random.split(key, 4)
        n2 = N // 2
        A_real = jnp.log(jnp.ones((D_MODEL, n2), jnp.float32) * 0.5)
        A_imag = jnp.broadcast_to(jnp.arange(n2, dtype=jnp.float32) * math.pi, (D_MODEL, n2))
        C_real = jax.random.normal(k1, (D_MODEL, n2), jnp.float32)
        C_imag = jax.random.normal(k2, (D_MODEL, n2), jnp.float32)
        D = jnp.zeros((D_MODEL,), jnp.float32)
        u = jax.random.normal(k3, (BATCH, L, D_MODEL), jnp.float32)
        return {'u': u, 'A_real': A_real, 'A_imag': A_imag, 'C_real': C_real, 'C_imag': C_imag, 'D': D}
    _L1_attn_all = _L1_attn_setup()
    _L1_attn_in = {k: v for k, v in _L1_attn_all.items() if k in ('A_real', 'A_imag', 'C_real', 'C_imag', 'D')}
    del _L1_attn_all

    def _L1_ffn_setup():
        import jax, jax.numpy as jnp
        import numpy as np
        NUM_EXPERTS = 8
        TOP_K = 2
        B, S, D = (8, 2048, 64)

        def _moe(tokens, router_w, w1, b1, w2, b2):
            N = tokens.shape[0]
            E = router_w.shape[0]
            logits = tokens.astype(jnp.float32) @ router_w.astype(jnp.float32).T
            probs = jax.nn.softmax(logits, axis=-1)
            rw, re = jax.lax.top_k(probs, TOP_K)
            if TOP_K > 1:
                rw = rw / jnp.maximum(rw.sum(-1, keepdims=True), 1e-12)
            rw = rw.astype(tokens.dtype)
            combine = jnp.zeros((N, E), tokens.dtype).at[jnp.arange(N)[:, None], re].set(rw)
            out = tokens
            for e in range(E):
                h = jax.nn.gelu(tokens @ w1[e] + b1[e], approximate=False)
                y = h @ w2[e] + b2[e]
                out = out + combine[:, e:e + 1] * y
            return out
        key = jax.random.key(seed)
        ks = jax.random.split(key, 4)
        scale = 1.0 / np.sqrt(D).astype(np.float32)
        return {'input_embeddings': jax.random.normal(ks[0], (B, S, D), jnp.float32), 'router_w': jax.random.normal(ks[1], (NUM_EXPERTS, D), jnp.float32) * scale, 'w1': jax.random.normal(ks[2], (NUM_EXPERTS, D, D), jnp.float32) * scale, 'b1': jnp.zeros((NUM_EXPERTS, D), jnp.float32), 'w2': jax.random.normal(ks[3], (NUM_EXPERTS, D, D), jnp.float32) * scale, 'b2': jnp.zeros((NUM_EXPERTS, D), jnp.float32)}
    _L1_ffn_all = _L1_ffn_setup()
    _L1_ffn_in = {k: v for k, v in _L1_ffn_all.items() if k in ('router_w', 'w1', 'b1', 'w2', 'b2')}
    del _L1_ffn_all
    return {'x': x, 'L0_tok_W': _L0_tok_in['W'], 'L0_attn_q_weight': _L0_attn_in['q_weight'], 'L0_ffn_route_id': _L0_ffn_in['route_id'], 'L0_ffn_Wi': _L0_ffn_in['Wi'], 'L0_ffn_bi': _L0_ffn_in['bi'], 'L0_ffn_Wr': _L0_ffn_in['Wr'], 'L0_ffn_br': _L0_ffn_in['br'], 'L0_ffn_Ws': _L0_ffn_in['Ws'], 'L0_ffn_bs': _L0_ffn_in['bs'], 'L0_ffn_Wo': _L0_ffn_in['Wo'], 'L0_ffn_bo': _L0_ffn_in['bo'], 'L1_attn_A_real': _L1_attn_in['A_real'], 'L1_attn_A_imag': _L1_attn_in['A_imag'], 'L1_attn_C_real': _L1_attn_in['C_real'], 'L1_attn_C_imag': _L1_attn_in['C_imag'], 'L1_attn_D': _L1_attn_in['D'], 'L1_ffn_router_w': _L1_ffn_in['router_w'], 'L1_ffn_w1': _L1_ffn_in['w1'], 'L1_ffn_b1': _L1_ffn_in['b1'], 'L1_ffn_w2': _L1_ffn_in['w2'], 'L1_ffn_b2': _L1_ffn_in['b2']}

def reference(x, L0_tok_W, L0_attn_q_weight, L0_ffn_route_id, L0_ffn_Wi, L0_ffn_bi, L0_ffn_Wr, L0_ffn_br, L0_ffn_Ws, L0_ffn_bs, L0_ffn_Wo, L0_ffn_bo, L1_attn_A_real, L1_attn_A_imag, L1_attn_C_real, L1_attn_C_imag, L1_attn_D, L1_ffn_router_w, L1_ffn_w1, L1_ffn_b1, L1_ffn_w2, L1_ffn_b2):
    import jax
    import jax.numpy as jnp

    def _L0_tok_ref(x, W):
        import jax, jax.numpy as jnp
        import numpy as np
        PATCH_LEN = 16
        STRIDE = 8
        PAD = 8
        B, C, T, V = x.shape
        xp = jnp.pad(x, ((0, 0), (0, 0), (0, PAD), (0, 0)), mode='edge')
        Tp = T + PAD
        N = (Tp - PATCH_LEN) // STRIDE + 1
        idx = jnp.arange(N)[:, None] * STRIDE + jnp.arange(PATCH_LEN)[None, :]
        patches = xp[:, :, idx, :]
        patches = jnp.transpose(patches, (0, 4, 2, 3, 1))
        xf = jnp.fft.rfft(patches, axis=-2, norm='ortho')
        F = xf.shape[-2]
        x_real = xf.real.reshape(B, V, N, F * C)
        x_imag = xf.imag.reshape(B, V, N, F * C)
        x_emb = jnp.concatenate([x_real, x_imag], axis=-1)
        x_emb = x_emb @ W.T
        return x_emb.reshape(B, V * N, -1)

    def _L0_attn_ref(input, q_weight):
        import jax, jax.numpy as jnp
        import numpy as np
        query = jnp.einsum('bnd,de->bne', input, q_weight)
        att = jax.nn.sigmoid(jnp.einsum('bnd,bmd->bnm', query, input))
        value = jnp.einsum('bnm,bmd->bnd', att, input)
        return value

    def _L0_ffn_ref(x, route_id, Wi, bi, Wr, br, Ws, bs, Wo, bo):
        import jax, jax.numpy as jnp
        import numpy as np
        B, T, IN_DIM = (64, 64, 64)
        HID, OUT_DIM = (128, 64)
        N_LAYERS, N_EXPERTS, N_SHARED = (2, 16, 1)
        flat = x.reshape(-1, x.shape[-1])
        n_tok = flat.shape[0]
        route = jnp.repeat(route_id, n_tok // route_id.shape[0])
        h = jax.nn.relu(flat @ Wi.T + bi)
        n_layers, n_experts = (Wr.shape[0], Wr.shape[1])
        for l in range(n_layers):
            shared = (jnp.einsum('nd,shd->snh', h, Ws[l]) + bs[l][:, None, :]).mean(axis=0)
            routed = jnp.zeros_like(h)
            for e in range(n_experts):
                ye = h @ Wr[l, e].T + br[l, e]
                routed = routed + jnp.where((route == e)[:, None], ye, 0.0)
            h = jax.nn.relu(shared + routed + h)
        out = h @ Wo.T + bo
        return out.reshape(*x.shape[:-1], out.shape[-1])

    def _L1_attn_ref(u, A_real, A_imag, C_real, C_imag, D):
        import math
        import jax
        import jax.numpy as jnp
        import numpy as np
        from jax import lax
        D_MODEL = 64
        N = 64
        L = 512
        BATCH = 8
        DT = 0.1
        batch, Lseq, d_model = u.shape
        A = (-jnp.exp(A_real) + 1j * A_imag).astype(jnp.complex64)
        A_disc = jnp.exp(A * DT)
        C = (C_real + 1j * C_imag).astype(jnp.complex64)
        freqs = jnp.arange(Lseq + 1, dtype=jnp.float32) * 0.5
        omega = jnp.exp(-2j * math.pi * freqs.astype(jnp.complex64) / Lseq)
        k_f = (C[:, :, None] / (1.0 - omega[None, None, :] * A_disc[:, :, None])).sum(axis=1)
        k = jnp.fft.irfft(k_f, n=2 * Lseq, axis=-1)[:, :Lseq].astype(u.dtype)
        pad_left = (Lseq - 1) // 2
        pad_right = Seq = Lseq // 2
        uT = jnp.transpose(u, (0, 2, 1))
        y = lax.conv_general_dilated(uT, k[:, None, :], window_strides=(1,), padding=[(pad_left, pad_right)], feature_group_count=d_model, dimension_numbers=('NCH', 'OIH', 'NCH'))
        y = y + D[None, :, None]
        return jnp.transpose(y, (0, 2, 1))

    def _L1_ffn_ref(input_embeddings, router_w, w1, b1, w2, b2):
        import jax, jax.numpy as jnp
        import numpy as np
        NUM_EXPERTS = 8
        TOP_K = 2
        B, S, D = (8, 2048, 64)

        def _moe(tokens, router_w, w1, b1, w2, b2):
            N = tokens.shape[0]
            E = router_w.shape[0]
            logits = tokens.astype(jnp.float32) @ router_w.astype(jnp.float32).T
            probs = jax.nn.softmax(logits, axis=-1)
            rw, re = jax.lax.top_k(probs, TOP_K)
            if TOP_K > 1:
                rw = rw / jnp.maximum(rw.sum(-1, keepdims=True), 1e-12)
            rw = rw.astype(tokens.dtype)
            combine = jnp.zeros((N, E), tokens.dtype).at[jnp.arange(N)[:, None], re].set(rw)
            out = tokens
            for e in range(E):
                h = jax.nn.gelu(tokens @ w1[e] + b1[e], approximate=False)
                y = h @ w2[e] + b2[e]
                out = out + combine[:, e:e + 1] * y
            return out
        b, s, d = input_embeddings.shape
        tokens = input_embeddings.reshape(b * s, d)
        return _moe(tokens, router_w, w1, b1, w2, b2).reshape(b, s, d)
    h = _L0_tok_ref(x, L0_tok_W)
    h = h + _L0_attn_ref(_layernorm(h, axis=-1), L0_attn_q_weight)
    h = h + _L0_ffn_ref(_layernorm(h, axis=-1), L0_ffn_route_id, L0_ffn_Wi, L0_ffn_bi, L0_ffn_Wr, L0_ffn_br, L0_ffn_Ws, L0_ffn_bs, L0_ffn_Wo, L0_ffn_bo)
    h = h + _L1_attn_ref(_layernorm(h, axis=-1), L1_attn_A_real, L1_attn_A_imag, L1_attn_C_real, L1_attn_C_imag, L1_attn_D)
    h = h + _L1_ffn_ref(_layernorm(h, axis=-1), L1_ffn_router_w, L1_ffn_w1, L1_ffn_b1, L1_ffn_w2, L1_ffn_b2)
    return h

_drawn_inputs = setup_inputs


def setup_inputs(seed=0):
    import zlib

    import numpy as np

    out = dict(_drawn_inputs(seed))
    spreads = {'L0_ffn_bi': (0.0, 0.8),
     'L0_ffn_bo': (0.0, 2.0),
     'L1_attn_A_real': (-0.6931471824645996, 0.2),
     'L1_attn_D': (0.0, 2.0),
     'L1_ffn_b1': (0.0, 0.8),
     'L1_ffn_b2': (0.0, 2.0)}
    factors = {'L0_ffn_Wi': 8.0,
     'L0_ffn_Wr': 8.0,
     'L0_ffn_br': 33.344,
     'L0_ffn_Ws': 8.0,
     'L0_ffn_bs': 29.284,
     'L0_ffn_Wo': 8.0,
     'L1_ffn_router_w': 8.0,
     'L1_ffn_w1': 7.784,
     'L1_ffn_w2': 7.109}
    for name, (base, spread) in spreads.items():
        noise = np.random.default_rng([zlib.crc32(name.encode()), seed]).standard_normal(out[name].shape)
        drawn = base * np.exp(spread * noise) if base else spread * noise
        out[name] = jnp.asarray(drawn.astype(out[name].dtype))
    for name, factor in factors.items():
        out[name] = (out[name] * factor).astype(out[name].dtype)
    return out
```

```python
from contextlib import ExitStack
import math

import numpy as np

import concourse.bass as bass
from concourse import mybir

ALU = mybir.AluOpType
ACT = mybir.ActivationFunctionType
AX = mybir.AxisListType
F32 = mybir.dt.float32
BF16 = mybir.dt.bfloat16
I32 = mybir.dt.int32
ds = bass.ds

B, C, T_IN, V = 4, 64, 128, 64
D = 64
PATCH, STRIDE = 16, 8
NPATCH = T_IN // STRIDE
NF = PATCH // 2 + 1
RF = 2 * NF
Q4 = STRIDE // 2
L = V * NPATCH
P = 128
NT, NV = 4, 2
SLOTS = NT * NV
HID = 128
LAYERS, EXPERTS = 2, 16
GROUPS = 64
GPB = GROUPS // B
GTOK = B * L // GROUPS
NS = 32
DT = 0.1
NFFT = 1536
RADIX = NFFT // P
NX = RADIX
SETS = RADIX // 2
NBLK = 2 + 4 * (SETS - 1)
SHIFT = (L - 1) // 2
COS30 = math.sqrt(0.75)
MOE, TOPW = 8, 2
PAIRS = MOE // 2
EPS = 1e-5
ROUND = 1.5 * 2.0 ** 23
TURN = 6.2831850
NTAB = 2 * L // P + L // P
NCOL = NTAB + 1


def patch_dft():
    a = 2 * np.pi * np.arange(NF)[:, None] * np.arange(PATCH)[None, :] / PATCH
    return np.concatenate([np.cos(a), -np.sin(a)]) / math.sqrt(PATCH)


def forward_blocks():
    p = np.arange(P)[:, None]
    out = np.zeros((P, NBLK, P))
    g = np.arange(64)[None, :]
    for half, r in ((0, 0), (1, 6)):
        a = 2 * np.pi * (RADIX * g + r) * p / NFFT
        c, s = np.cos(a), -np.sin(a)
        if r == 0:
            s[:, 0] = np.cos(np.pi * p[:, 0])
        out[:, 0, half * 64:half * 64 + 64] = c
        out[:, 1, half * 64:half * 64 + 64] = s
    g = np.arange(P)[None, :]
    for r in range(1, SETS):
        a = 2 * np.pi * (RADIX * g + r) * p / NFFT
        fold = -1.0 if r % 2 else -COS30
        k = 4 * r - 2
        out[:, k + 0] = np.cos(a)
        out[:, k + 1] = fold * np.sin(a)
        out[:, k + 2] = -np.sin(a)
        out[:, k + 3] = fold * np.cos(a)
    return out


def inverse_blocks():
    p = np.arange(P)[None, :]
    out = np.zeros((P, NBLK, P))
    g = np.arange(64)[:, None]
    for half, r in ((0, 0), (1, 6)):
        a = 2 * np.pi * (RADIX * g + r) * p / NFFT
        c, s = 2 * np.cos(a) / NFFT, -2 * np.sin(a) / NFFT
        if r == 0:
            c[0] /= 2
            s[0] = np.cos(np.pi * p[0]) / NFFT
        out[half * 64:half * 64 + 64, 0] = c
        out[half * 64:half * 64 + 64, 1] = s
    g = np.arange(P)[:, None]
    for r in range(1, SETS):
        a = 2 * np.pi * (RADIX * g + r) * p / NFFT
        c, s = 2 * np.cos(a) / NFFT, 2 * np.sin(a) / NFFT
        fold = 1.0 if r % 2 else COS30
        k = 4 * r - 2
        out[:, k + 0], out[:, k + 1] = c, -s
        out[:, k + 2], out[:, k + 3] = fold * s, fold * c
    return out


def phase_tables():
    f = np.zeros((P, SETS))
    f[:64, 0] = RADIX * np.arange(64)
    f[64:, 0] = RADIX * np.arange(64) + 6
    for r in range(1, SETS):
        f[:, r] = RADIX * np.arange(P) + r
    a = 2 * np.pi * f * SHIFT / NFFT
    c, s = np.cos(a), np.sin(a)
    cb, sb, cd, sd = c.copy(), s.copy(), c.copy(), s.copy()
    cb[0, 0] = sb[0, 0] = 0.0
    cd[0, 0], sd[0, 0] = 0.0, 1.0
    return np.stack([c, -s, -sb, -cb, cd, -sd], 1)


def hilbert_band():
    m = (np.arange(3 * L)[None, :] - (2 * L - P)) - np.arange(P)[:, None]
    odd = m % 2 != 0
    h = np.zeros(m.shape)
    h[odd] = -1.0 / (L * np.tan(np.pi * m[odd] / (2 * L)))
    return h


def turn_offsets():
    im = (np.arange(P) // NS) % 2
    off = np.zeros((P, 2, NCOL))
    shift = np.zeros((P, NCOL))
    shift[:, :2 * L // P] = np.where(im[:, None] == 1, -0.25, 0.0)
    shift[:, 2 * L // P:NTAB] = np.where(im[:, None] == 1, 0.0, 0.25)
    off[:, 0] = shift + 0.25
    off[:, 1] = shift
    return off


def constants():
    f = np.float32
    im = ((np.arange(P) // NS) % 2).astype(f)
    cols = np.concatenate([P * np.arange(2 * L // P), P * np.arange(L // P), [2 * L]])
    sel = np.zeros((3 * MOE, PAIRS, P), f)
    for i in range(3):
        for e in range(MOE):
            sel[i * MOE + e, e // 2, (e % 2) * 64:(e % 2) * 64 + 64] = 1
    return {
        "c_ident": np.eye(P, dtype=f),
        "c_dft": patch_dft().astype(f),
        "c_fwd": forward_blocks().astype(f),
        "c_inv": inverse_blocks().astype(f),
        "c_phase": phase_tables().astype(f),
        "c_hilb": hilbert_band().astype(f),
        "c_ramp": np.broadcast_to(np.arange(P, dtype=f), (P, P)).copy(),
        "c_cols": np.broadcast_to(cols.astype(f), (P, NCOL)).copy(),
        "c_off": turn_offsets().astype(f),
        "c_quarter": (0.25 * im)[:, None].astype(f),
        "c_first": np.broadcast_to(MOE - np.arange(MOE, dtype=f), (P, MOE)).copy(),
        "c_sel": sel,
    }


class Steps:

    def __init__(self, engine, sem):
        self.engine, self.sem, self.base, self.n = engine, sem, 0, 0

    def done(self, instruction):
        instruction.then_inc(self.sem, 1)
        self.n += 1

    def wait(self):
        self.engine.wait_ge(self.sem, self.base + self.n)

    def seq(self, instruction):
        self.done(instruction)
        self.wait()

    def trip(self, index, per_trip):
        self.first = self.base + self.n
        self.per = per_trip
        self.base, self.n = index * per_trip + self.first, 0

    def leave(self, trips):
        assert self.n == self.per, (self.n, self.per)
        self.base, self.n = self.first + trips * self.per, 0


def seq_of(ap, b):
    return ap[:, ds(b, 1)].rearrange("p x s d -> p (x s) d")


def small_of(ap, b):
    return ap[:, ds(b, 1)].rearrange("p x s -> p (x s)")


def over_last(ap, n):
    return ap.unsqueeze(2).to_broadcast([ap.shape[0], ap.shape[1], n])


def build_tower(nc, x, tok_w, q_w, route, wi, bi, wr, br, ws, bs, wo, bo, a_re, a_im, c_re, c_im, dvec,
                router_w, w1, b1, w2, b2, c_ident, c_dft, c_fwd, c_inv, c_phase, c_hilb, c_ramp, c_cols,
                c_off, c_quarter, c_first, c_sel, out, **taps):
    with ExitStack() as ctx:
        def sb(name, shape, dt=F32):
            return ctx.enter_context(nc.sbuf_tensor(name, shape, dt))

        def region(name, floats):
            return sb(name, [P, floats])

        def part(area, first, shape, dt=F32):
            floats = math.prod(shape[1:]) * mybir.dt.size(dt) // 4
            ap = area[0:shape[0], first:first + floats]
            if dt != F32:
                ap = ap.bitcast(dt)
            if len(shape) == 2:
                return ap
            names = ["x%d" % i for i in range(len(shape) - 1)]
            return ap.rearrange("p (%s) -> p %s" % (" ".join(names), " ".join(names)),
                                **dict(zip(names[1:], shape[2:])))

        def sem(name):
            return ctx.enter_context(nc.semaphore(name))

        ident = sb("ident", [P, P])
        ident_b = sb("ident_b", [P, P], BF16)
        dft = sb("dft", [RF, PATCH])
        weff = sb("weff", [P, Q4, 2, D])
        wq = sb("wq", [P, 2, D])
        wi_raw = sb("wi_raw", [HID, 2, D])
        wi_t = sb("wi_t", [P, HID])
        ws_raw = sb("ws_raw", [HID, LAYERS, HID])
        base_t = sb("base_t", [HID, LAYERS, HID])
        b_raw = sb("b_raw", [LAYERS * (EXPERTS + 2), HID])
        b_t = sb("b_t", [HID, LAYERS * (EXPERTS + 2)])
        bi_c = sb("bi_c", [HID, 1])
        wo_raw = sb("wo_raw", [D, HID])
        wo_t = sb("wo_t", [HID, D])
        bo_b = sb("bo_b", [P, D])
        route_i = sb("route_i", [1, GROUPS], I32)
        route_f = sb("route_f", [1, GROUPS])
        route_ok = sb("route_ok", [1, GROUPS])
        route_lo = sb("route_lo", [1, GROUPS])
        route_x = sb("route_x", [1, GROUPS])
        route_e = sb("route_e", [1, GROUPS], I32)
        dvec_b = sb("dvec_b", [P, D])
        phase = sb("phase", [P, 6, SETS])
        ramp = sb("ramp", [P, P])
        cols = sb("cols", [P, NCOL])
        off = sb("off", [P, 2, NCOL])
        quarter = sb("quarter", [P, 1])
        rw_raw = sb("rw_raw", [MOE, 2, D])
        rw_t = sb("rw_t", [P, MOE])
        w1_s = sb("w1_s", [P, MOE, D])
        b1_raw = sb("b1_raw", [PAIRS, P])
        b1_t = sb("b1_t", [P, PAIRS])
        w2_s = sb("w2_s", [P, PAIRS, D])
        b2_f = sb("b2_f", [3 * MOE, D])
        b2_r = sb("b2_r", [3 * MOE, 2, D])
        b2_s = sb("b2_s", [3 * MOE, 3, D], BF16)
        first_w = sb("first_w", [P, MOE])
        sel_f = sb("sel_f", [3 * MOE, PAIRS, P])
        sel = sb("sel", [3 * MOE, PAIRS, P], BF16)
        minus_half = sb("minus_half", [P, SLOTS])

        area = region("area_x", 2 * (NPATCH + 1) * Q4 * V)
        x_one = (NPATCH + 1) * Q4 * V
        xs = [part(area, i * x_one, [P, NPATCH + 1, Q4, V]) for i in range(2)]
        hilb = part(area, 0, [P, 3 * L])
        fwd = part(area, 3 * L, [P, NBLK, P])
        inv = part(area, 3 * L + NBLK * P, [P, NBLK, P])

        area = region("area_w", 4096)
        tokw = part(area, 0, [RF, D, C])
        wr_raw = part(area, 0, [HID, LAYERS * EXPERTS, HID])
        even = part(area, 0, [P, SETS, B * D])
        odd = part(area, SETS * B * D, [P, SETS, B * D])
        result = [part(area, i * 512, [P, SLOTS, D]) for i in range(2)]
        gate_t = [part(area, 3072 + i * L // 2, [3 * MOE, L], BF16) for i in range(2)]

        area = region("area_t", LAYERS * (EXPERTS + 1) * (HID + 1))
        table = part(area, 0, [HID, LAYERS, EXPERTS + 1, HID + 1])
        u = part(area, 0, [P, L // P, B, D])
        gelu = [part(area, i * L, [P, L]) for i in range(2)]
        gated = [part(area, (2 + i) * L, [P, L]) for i in range(2)]

        area = region("area_a", 4096)
        row_y = part(area, 0, [P, NS, P])
        row_e = part(area, 0, [P, NS, P])
        att = [part(area, i * L, [P, L]) for i in range(4)]
        fly = part(area, 0, [P, 16, B * D])

        area = region("area_b", 4096)
        row_z = part(area, 0, [P, NS, P])
        beta = part(area, 0, [P, NS, P])
        hid = [part(area, i * L, [HID, L]) for i in range(2)]
        hid_in = [part(area, (2 + i) * L, [HID, L]) for i in range(2)]
        y_spec = part(area, 0, [P, SETS, 2, B * D])

        area = region("area_s", 6 * NS * NCOL)
        col_y = part(area, 0, [P, NS, NCOL])
        col_e = part(area, NS * NCOL, [P, NS, NCOL])
        col_tab = part(area, 2 * NS * NCOL, [P, 2, NS, NCOL])
        col_z = part(area, 4 * NS * NCOL, [P, 2, NS, NCOL])
        staged = [part(area, i * GPB * (HID + 1), [HID, GPB, HID + 1]) for i in range(2)]
        z = part(area, 0, [P, SETS, 2, B * D])

        area = region("area_q", 2 * L)
        s_im = part(area, 0, [P, 2 * L // P, D])
        s_re = part(area, L, [P, L // P, D])
        k_fm = part(area, L + L // 2, [P, NT * P])
        q_fm = [part(area, i * L, [P, L]) for i in range(2)]
        prod_a = [part(area, i * 512, [P, 2, B * D]) for i in range(2)]
        prod_b = [part(area, (2 + i) * 512, [P, 2, B * D]) for i in range(2)]

        area = region("area_f", 2 * NT * P)
        tok_fm = [part(area, i * NT * P, [P, NT * P]) for i in range(2)]
        pv_fm = [part(area, i * NT * P, [P, NT * P]) for i in range(2)]
        moe_fm = [part(area, i * NT * P, [P, NT * P]) for i in range(2)]
        xr = sb("xr", [P, NX, B * D])

        h = sb("h", [P, B, SLOTS, D])
        mean = sb("mean", [P, B, SLOTS])
        var = sb("var", [P, B, SLOTS])
        rstd = sb("rstd", [P, B, SLOTS])
        stat = sb("stat", [P, SLOTS, 6])
        st = [sb(f"st{i}", [P, SLOTS]) for i in range(5)]
        centred = sb("centred", [P, SLOTS, D])
        ln = [sb(f"ln{i}", [P, SLOTS, D]) for i in range(2)]
        ln_fm = [sb(f"ln_fm{i}", [P, NT * P]) for i in range(2)]

        par_raw = sb("par_raw", [D, 4, 4, NS])
        par_t = sb("par_t", [P, 4, NS])
        lam = sb("lam", [P, NS])
        turns = sb("turns", [P, NS])
        small = [sb(f"small{i}", [P, NS]) for i in range(6)]
        alpha = sb("alpha", [P, NS, NTAB])
        k_time = sb("k_time", [P, L // P, 1, D])
        k_spec = sb("k_spec", [P, SETS, 2, D])
        k_mul = [sb(f"k_mul{i}", [P, SETS, D]) for i in range(2)]
        k_abd = sb("k_abd", [P, SETS, 3, D])
        sm_d = sb("sm_d", [P, 2 * SLOTS, MOE])
        sm_p = sb("sm_p", [P, 2 * SLOTS, MOE])
        sm_key = sb("sm_key", [P, 2 * SLOTS, MOE])
        sm_one = [sb(f"sm_one{i}", [P, 2 * SLOTS, MOE]) for i in range(2)]
        sm_c = sb("sm_c", [P, 2 * SLOTS, MOE])
        sm_r = [sb(f"sm_r{i}", [P, 2 * SLOTS]) for i in range(5)]
        split = sb("split", [P, 2 * SLOTS, 3 * MOE], BF16)

        wide_t = ctx.enter_context(nc.psum_tensor("wide", [P, 2, 2 * 512], F32))
        wide = [wide_t[:, i] for i in range(2)]
        turn = [ctx.enter_context(nc.psum_tensor(f"turn{i}", [P, 512], F32)) for i in range(2)]
        acc_t = ctx.enter_context(nc.psum_tensor("acc", [P, 2, 512], F32))
        acc = [acc_t[:, i] for i in range(2)]

        ld_tok, ld_attn, ld_ffn, ld_ssm, ld_conv, ld_moe = (
            sem(n) for n in ("ld_tok", "ld_attn", "ld_ffn", "ld_ssm", "ld_conv", "ld_moe"))
        x_in = [sem(f"x_in{i}") for i in range(2)]
        ve, ae, pe_s, ge = sem("dve_step"), sem("act_step"), sem("pe_step"), sem("pool_step")
        s = {n: sem(n) for n in (
            "weff_mm", "weff_ready", "tok_mm", "tok_copied", "tok_turned", "h_ready", "stats_ready",
            "ln_ready", "ln_turned", "ln_fm_ready", "ln_used",
            "q_mm", "q_ready", "score_mm", "att_ready", "pv_step", "pv_mm", "pv_copied", "pv_turned",
            "wgt_turned", "wgt_ready", "begun", "route_ready", "staged_ready", "bo_added",
            "hid_mm", "hid_relu", "bias_added", "ffn_mm", "staged_used",
            "par_turned", "tab_mul", "tab_ready", "exp_in", "exp_out", "sin_in", "sin_out",
            "s_mm", "s_ready", "hil_mm", "hil_copied", "k_turned", "k_ready", "k_fly", "k_dft",
            "k_spec_ready", "k_mul_ready", "u_ready", "u_fly", "u_dft", "u_prod", "y_ready", "z_mm",
            "z_copied", "even_ready", "route_mm", "sm_in", "sm_exp", "split_ready", "gate_turned",
            "gate_ready", "up_mm", "gelu_ready", "gate_mm", "gated_ready", "down_mm", "moe_copied",
            "moe_turned", "res_ready", "res_stored", "beta_ready", "alpha_ready", "small_turned",
            "moe_bias_ready", "gate_step", "passed")}
        block = ctx.enter_context(nc.Block())

        def stand_apart(engine):
            engine.sem_inc(s["passed"], 1)

        @block.sync
        def _(sp):
            sp.dma_start(ident[:], c_ident).then_inc(ld_tok, 16)
            sp.dma_start(dft[:], c_dft).then_inc(ld_tok, 16)
            sp.dma_start(tokw[:], tok_w.rearrange("o (r c) -> r o c", c=C)).then_inc(ld_tok, 16)

            def load_x(b, par):
                src = x[b].rearrange("c (n h q) v -> h c n (q v)", h=2, q=Q4)
                edge = x[b, :, T_IN - 1:T_IN, :]
                for hh in range(2):
                    half = xs[par][hh * C:(hh + 1) * C]
                    sp.dma_start(half[:, 0:NPATCH].rearrange("c n q v -> c n (q v)"),
                                 src[hh]).then_inc(x_in[par], 16)
                    sp.dma_start(half[:, NPATCH], edge.to_broadcast([C, Q4, V])).then_inc(x_in[par], 16)

            for i, a in enumerate((a_re, a_im, c_re, c_im)):
                sp.dma_start(par_raw[:, i], a.unsqueeze(1).to_broadcast([D, 4, NS])).then_inc(ld_ssm, 16)
            for dst, src in ((ramp, c_ramp), (cols, c_cols), (off, c_off), (quarter, c_quarter)):
                sp.dma_start(dst[:], src).then_inc(ld_ssm, 16)
            load_x(0, 0)
            load_x(1, 1)
            for i in range(2):
                sp.dma_start(wq[i * D:(i + 1) * D], q_w.unsqueeze(1).to_broadcast([D, 2, D])).then_inc(ld_attn, 16)
            sp.wait_ge(s["tok_mm"], 1)
            load_x(2, 0)
            sp.wait_ge(s["tok_mm"], 2)
            load_x(3, 1)
            sp.wait_ge(s["weff_mm"], 1)
            sp.dma_start(wr_raw[:], wr.rearrange("l e h d -> h (l e) d")).then_inc(ld_ffn, 16)
            sp.dma_start(ws_raw[:], ws.rearrange("l s h d -> h (l s) d")).then_inc(ld_ffn, 16)
            for i in range(2):
                sp.dma_start(wi_raw[:, i], wi).then_inc(ld_ffn, 16)
            sp.dma_start(b_raw[0:LAYERS * EXPERTS], br.rearrange("l e h -> (l e) h")).then_inc(ld_ffn, 16)
            sp.dma_start(b_raw[LAYERS * EXPERTS:LAYERS * (EXPERTS + 1)],
                         bs.rearrange("l s h -> (l s) h")).then_inc(ld_ffn, 16)
            sp.dma_start(bi_c[:], bi.unsqueeze(1)).then_inc(ld_ffn, 16)
            sp.dma_start(wo_raw[:], wo).then_inc(ld_ffn, 16)
            sp.dma_start(bo_b[:], bo.unsqueeze(0).to_broadcast([P, D])).then_inc(ld_ffn, 16)
            sp.dma_start(route_i[:], route.unsqueeze(0)).then_inc(ld_ffn, 16)
            sp.wait_ge(s["tok_mm"], B)
            for dst, src in ((hilb, c_hilb), (fwd, c_fwd), (inv, c_inv), (phase, c_phase)):
                sp.dma_start(dst[:], src).then_inc(ld_conv, 16)
            sp.dma_start(dvec_b[:], dvec.unsqueeze(0).to_broadcast([P, D])).then_inc(ld_conv, 16)
            for i in range(2):
                sp.dma_start(rw_raw[:, i], router_w).then_inc(ld_moe, 16)
                sp.dma_start(w1_s[i * D:(i + 1) * D], w1.rearrange("e d f -> d e f")).then_inc(ld_moe, 16)
            sp.dma_start(b1_raw[:], b1.rearrange("(q e) f -> q (e f)", e=2)).then_inc(ld_moe, 16)
            sp.dma_start(w2_s[:], w2.rearrange("(q e) f o -> (e f) q o", e=2)).then_inc(ld_moe, 16)
            for i in range(3):
                sp.dma_start(b2_f[i * MOE:(i + 1) * MOE], b2).then_inc(ld_moe, 16)
            sp.dma_start(first_w[:], c_first).then_inc(ld_moe, 16)
            sp.dma_start(sel_f[:], c_sel).then_inc(ld_moe, 16)
            sp.sem_inc(s["res_stored"], 16)
            for b in range(B):
                sp.wait_ge(s["res_ready"], b + 3)
                dst = out[b].rearrange("(v t p) d -> p t v d", v=NV, t=NT)
                res = result[b % 2].rearrange("p (t v) d -> p t v d", v=NV)
                for v in range(NV):
                    sp.dma_start(dst[:, :, v], res[:, :, v]).then_inc(s["res_stored"], 16)
            sp.wait_ge(s["res_stored"], 16 * NV * B + 16)

        @block.tensor
        def _(pe):
            def transposes(dst, src):
                for t in range(NT):
                    last = pe.transpose(dst[:, t * P:(t + 1) * P], src[:, t * P:(t + 1) * P], ident[:])
                return last

            def fm_transposes(par):
                return transposes(turn[par], ln[par].rearrange("p s d -> p (s d)"))

            def spectrum(out_of, src, n, copied=None):
                for half, i in ((0, 0), (1, 1)):
                    for part in range(2):
                        pe.matmul(out_of(0, part)[half * 64:(half + 1) * 64], fwd[:, part, half * 64:(half + 1) * 64],
                                  src[:, i, 0:n], start=True, stop=True)
                for r in range(1, SETS):
                    for part in range(2):
                        for k in range(2):
                            last = pe.matmul(out_of(r, part), fwd[:, 4 * r - 2 + 2 * part + k],
                                             src[:, 2 * r + k, 0:n], start=(k == 0), stop=(k == 1))
                return last

            pe.wait_ge(ld_tok, 16 * 3)
            for o in range(D):
                last = pe.matmul(wide[0][0:C, o * PATCH:(o + 1) * PATCH], tokw[:, o, :], dft[:],
                                 start=True, stop=True)
            last.then_inc(s["weff_mm"], 1)

            pe.wait_ge(ld_ssm, 16 * 8)
            for i in range(4):
                last = pe.transpose(wide[1][:, i * D:(i + 1) * D], par_raw[:, i].rearrange("d r n -> d (r n)"),
                                    ident[0:D, 0:D])
            last.then_inc(s["par_turned"], 1)
            pe.wait_ge(s["weff_ready"], 2)

            with pe.Fori(0, B // 2) as pair:
                for par in range(2):
                    b = pair * 2 + par
                    pe.wait_ge(x_in[par], pair * 64 + 64)
                    pe.wait_ge(s["tok_copied"], b + 1)
                    for k in range(2 * Q4):
                        q, lohi = k // 2, k % 2
                        for v in range(NV):
                            last = pe.matmul(acc[par][v * D:(v + 1) * D], weff[:, q, lohi, :],
                                             xs[par][:, lohi:lohi + NPATCH, q, v * 32:(v + 1) * 32],
                                             start=(k == 0), stop=(k == 2 * Q4 - 1))
                    last.then_inc(s["tok_mm"], 1)
                for par in range(2):
                    b = pair * 2 + par
                    pe.wait_ge(s["tok_copied"], b + 3)
                    pe.wait_ge(s["h_ready"], b + 1)
                    transposes(turn[par], tok_fm[par]).then_inc(s["tok_turned"], 1)

            pe.wait_ge(ld_ffn, 16 * 10)
            pe.wait_ge(s["h_ready"], B + 2)
            for i in range(LAYERS):
                last = pe.transpose(turn[0][:, i * HID:(i + 1) * HID], ws_raw[:, i], ident[:])
            pe.transpose(turn[0][:, 256:256 + HID], wi_raw[:].rearrange("h c d -> h (c d)"), ident[:])
            pe.transpose(turn[0][:, 384:384 + D], wo_raw[:], ident[0:D, 0:D])
            nb = LAYERS * (EXPERTS + 1)
            pe.transpose(turn[1][:, 0:nb], b_raw[0:nb], ident[0:nb, 0:nb]).then_inc(s["wgt_turned"], 1)
            for g in range(LAYERS * EXPERTS // 8):
                if g == 1:
                    pe.wait_ge(s["small_turned"], 1)
                if g >= 2:
                    pe.wait_ge(s["wgt_ready"], g)
                for i in range(8):
                    last = pe.transpose(wide[g % 2][:, i * HID:(i + 1) * HID], wr_raw[:, g * 8 + i], ident[:])
                last.then_inc(s["wgt_turned"], 1)

            pe.wait_ge(s["beta_ready"], 1)
            pe.wait_ge(s["alpha_ready"], 1)
            pe.wait_ge(s["wgt_ready"], LAYERS * EXPERTS // 8 + 1)
            for dd in range(NS):
                for dh in range(2):
                    rows = slice(dh * 64, dh * 64 + 64)
                    o0 = (dd // 16) * 512 + (dd % 16) * NTAB
                    last = pe.matmul(wide[dh][:, o0:o0 + NTAB], beta[rows, dd, :], alpha[rows, dd, :],
                                     start=True, stop=True)
            last.then_inc(s["s_mm"], 1)

            pe.wait_ge(s["s_ready"], 2)
            pe.wait_ge(ld_conv, 16 * 5)
            pe.wait_ge(s["tok_copied"], B + 2)
            for j in range(2 * L // P):
                for th in range(2):
                    x0 = 2 * L - P - j * P + th * 512
                    last = pe.matmul(acc[0][th * D:(th + 1) * D], s_im[:, j, :], hilb[:, x0:x0 + 512],
                                     start=(j == 0), stop=(j == 2 * L // P - 1))
            last.then_inc(s["hil_mm"], 1)
            pe.wait_ge(s["hil_copied"], 1)
            pe.wait_ge(s["wgt_ready"], 1)
            transposes(turn[0], k_fm).then_inc(s["k_turned"], 1)
            pe.wait_ge(s["k_fly"], 2)
            spectrum(lambda r, part: wide[0][:, r * P + part * D:r * P + (part + 1) * D], xr, D).then_inc(s["k_dft"], 1)

            pe.wait_ge(ld_attn, 16 * 2)
            pe.wait_ge(s["k_spec_ready"], 1)
            pe.wait_ge(s["k_ready"], 1)

            def attention_inputs(pair, par):
                b = pair * 2 + par
                pe.wait_ge(s["ln_ready"], b + 2)
                pe.wait_ge(s["h_ready"], b + B + 1)
                fm_transposes(par).then_inc(s["ln_turned"], 1)
                pe.wait_ge(s["ln_fm_ready"], b + 1)
                slot = par
                pe.wait_ge(s["att_ready"], b * 8 + 1)
                for v in range(NV):
                    rows = slice(v * D, (v + 1) * D)
                    last = pe.matmul(wide[slot][:, v * 512:(v + 1) * 512], wq[rows].rearrange("d c e -> d (c e)"),
                                     ln_fm[par][rows, :], start=True, stop=True)
                last.then_inc(s["q_mm"], 1)
                pe.wait_ge(s["q_ready"], b + 1)

            def scores(b, par, m):
                t, v = m // NV, m % NV
                rows = slice(v * D, (v + 1) * D)
                pe.wait_ge(s["att_ready"], b * 8 + (2 if m == 0 else m + 1))
                for c in range(2):
                    last = pe.matmul(wide[(par + 1 + m) % 2][:, c * 512:(c + 1) * 512],
                                     ln_fm[par][rows, t * P:(t + 1) * P], q_fm[par][rows, c * 512:(c + 1) * 512],
                                     start=True, stop=True)
                last.then_inc(s["score_mm"], 1)

            def attend(pair, par):
                b = pair * 2 + par
                scores(b, par, 0)
                scores(b, par, 1)
                pe.wait_ge(s["pv_copied"], b + 1)
                for m in range(SLOTS):
                    pe.wait_ge(s["att_ready"], b * 8 + m + 3)
                    if m + 2 < SLOTS:
                        scores(b, par, m + 2)
                    for c in range(2):
                        last = pe.matmul(acc[par][c * D:(c + 1) * D], ln[par][:, m, :],
                                         att[m % 4][:, c * 512:(c + 1) * 512],
                                         start=(m == 0), stop=(m == SLOTS - 1))
                    last.then_inc(s["pv_step"], 1)

            def attention_back(pair, par):
                b = pair * 2 + par
                pe.wait_ge(s["pv_copied"], b + 3)
                transposes(turn[par], pv_fm[par]).then_inc(s["pv_turned"], 1)

            with pe.Fori(0, B // 2) as pair:
                attention_inputs(pair, 0)
                attend(pair, 0)
                attention_inputs(pair, 1)
                attention_back(pair, 0)
                attend(pair, 1)
                attention_back(pair, 1)

            with pe.Fori(0, B // 2) as pair:
                for par in range(2):
                    b = pair * 2 + par
                    pe.wait_ge(s["ln_ready"], b + B + 2)
                    pe.wait_ge(s["h_ready"], B + 2 + B)
                    fm_transposes(par).then_inc(s["ln_turned"], 1)
                for par in range(2):
                    b = pair * 2 + par
                    pe.wait_ge(s["ln_fm_ready"], b + B + 1)
                    pe.wait_ge(s["bias_added"], pair * 4 + par + 1)
                    if par == 0:
                        pe.wait_ge(s["att_ready"], 8 * B + 2)
                    for v in range(NV):
                        rows = slice(v * D, (v + 1) * D)
                        last = pe.matmul(wide[par][:, v * 512:(v + 1) * 512], wi_t[rows, :], ln_fm[par][rows, :],
                                         start=True, stop=True)
                    last.then_inc(s["hid_mm"], 1)
                for layer in range(LAYERS):
                    for par in range(2):
                        pe.wait_ge(s["hid_relu"], pair * 6 + 2 * layer + par + 1)
                        pe.wait_ge(s["staged_ready"], pair * 4 + 2 * layer + par + 1)
                        for g in range(GPB):
                            last = pe.matmul(wide[par][:, g * GTOK:(g + 1) * GTOK], staged[par][:, g, 0:HID],
                                             hid[par][:, g * GTOK:(g + 1) * GTOK], start=True, stop=True)
                        last.then_inc(s["hid_mm"], 1)
                for par in range(2):
                    b = pair * 2 + par
                    pe.wait_ge(s["hid_relu"], pair * 6 + 5 + par)
                    pe.wait_ge(s["h_ready"], b + 2 * B + 1)
                    for m in range(SLOTS):
                        t, v = m // NV, m % NV
                        last = pe.matmul(acc[par][:, m * D:(m + 1) * D], hid[par][:, v * 512 + t * P:v * 512 + (t + 1) * P],
                                         wo_t[:], start=True, stop=True)
                    last.then_inc(s["ffn_mm"], 1)

            pe.wait_ge(s["u_fly"], 2)
            pe.wait_ge(s["h_ready"], 3 * B + 2)
            banks = [wide_t[:, r // 2, (r % 2) * 512:(r % 2) * 512 + 512] for r in range(4)] + [t[:] for t in turn]
            n = B * D
            spectrum(lambda r, part: banks[r][:, part * n:(part + 1) * n], xr, n).then_inc(s["u_dft"], 1)
            pe.wait_ge(s["y_ready"], 1)
            for half in range(2):
                rows = slice(half * 64, half * 64 + 64)
                for part in range(2):
                    last = pe.matmul((banks[0], acc[0])[half][:, 0:n], inv[rows, part], y_spec[rows, 0, part],
                                     start=(part == 0), stop=(part == 1))
            last.then_inc(s["z_mm"], 1)
            for r in range(1, SETS):
                pe.wait_ge(s["y_ready"], r + 1)
                for part in range(2):
                    for k in range(2):
                        last = pe.matmul(banks[r][:, part * n:(part + 1) * n], inv[:, 4 * r - 2 + 2 * part + k],
                                         y_spec[:, r, k], start=(k == 0), stop=(k == 1))
                last.then_inc(s["z_mm"], 1)

            def down(b, par, qd):
                pe.wait_ge(s["gated_ready"], b * PAIRS + qd + 3)
                for v in range(NV):
                    last = pe.matmul(acc[par][v * D:(v + 1) * D], w2_s[:, qd, :], gated[qd % 2][:, v * 512:(v + 1) * 512],
                                     start=(qd == 0), stop=False)
                if qd == PAIRS - 1:
                    for i in range(3):
                        for v in range(NV):
                            last = pe.matmul(acc[par][v * D:(v + 1) * D], b2_s[:, i, :], gate_t[par][:, v * 512:(v + 1) * 512],
                                             start=False, stop=(i == 2))
                last.then_inc(s["down_mm"], 1)

            pe.wait_ge(ld_moe, 16 * 11)
            pe.wait_ge(s["z_copied"], 1)
            pe.transpose(acc[0][:, 0:MOE], rw_raw[:].rearrange("e c d -> e (c d)"), ident[0:MOE, 0:MOE])
            pe.transpose(acc[0][:, 16:16 + PAIRS], b1_raw[:], ident[0:PAIRS, 0:PAIRS]).then_inc(s["wgt_turned"], 1)
            pe.wait_ge(s["wgt_ready"], LAYERS * EXPERTS // 8 + 2)
            pe.wait_ge(s["z_copied"], SETS)
            pe.wait_ge(s["moe_bias_ready"], 1)
            with pe.Fori(0, B // 2) as pair:
                for par in range(2):
                    b = pair * 2 + par
                    pe.wait_ge(s["ln_ready"], b + 3 * B + 2)
                    pe.wait_ge(s["res_ready"], b + 1)
                    fm_transposes(par).then_inc(s["ln_turned"], 1)
                for par in range(2):
                    b = pair * 2 + par
                    pe.wait_ge(s["ln_fm_ready"], b + 2 * B + 1)
                    for m in range(SLOTS):
                        t, v = m // NV, m % NV
                        rows = slice(v * D, (v + 1) * D)
                        c0 = (par * NT + t) * MOE
                        last = pe.matmul(acc[v][:, c0:c0 + MOE], ln_fm[par][rows, t * P:(t + 1) * P], rw_t[rows, :],
                                         start=True, stop=True)
                last.then_inc(s["route_mm"], 1)
                pe.wait_ge(s["split_ready"], pair + 1)
                for par in range(2):
                    b = pair * 2 + par
                    narrow = turn[par][:].bitcast(BF16)
                    for m in range(SLOTS):
                        t, v = m // NV, m % NV
                        last = pe.transpose(narrow[0:3 * MOE, (v * NT + t) * P:(v * NT + t + 1) * P],
                                            split[:, (v * 2 + par) * NT + t, :], ident_b[:])
                    last.then_inc(s["gate_turned"], 1)
                for par in range(2):
                    b = pair * 2 + par
                    pe.wait_ge(s["gate_ready"], b + 1)
                    for qd in range(PAIRS):
                        pe.wait_ge(s["gelu_ready"], b * PAIRS + qd + 1)
                        for v in range(NV):
                            rows = slice(v * D, (v + 1) * D)
                            last = pe.matmul(wide[0][:, v * 512:(v + 1) * 512],
                                             w1_s[rows, 2 * qd:2 * qd + 2].rearrange("d e f -> d (e f)"),
                                             ln_fm[par][rows, :], start=True, stop=True)
                        last.then_inc(s["up_mm"], 1)
                        pe.wait_ge(s["gated_ready"], b * PAIRS + qd + 2)
                        for v in range(NV):
                            last = pe.matmul(wide[1][:, v * 512:(v + 1) * 512], sel[:, qd, :],
                                             gate_t[par][:, v * 512:(v + 1) * 512], start=True, stop=True)
                        last.then_inc(s["gate_mm"], 1)
                        if qd == 0:
                            pe.wait_ge(s["moe_copied"], b + 1)
                        else:
                            down(b, par, qd - 1)
                    down(b, par, PAIRS - 1)
                for par in range(2):
                    b = pair * 2 + par
                    pe.wait_ge(s["moe_copied"], b + 3)
                    transposes(turn[par], moe_fm[par]).then_inc(s["moe_turned"], 1)

        @block.scalar
        def _(act):
            step = Steps(act, ae)
            act.sem_inc(s["tok_copied"], 2)
            act.sem_inc(s["att_ready"], 2)
            act.sem_inc(s["gelu_ready"], 1)

            act.wait_ge(s["weff_mm"], 1)
            for hh in range(2):
                src = wide[0][0:C].rearrange("c (o k h q) -> c h q k o", k=2, h=2, q=Q4)
                act.copy(weff[hh * C:(hh + 1) * C], src[:, hh]).then_inc(s["weff_ready"], 1)
            act.wait_ge(s["small_turned"], 1)
            act.activation(small[5][:], par_t[:, 0], ACT.Exp).then_inc(s["exp_out"], 1)

            with act.Fori(0, B // 2) as pair:
                for par in range(2):
                    b = pair * 2 + par
                    act.wait_ge(s["tok_mm"], b + 1)
                    act.copy(tok_fm[par][:].rearrange("m (v n) -> m n v", n=NPATCH),
                             acc[par].rearrange("m (n v) -> m n v", n=NPATCH)).then_inc(s["tok_copied"], 1)

            act.wait_ge(s["exp_in"], 1)
            act.activation(row_e[:], row_e[:], ACT.Exp).then_inc(s["exp_out"], 1)
            act.wait_ge(s["tab_mul"], 2)
            act.activation(col_e[:], col_e[:], ACT.Exp).then_inc(s["exp_out"], 1)
            act.wait_ge(s["sin_in"], 1)
            act.activation(row_z[:], row_z[:], ACT.Sin, scale=-TURN).then_inc(s["sin_out"], 1)
            act.wait_ge(s["sin_in"], 2)
            act.activation(col_tab[:], col_z[:], ACT.Sin, scale=-TURN).then_inc(s["sin_out"], 1)

            act.wait_ge(s["s_mm"], 1)
            n_im = 2 * L // P
            src = wide_t[:].rearrange("p x (y k) -> p (x y) k", k=512)[:, :, 0:16 * NTAB].rearrange(
                "p z (d j) -> p z d j", j=NTAB)
            act.copy(s_im[:].rearrange("p j (z d) -> p z d j", z=4), src[:, :, :, 0:n_im]).then_inc(s["s_ready"], 1)
            act.copy(s_re[:].rearrange("p j (z d) -> p z d j", z=4), src[:, :, :, n_im:NTAB]).then_inc(s["s_ready"], 1)
            act.wait_ge(s["hil_mm"], 1)
            act.copy(k_fm[:], acc[0]).then_inc(s["hil_copied"], 1)
            act.wait_ge(s["k_dft"], 1)
            act.copy(k_spec[:].rearrange("p r c d -> p (r c d)"), wide[0][:, 0:SETS * 2 * D]).then_inc(s["k_spec_ready"], 1)

            with act.Fori(0, B // 2) as pair:
                for par in range(2):
                    b = pair * 2 + par
                    for m in range(SLOTS):
                        act.wait_ge(s["score_mm"], b * 8 + m + 1)
                        act.wait_ge(s["pv_step"], b * 8 + m + 1)
                        act.activation(att[m % 4][:], wide[(par + 1 + m) % 2], ACT.Sigmoid).then_inc(s["att_ready"], 1)

            act.wait_ge(ld_ffn, 16 * 10)
            with act.Fori(0, B // 2) as pair:
                for par in range(2):
                    act.wait_ge(s["hid_mm"], pair * 6 + par + 1)
                    act.activation(hid[par][:], wide[par], ACT.Relu, bias=bi_c[:, 0:1]).then_inc(s["hid_relu"], 1)
                for layer in range(LAYERS):
                    for par in range(2):
                        act.wait_ge(s["bias_added"], pair * 4 + 2 * layer + par + 3)
                        act.activation(hid[par][:], hid_in[par][:], ACT.Relu).then_inc(s["hid_relu"], 1)

            act.wait_ge(s["z_mm"], 1)
            act.copy(z[:, 0, 0], wide_t[:, 0, 0:B * D])
            act.copy(z[:, 0, 1], acc[0][:, 0:B * D]).then_inc(s["z_copied"], 1)
            for r in range(1, SETS):
                act.wait_ge(s["z_mm"], r + 1)
                src = wide_t[:, r // 2, (r % 2) * 512:(r % 2) * 512 + 512] if r < 4 else turn[r - 4][:]
                act.copy(z[:, r].rearrange("p c n -> p (c n)"), src).then_inc(s["z_copied"], 1)

            with act.Fori(0, B // 2) as pair:
                act.wait_ge(s["sm_in"], pair + 1)
                act.activation(sm_p[:], sm_d[:], ACT.Exp).then_inc(s["sm_exp"], 1)
                for par in range(2):
                    b = pair * 2 + par
                    for qd in range(PAIRS):
                        act.wait_ge(s["up_mm"], b * PAIRS + qd + 1)
                        act.wait_ge(s["gated_ready"], b * PAIRS + qd + 1)
                        act.activation(gelu[qd % 2][:], wide[0], ACT.Gelu, bias=b1_t[:, qd:qd + 1]).then_inc(s["gelu_ready"], 1)

        @block.vector
        def _(dve):
            step = Steps(dve, ve)
            dve.sem_inc(s["h_ready"], 2)
            dve.sem_inc(s["pv_copied"], 2)
            dve.sem_inc(s["bias_added"], 2)
            dve.sem_inc(s["gated_ready"], 2)
            dve.sem_inc(s["stats_ready"], 1)
            dve.sem_inc(s["moe_copied"], 2)
            dve.sem_inc(s["res_ready"], 2)

            def stats(b, hb, stage):
                dve.wait_ge(s["stats_ready"], b + stage * B + 1)
                stand_apart(dve)
                for m in range(SLOTS):
                    last = dve.bn_stats(stat[:, m, :], hb[:, m, :])
                step.seq(last)
                dve.tensor_tensor(st[0][:], stat[:, :, 1], stat[:, :, 4], ALU.add)
                dve.tensor_tensor(st[1][:], stat[:, :, 1], stat[:, :, 4], ALU.subtract)
                step.seq(dve.tensor_tensor(st[2][:], stat[:, :, 2], stat[:, :, 5], ALU.add))
                dve.tensor_scalar(small_of(mean, b), st[0][:], 0.5, None, ALU.mult)
                step.seq(dve.tensor_tensor(st[3][:], st[1][:], st[1][:], ALU.mult))
                step.seq(dve.scalar_tensor_tensor(st[4][:], st[3][:], D / 4.0, st[2][:], ALU.mult, ALU.add))
                dve.tensor_scalar(small_of(var, b), st[4][:], 1.0 / D, EPS, ALU.mult, ALU.add).then_inc(s["stats_ready"], 1)

            STATS = 4

            def odd_fly(src, dst, n):
                f = [fly[:, i, 0:n] for i in range(8)]
                o = [dst[:, i, 0:n] for i in range(NX)]
                tt, sst = dve.tensor_tensor, dve.scalar_tensor_tensor
                tt(f[0], src(0), src(6), ALU.subtract)
                tt(f[1], src(1), src(7), ALU.subtract)
                tt(f[4], src(2), src(4), ALU.subtract)
                step.seq(tt(f[5], src(2), src(4), ALU.add))
                tt(f[2], f[1], src(5), ALU.subtract)
                step.seq(tt(f[3], f[1], src(5), ALU.add))
                sst(f[6], f[4], 0.5, f[0], ALU.mult, ALU.add)
                tt(o[6], f[0], f[4], ALU.subtract)
                tt(o[7], f[3], src(3), ALU.subtract)
                step.seq(sst(f[7], f[3], 0.5, src(3), ALU.mult, ALU.add))
                sst(o[2], f[2], COS30, f[6], ALU.mult, ALU.add)
                sst(o[3], f[5], COS30, f[7], ALU.mult, ALU.add)
                sst(o[10], f[2], -COS30, f[6], ALU.mult, ALU.add)
                return sst(o[11], f[5], -COS30, f[7], ALU.mult, ALU.add)

            dve.wait_ge(s["par_turned"], 1)
            for dh in range(2):
                rows = slice(dh * 64, dh * 64 + 64)
                last = dve.tensor_copy(par_t[rows], wide[1][rows, 0:4 * D].rearrange(
                    "p (i x d) -> p i x d", i=4, x=2)[:, :, dh])
            last.then_inc(s["small_turned"], 1)
            dve.wait_ge(s["small_turned"], 1)
            step.seq(dve.tensor_scalar(small[0][:], par_t[:, 1], DT / (2 * math.pi), None, ALU.mult))
            step.seq(dve.tensor_scalar(small[1][:], small[0][:], ROUND, -ROUND, ALU.add, ALU.add))
            step.seq(dve.tensor_tensor(turns[:], small[0][:], small[1][:], ALU.subtract))
            dve.wait_ge(s["exp_out"], 1)
            dve.tensor_scalar(lam[:], small[5][:], -DT, None, ALU.mult).then_inc(s["tab_mul"], 1)
            step.seq(dve.tensor_tensor(row_y[:], ramp[:].unsqueeze(1).to_broadcast([P, NS, P]),
                                       over_last(turns[:], P), ALU.mult))
            step.seq(dve.tensor_scalar(row_y[:], row_y[:], quarter[:, 0:1], None, ALU.add))
            step.seq(dve.tensor_scalar(row_z[:], row_y[:], ROUND, -ROUND, ALU.add, ALU.add))
            dve.tensor_tensor(row_z[:], row_z[:], row_y[:], ALU.subtract).then_inc(s["sin_in"], 1)

            with dve.Fori(0, B // 2) as pair:
                step.trip(pair, 2 * STATS)
                for par in range(2):
                    b = pair * 2 + par
                    dve.wait_ge(s["tok_turned"], b + 1)
                    hb = seq_of(h, b)
                    dve.tensor_copy(hb, turn[par][:].rearrange("p (s d) -> p s d", d=D)).then_inc(s["h_ready"], 1)
                    dve.wait_ge(s["h_ready"], b + 3)
                    stats(b, hb, 0)
            step.leave(B // 2)

            def by_col(i):
                return cols[:].unsqueeze(1).to_broadcast([P, NS, NCOL])
            dve.tensor_tensor(col_y[:], by_col(0), over_last(turns[:], NCOL), ALU.mult)
            step.seq(dve.tensor_tensor(col_e[:], by_col(0), over_last(lam[:], NCOL), ALU.mult))
            dve.sem_inc(s["tab_mul"], 1)
            for i in range(2):
                last = dve.tensor_tensor(col_tab[:, i], col_y[:], off[:, i].unsqueeze(1).to_broadcast([P, NS, NCOL]), ALU.add)
            step.seq(last)
            step.seq(dve.tensor_scalar(col_z[:], col_tab[:], ROUND, -ROUND, ALU.add, ALU.add))
            dve.tensor_tensor(col_z[:], col_z[:], col_tab[:], ALU.subtract).then_inc(s["sin_in"], 1)
            dve.wait_ge(s["sin_out"], 2)
            dve.wait_ge(s["exp_out"], 3)
            c_r, c_i = par_t[:, 2], par_t[:, 3]
            d_r, d_i, z_r, q_r, q_i, w = (t[:] for t in small)
            e_last = col_e[:, :, NTAB]
            tt = dve.tensor_tensor
            tt(d_r, col_tab[:, 0, :, NTAB], e_last, ALU.mult)
            step.seq(tt(d_i, col_tab[:, 1, :, NTAB], e_last, ALU.mult))
            step.seq(dve.tensor_scalar(z_r, d_r, -1.0, 1.0, ALU.mult, ALU.add))
            tt(q_r, z_r, z_r, ALU.mult)
            step.seq(tt(q_i, d_i, d_i, ALU.mult))
            step.seq(tt(w, q_r, q_i, ALU.add))
            tt(q_r, c_r, z_r, ALU.mult)
            tt(q_i, c_i, d_i, ALU.mult)
            step.seq(dve.reciprocal(d_r, w))
            step.seq(tt(q_r, q_r, q_i, ALU.subtract))
            tt(q_i, c_r, d_i, ALU.mult)
            step.seq(tt(z_r, c_i, z_r, ALU.mult))
            step.seq(tt(q_i, q_i, z_r, ALU.add))
            tt(q_r, q_r, d_r, ALU.mult)
            step.seq(tt(q_i, q_i, d_r, ALU.mult))
            tt(col_z[:, 0, :, 0:NTAB], col_tab[:, 0, :, 0:NTAB], over_last(q_r, NTAB), ALU.mult)
            step.seq(tt(col_z[:, 1, :, 0:NTAB], col_tab[:, 1, :, 0:NTAB], over_last(q_i, NTAB), ALU.mult))
            step.seq(tt(alpha[:], col_z[:, 0, :, 0:NTAB], col_z[:, 1, :, 0:NTAB], ALU.subtract))
            tt(alpha[:], alpha[:], col_e[:, :, 0:NTAB], ALU.mult).then_inc(s["alpha_ready"], 1)

            dve.wait_ge(ld_ffn, 16 * 10)
            dve.wait_ge(s["wgt_turned"], 1)
            dve.tensor_tensor(base_t[:], turn[0][:, 0:2 * HID].rearrange("d (l h) -> d l h", l=LAYERS),
                              ident[:].unsqueeze(1).to_broadcast([P, LAYERS, P]), ALU.add)
            dve.tensor_copy(wi_t[:], turn[0][:, 256:256 + HID])
            dve.tensor_copy(wo_t[:], turn[0][:, 384:384 + D])
            dve.tensor_copy(b_t[:, 0:LAYERS * (EXPERTS + 1)], turn[1][:, 0:LAYERS * (EXPERTS + 1)]).then_inc(s["wgt_ready"], 1)
            dve.wait_ge(s["wgt_ready"], 1)
            for layer in range(LAYERS):
                shared = b_t[:, LAYERS * EXPERTS + layer:LAYERS * EXPERTS + layer + 1]
                dve.tensor_scalar(table[:, layer, 0:EXPERTS, HID], b_t[:, layer * EXPERTS:(layer + 1) * EXPERTS],
                                  shared, None, ALU.add)
                dve.tensor_copy(table[:, layer, EXPERTS, HID:HID + 1], shared)
                dve.tensor_copy(table[:, layer, EXPERTS, 0:HID], base_t[:, layer])
            step.seq(dve.tensor_copy(route_f[:], route_i[:]))
            dve.tensor_scalar(route_ok[:], route_f[:], 0.0, None, ALU.is_ge)
            dve.tensor_scalar(route_lo[:], route_f[:], float(EXPERTS - 1), None, ALU.is_le)
            step.seq(dve.tensor_scalar(route_x[:], route_f[:], float(-EXPERTS), None, ALU.add))
            step.seq(dve.tensor_tensor(route_ok[:], route_ok[:], route_lo[:], ALU.mult))
            step.seq(dve.tensor_tensor(route_x[:], route_x[:], route_ok[:], ALU.mult))
            dve.tensor_scalar(route_e[:], route_x[:], float(EXPERTS), None, ALU.add).then_inc(s["route_ready"], 1)
            for g in range(LAYERS * EXPERTS // 8):
                layer, e0 = g // 2, (g % 2) * 8
                dve.wait_ge(s["wgt_turned"], g + 2)
                dve.tensor_tensor(table[:, layer, e0:e0 + 8, 0:HID], wide[g % 2].rearrange("d (e h) -> d e h", e=8),
                                  base_t[:, layer].unsqueeze(1).to_broadcast([P, 8, HID]), ALU.add).then_inc(s["wgt_ready"], 1)

            dve.wait_ge(s["k_turned"], 1)
            dve.wait_ge(s["s_ready"], 2)
            dve.tensor_tensor(k_time[:].rearrange("p (v t) x d -> p t v (x d)", v=NV),
                              turn[0][:].rearrange("p (t v d) -> p t v d", t=NT, v=NV),
                              s_re[:].rearrange("p (v t) d -> p t v d", v=NV), ALU.add).then_inc(s["k_ready"], 1)
            dve.wait_ge(s["k_ready"], 1)
            odd_fly(lambda j: k_time[:, j].rearrange("p x d -> p (x d)"), xr, D).then_inc(s["k_fly"], 1)

            def to_ln_fm(count, par):
                dve.wait_ge(s["ln_turned"], count + 1)
                dve.tensor_copy(ln_fm[par][:], turn[par][:]).then_inc(s["ln_fm_ready"], 1)

            def inputs(pair, par):
                b = pair * 2 + par
                to_ln_fm(b, par)
                dve.wait_ge(s["q_mm"], b + 1)
                dve.tensor_copy(q_fm[par][:], wide[par]).then_inc(s["q_ready"], 1)

            def weighted(pair, par):
                b = pair * 2 + par
                dve.wait_ge(s["pv_step"], b * 8 + 12)
                dve.tensor_copy(pv_fm[par][:], acc[par]).then_inc(s["pv_copied"], 1)

            def residual(pair, par):
                b = pair * 2 + par
                dve.wait_ge(s["pv_turned"], b + 1)
                hb = seq_of(h, b)
                dve.tensor_tensor(hb, turn[par][:].rearrange("p (s d) -> p s d", d=D), hb, ALU.add).then_inc(s["h_ready"], 1)
                dve.wait_ge(s["h_ready"], b + B + 3)
                stats(b, hb, 1)

            with dve.Fori(0, B // 2) as pair:
                step.trip(pair, 2 * STATS)
                inputs(pair, 0)
                weighted(pair, 0)
                inputs(pair, 1)
                residual(pair, 0)
                weighted(pair, 1)
                residual(pair, 1)
            step.leave(B // 2)

            with dve.Fori(0, B // 2) as pair:
                step.trip(pair, 2 * STATS)
                for par in range(2):
                    to_ln_fm(pair * 2 + par + B, par)
                for layer in range(LAYERS):
                    for par in range(2):
                        dve.wait_ge(s["hid_mm"], pair * 6 + 2 * (layer + 1) + par + 1)
                        dve.wait_ge(s["staged_ready"], pair * 4 + 2 * layer + par + 1)
                        dve.tensor_tensor(hid_in[par][:].rearrange("h (g t) -> h g t", g=GPB),
                                          wide[par].rearrange("h (g t) -> h g t", g=GPB),
                                          over_last(staged[par][:, :, HID], GTOK), ALU.add).then_inc(s["bias_added"], 1)
                for par in range(2):
                    b = pair * 2 + par
                    dve.wait_ge(s["ffn_mm"], b + 1)
                    dve.wait_ge(s["bo_added"], b + 1)
                    hb = seq_of(h, b)
                    dve.tensor_tensor(hb, acc[par].rearrange("p (s d) -> p s d", d=D), hb, ALU.add).then_inc(s["h_ready"], 1)
                    dve.wait_ge(s["h_ready"], b + 2 * B + 3)
                    stats(b, hb, 2)
            step.leave(B // 2)

            n = B * D
            dve.wait_ge(s["ln_ready"], 3 * B + 1)
            odd_fly(lambda j: u[:, j].rearrange("p b d -> p (b d)"), xr, n).then_inc(s["u_fly"], 1)
            dve.wait_ge(s["u_dft"], 1)
            dve.wait_ge(s["k_mul_ready"], 1)
            for r in range(SETS):
                src = (wide_t[:, r // 2, (r % 2) * 512:(r % 2) * 512 + 512] if r < 4 else turn[r - 4][:])
                if r >= 2:
                    dve.wait_ge(s["y_ready"], r - 1)
                four = "p (c b d) -> p c b d"
                for part in range(2):
                    src_p = src.rearrange(four, c=2, b=B)[:, part]
                    dve.tensor_tensor(prod_a[r % 2][:, part].rearrange("p (b d) -> p b d", b=B), src_p,
                                      k_abd[:, r, part].unsqueeze(1).to_broadcast([P, B, D]), ALU.mult)
                last = dve.tensor_tensor(prod_b[r % 2][:].rearrange("p c (b d) -> p (c b) d", b=B),
                                         src.rearrange("p (c b d) -> p (c b) d", c=2, b=B),
                                         k_abd[:, r, 2].unsqueeze(1).to_broadcast([P, 2 * B, D]), ALU.mult)
                last.then_inc(s["u_prod"], 1)
            dve.wait_ge(s["z_copied"], SETS)
            zr = [z[:, r, 0] for r in range(SETS)]
            zi = [z[:, r, 1] for r in range(SETS)]
            f = [fly[:, i] for i in range(8)]
            tt, sst = dve.tensor_tensor, dve.scalar_tensor_tensor
            tt(f[0], zr[1], zr[5], ALU.add)
            tt(f[1], zr[1], zr[5], ALU.subtract)
            tt(f[2], zi[1], zi[5], ALU.add)
            step.seq(tt(f[3], zi[1], zi[5], ALU.subtract))
            sst(f[4], f[2], 0.5, zi[3], ALU.mult, ALU.add)
            step.seq(sst(f[5], f[0], 0.5, zr[3], ALU.mult, ALU.subtract))
            tt(odd[:, 0], f[0], zr[3], ALU.add)
            sst(odd[:, 1], f[1], COS30, f[4], ALU.mult, ALU.subtract)
            sst(odd[:, 2], f[3], -COS30, f[5], ALU.mult, ALU.add)
            tt(odd[:, 3], zi[3], f[2], ALU.subtract)
            sst(odd[:, 4], f[3], -COS30, f[5], ALU.mult, ALU.subtract)
            step.seq(sst(odd[:, 5], f[1], -COS30, f[4], ALU.mult, ALU.subtract))
            dve.wait_ge(s["even_ready"], 1)
            tt(fly[:, 8:14], even[:], odd[:], ALU.add)
            step.seq(tt(fly[:, 14:16], even[:, 0:2], odd[:, 0:2], ALU.subtract))
            with dve.Fori(0, B) as b:
                step.trip(b, STATS)
                y = fly[:, 8:16].rearrange("p (v t) (b d) -> p t v b d", v=NV, b=B)[:, :, :, ds(b, 1)].rearrange(
                    "p t v x d -> p t v (x d)")
                hb = seq_of(h, b)
                h4 = hb.rearrange("p (t v) d -> p t v d", v=NV)
                dve.wait_ge(s["bo_added"], 2 * B)
                dve.tensor_tensor(h4, h4, y, ALU.add).then_inc(s["h_ready"], 1)
                dve.wait_ge(s["h_ready"], b + 3 * B + 3)
                stats(b, hb, 3)
            step.leave(B)

            dve.wait_ge(ld_moe, 16 * 11)
            dve.wait_ge(s["wgt_turned"], LAYERS * EXPERTS // 8 + 2)
            dve.tensor_copy(rw_t[:], acc[0][:, 0:MOE])
            dve.tensor_copy(b1_t[:], acc[0][:, 16:16 + PAIRS]).then_inc(s["wgt_ready"], 1)
            SOFTMAX = 17
            with dve.Fori(0, B // 2) as pair:
                step.trip(pair, SOFTMAX)
                for par in range(2):
                    to_ln_fm(pair * 2 + par + 2 * B, par)
                dve.wait_ge(s["route_mm"], pair + 1)
                logits = acc_t[:, :, 0:SLOTS * MOE].rearrange("p v (s e) -> p v s e", e=MOE)
                m1, m2, k1, tot, rec = (t[:] for t in sm_r)
                by_half = "p (v s) e -> p v s e"
                step.seq(dve.tensor_reduce(m1.rearrange("p (v s) -> p v s", v=NV), logits, AX.X, ALU.max))
                dve.tensor_tensor(sm_d[:].rearrange(by_half, v=NV), logits,
                                  over_last(m1, MOE).rearrange(by_half, v=NV), ALU.subtract).then_inc(s["sm_in"], 1)
                dve.wait_ge(s["sm_exp"], pair + 1)
                step.seq(dve.tensor_reduce(tot, sm_p[:], AX.X, ALU.add))
                step.seq(dve.reciprocal(rec, tot))
                step.seq(dve.tensor_tensor(sm_p[:], sm_p[:], over_last(rec, MOE), ALU.mult))
                weight = first_w[:].unsqueeze(1).to_broadcast([P, 2 * SLOTS, MOE])

                def largest(src, top, one):
                    step.seq(dve.tensor_reduce(top, src, AX.X, ALU.max))
                    step.seq(dve.tensor_tensor(sm_key[:], src, over_last(top, MOE), ALU.is_equal))
                    step.seq(dve.tensor_tensor(sm_key[:], sm_key[:], weight, ALU.mult))
                    step.seq(dve.tensor_reduce(k1, sm_key[:], AX.X, ALU.max))
                    step.seq(dve.tensor_tensor(one, sm_key[:], over_last(k1, MOE), ALU.is_equal))

                largest(sm_p[:], m1, sm_one[0][:])
                step.seq(dve.scalar_tensor_tensor(sm_d[:], sm_one[0][:], -2.0, sm_p[:], ALU.mult, ALU.add))
                largest(sm_d[:], m2, sm_one[1][:])
                dve.tensor_tensor(sm_one[0][:], sm_one[0][:], sm_one[1][:], ALU.add)
                step.seq(dve.tensor_tensor(tot, m1, m2, ALU.add))
                step.seq(dve.tensor_scalar(tot, tot, 1e-12, None, ALU.max))
                dve.tensor_tensor(sm_c[:], sm_one[0][:], sm_p[:], ALU.mult)
                dve.reciprocal(rec, tot).then_inc(s["gate_step"], 1)
                dve.wait_ge(s["gate_step"], pair * 5 + 1)
                dve.tensor_tensor(sm_c[:], sm_c[:], over_last(rec, MOE), ALU.mult).then_inc(s["gate_step"], 1)
                dve.wait_ge(s["gate_step"], pair * 5 + 2)
                dve.tensor_copy(split[:, :, 0:MOE], sm_c[:]).then_inc(s["gate_step"], 1)
                dve.wait_ge(s["gate_step"], pair * 5 + 3)
                dve.tensor_tensor(sm_key[:], sm_c[:], split[:, :, 0:MOE], ALU.subtract).then_inc(s["gate_step"], 1)
                dve.wait_ge(s["gate_step"], pair * 5 + 4)
                dve.tensor_copy(split[:, :, MOE:2 * MOE], sm_key[:]).then_inc(s["gate_step"], 1)
                dve.wait_ge(s["gate_step"], pair * 5 + 5)
                dve.tensor_tensor(split[:, :, 2 * MOE:3 * MOE], sm_key[:], split[:, :, MOE:2 * MOE],
                                  ALU.subtract).then_inc(s["split_ready"], 1)
                for par in range(2):
                    b = pair * 2 + par
                    dve.wait_ge(s["gate_turned"], b + 1)
                    dve.tensor_copy(gate_t[par][:], turn[par][0:3 * MOE].bitcast(BF16)).then_inc(s["gate_ready"], 1)
                for par in range(2):
                    b = pair * 2 + par
                    for qd in range(PAIRS):
                        dve.wait_ge(s["gelu_ready"], b * PAIRS + qd + 2)
                        dve.wait_ge(s["gate_mm"], b * PAIRS + qd + 1)
                        dve.wait_ge(s["down_mm"], b * PAIRS + qd + 1)
                        dve.tensor_tensor(gated[qd % 2][:], gelu[qd % 2][:], wide[1], ALU.mult).then_inc(s["gated_ready"], 1)
                    dve.wait_ge(s["down_mm"], b * PAIRS + PAIRS + 2)
                    dve.tensor_copy(moe_fm[par][:], acc[par]).then_inc(s["moe_copied"], 1)
                for par in range(2):
                    b = pair * 2 + par
                    dve.wait_ge(s["moe_turned"], b + 1)
                    dve.wait_ge(s["bo_added"], b + 2 * B + 1)
                    if par == 0:
                        dve.wait_ge(s["res_stored"], pair * (16 * NV * 2) + 16)
                    dve.tensor_tensor(result[par][:], turn[par][:].rearrange("p (s d) -> p s d", d=D), seq_of(h, b),
                                      ALU.add).then_inc(s["res_ready"], 1)
            step.leave(B // 2)

        @block.gpsimd
        def _(pool):
            step = Steps(pool, ge)
            pool.sem_inc(s["pv_step"], 4)
            pool.sem_inc(s["down_mm"], 2)
            pool.sem_inc(s["ln_ready"], 1)
            tt = pool.tensor_tensor
            pool.memset(minus_half[:], -0.5).then_inc(s["begun"], 1)
            pool.wait_ge(s["begun"], 1)

            def normalise(index, b, dst, waits):
                pool.wait_ge(s["stats_ready"], index + 2)
                stand_apart(pool)
                tt(small_of(rstd, b), small_of(var, b), minus_half[:], ALU.pow)
                pool.wait_ge(s["ln_ready"], index + 1)
                stand_apart(pool)
                step.seq(tt(centred[:], seq_of(h, b), over_last(small_of(mean, b), D), ALU.subtract))
                waits()
                stand_apart(pool)
                return tt(dst, centred[:], over_last(small_of(rstd, b), D), ALU.mult)

            def even_fly(src, dst, n):
                f = [fly[:, 8 + i, 0:n] for i in range(8)]
                o = [dst[:, i, 0:n] for i in range(NX)]
                tt(f[0], src(0), src(6), ALU.add)
                step.seq(tt(f[1], src(1), src(7), ALU.add))
                tt(f[2], f[0], src(3), ALU.add)
                tt(f[3], f[1], src(4), ALU.add)
                tt(f[4], src(2), src(5), ALU.add)
                tt(f[5], f[0], src(3), ALU.subtract)
                tt(f[6], f[1], src(4), ALU.subtract)
                step.seq(tt(f[7], src(2), src(5), ALU.subtract))
                tt(f[0], f[3], f[4], ALU.add)
                tt(o[9], f[3], f[4], ALU.subtract)
                tt(o[5], f[6], f[7], ALU.add)
                step.seq(tt(f[1], f[6], f[7], ALU.subtract))
                tt(o[0], f[2], f[0], ALU.add)
                tt(o[1], f[5], f[1], ALU.subtract)
                pool.tensor_scalar(f[3], f[0], -0.5, 0.0, ALU.mult, ALU.add)
                step.seq(pool.tensor_scalar(f[4], f[1], 0.5, 0.0, ALU.mult, ALU.add))
                tt(o[8], f[3], f[2], ALU.add)
                return tt(o[4], f[4], f[5], ALU.add)

            pool.wait_ge(s["tab_mul"], 1)
            pool.wait_ge(s["sin_in"], 1)
            tt(row_e[:], ramp[:].unsqueeze(1).to_broadcast([P, NS, P]), over_last(lam[:], P), ALU.mult).then_inc(s["exp_in"], 1)
            pool.wait_ge(s["exp_out"], 2)
            pool.wait_ge(s["sin_out"], 1)
            tt(beta[:], row_z[:], row_e[:], ALU.mult).then_inc(s["beta_ready"], 1)

            pool.wait_ge(s["k_ready"], 1)
            even_fly(lambda j: k_time[:, j].rearrange("p x d -> p (x d)"), xr, D).then_inc(s["k_fly"], 1)
            pool.wait_ge(s["k_spec_ready"], 1)
            for i, dst in enumerate((0, 2, 1)):
                step.wait()
                tt(k_mul[0][:], k_spec[:, :, 0], over_last(phase[:, 2 * i], D), ALU.mult)
                step.seq(tt(k_mul[1][:], k_spec[:, :, 1], over_last(phase[:, 2 * i + 1], D), ALU.mult))
                step.done(tt(k_abd[:, :, dst], k_mul[0][:], k_mul[1][:], ALU.add))
            step.wait()
            pool.sem_inc(s["k_mul_ready"], 1)

            with pool.Fori(0, B // 2) as pair:
                step.trip(pair, 2)
                for par in range(2):
                    b = pair * 2 + par
                    normalise(b, b, ln[par][:], lambda: pool.wait_ge(s["pv_copied"], b + 1)).then_inc(s["ln_ready"], 1)
            step.leave(B // 2)

            pool.wait_ge(s["route_ready"], 1)
            pool.wait_ge(s["wgt_ready"], 1 + LAYERS * EXPERTS // 8)
            pool.wait_ge(s["pv_copied"], B + 2)
            with pool.Fori(0, B // 2) as pair:
                step.trip(pair, 2)
                for par in range(2):
                    b = pair * 2 + par
                    normalise(b + B, b, ln[par][:], lambda: pool.wait_ge(s["ln_turned"], b + 3)).then_inc(s["ln_ready"], 1)
                for layer in range(LAYERS):
                    for par in range(2):
                        b = pair * 2 + par
                        pool.wait_ge(s["bias_added"], pair * 4 + 2 * layer + par + 1)
                        stand_apart(pool)
                        for g in range(GPB):
                            e = pool.value_load(route_e[0:1, ds(b * GPB + g, 1)], min_val=0, max_val=EXPERTS)
                            last = pool.tensor_copy(staged[par][:, g, :], table[:, layer, ds(e, 1), :].rearrange(
                                "d x h -> d (x h)"))
                        last.then_inc(s["staged_ready"], 1)
                    if layer == 0:
                        stand_apart(pool)
                        for par in range(2):
                            hb = seq_of(h, pair * 2 + par)
                            tt(hb, hb, bo_b[:].unsqueeze(1).to_broadcast([P, SLOTS, D]), ALU.add).then_inc(s["bo_added"], 1)
            step.leave(B // 2)

            pool.wait_ge(ld_conv, 16 * 5)
            with pool.Fori(0, B) as b:
                step.trip(b, 1)
                pool.wait_ge(s["stats_ready"], b + 2 * B + 2)
                stand_apart(pool)
                tt(small_of(rstd, b), small_of(var, b), minus_half[:], ALU.pow)
                pool.wait_ge(s["ln_ready"], b + 2 * B + 1)
                step.done(tt(centred[:], seq_of(h, b), over_last(small_of(mean, b), D), ALU.subtract))
                hb = seq_of(h, b)
                tt(hb, hb, dvec_b[:].unsqueeze(1).to_broadcast([P, SLOTS, D]), ALU.add).then_inc(s["bo_added"], 1)
                ub = u[:, :, ds(b, 1)].rearrange("p (v t) x d -> p v t (x d)", v=NV)
                r4 = small_of(rstd, b).rearrange("p (t v) -> p v t", v=NV).unsqueeze(3).to_broadcast([P, NV, NT, D])
                step.wait()
                stand_apart(pool)
                tt(ub, centred[:].rearrange("p (t v) d -> p v t d", v=NV), r4, ALU.mult).then_inc(s["ln_ready"], 1)
            step.leave(B)
            pool.wait_ge(s["ln_ready"], 3 * B + 1)
            even_fly(lambda j: u[:, j].rearrange("p b d -> p (b d)"), xr, B * D).then_inc(s["u_fly"], 1)
            for r in range(SETS):
                pool.wait_ge(s["u_prod"], r + 1)
                a_, b_ = prod_a[r % 2], prod_b[r % 2]
                tt(y_spec[:, r, 0], a_[:, 0], b_[:, 1], ALU.subtract)
                tt(y_spec[:, r, 1], b_[:, 0], a_[:, 1], ALU.add).then_inc(s["y_ready"], 1)
            pool.wait_ge(s["z_copied"], SETS)
            z0, z6 = z[:, 0, 0], z[:, 0, 1]
            z2r, z2i, z4r, z4i = z[:, 2, 0], z[:, 2, 1], z[:, 4, 0], z[:, 4, 1]
            f = [fly[:, 8 + i] for i in range(8)]
            tt(f[0], z0, z4r, ALU.add)
            tt(f[3], z2r, z6, ALU.add)
            pool.tensor_scalar(f[1], z4r, -0.5, 0.0, ALU.mult, ALU.add)
            step.seq(pool.tensor_scalar(f[4], z2r, 0.5, 0.0, ALU.mult, ALU.add))
            tt(f[2], f[1], z0, ALU.add)
            step.seq(tt(f[5], f[4], z6, ALU.subtract))
            tt(f[1], f[2], z4i, ALU.subtract)
            tt(f[6], f[2], z4i, ALU.add)
            tt(f[4], f[5], z2i, ALU.subtract)
            step.seq(tt(f[7], f[5], z2i, ALU.add))
            tt(even[:, 0], f[0], f[3], ALU.add)
            tt(even[:, 3], f[0], f[3], ALU.subtract)
            tt(even[:, 1], f[1], f[4], ALU.add)
            tt(even[:, 4], f[1], f[4], ALU.subtract)
            tt(even[:, 2], f[6], f[7], ALU.subtract)
            tt(even[:, 5], f[6], f[7], ALU.add).then_inc(s["even_ready"], 1)

            pool.wait_ge(ld_moe, 16 * 11)
            pool.tensor_copy(sel[:], sel_f[:])
            pool.tensor_copy(ident_b[:], ident[:])
            step.seq(pool.tensor_copy(b2_s[:, 0], b2_f[:]))
            step.seq(tt(b2_r[:, 0], b2_f[:], b2_s[:, 0], ALU.subtract))
            step.seq(pool.tensor_copy(b2_s[:, 1], b2_r[:, 0]))
            step.seq(tt(b2_r[:, 1], b2_r[:, 0], b2_s[:, 1], ALU.subtract))
            pool.tensor_copy(b2_s[:, 2], b2_r[:, 1]).then_inc(s["moe_bias_ready"], 1)
            with pool.Fori(0, B // 2) as pair:
                step.trip(pair, 2)
                for par in range(2):
                    b = pair * 2 + par
                    normalise(b + 3 * B, b, ln[par][:], lambda: pool.wait_ge(s["ln_turned"], b + 2 * B - 1)).then_inc(s["ln_ready"], 1)
                for par in range(2):
                    b = pair * 2 + par
                    pool.wait_ge(s["ln_ready"], b + 3 * B + 2)
                    stand_apart(pool)
                    hb = seq_of(h, b)
                    tt(hb, hb, ln[par][:], ALU.add).then_inc(s["bo_added"], 1)
            step.leave(B // 2)


_INS = {
    "x": "x", "L0_tok_W": "tok_w", "L0_attn_q_weight": "q_w", "L0_ffn_route_id": "route", "L0_ffn_Wi": "wi",
    "L0_ffn_bi": "bi", "L0_ffn_Wr": "wr", "L0_ffn_br": "br", "L0_ffn_Ws": "ws", "L0_ffn_bs": "bs",
    "L0_ffn_Wo": "wo", "L0_ffn_bo": "bo", "L1_attn_A_real": "a_re", "L1_attn_A_imag": "a_im",
    "L1_attn_C_real": "c_re", "L1_attn_C_imag": "c_im", "L1_attn_D": "dvec", "L1_ffn_router_w": "router_w",
    "L1_ffn_w1": "w1", "L1_ffn_b1": "b1", "L1_ffn_w2": "w2", "L1_ffn_b2": "b2",
}


def kernel(**inputs):
    from concourse import bacc
    from concourse.bass_utils import run_bass_kernel_spmd

    nc = bacc.Bacc("TRN2", target_bir_lowering=False, num_devices=1)
    arrays, args = {}, {}
    for name, short in _INS.items():
        arrays["in_" + short] = np.ascontiguousarray(inputs[name])
    for name, a in constants().items():
        arrays["in_" + name] = np.ascontiguousarray(a)
    for name, a in arrays.items():
        args[name[3:]] = nc.dram_tensor(name, a.shape, mybir.dt.from_np(a.dtype), kind="ExternalInput").ap()
    args["out"] = nc.dram_tensor("out_0", (B, L, D), F32, kind="ExternalOutput").ap()
    build_tower(nc, **args)
    r = run_bass_kernel_spmd(nc, [arrays], core_ids=[0])
    return r.results[0]["out_0"]
```

```python
from contextlib import ExitStack
import math

import numpy as np

import concourse.bass as bass
from concourse import mybir

ALU = mybir.AluOpType
ACT = mybir.ActivationFunctionType
AX = mybir.AxisListType
F32 = mybir.dt.float32
BF16 = mybir.dt.bfloat16
I32 = mybir.dt.int32
ds = bass.ds

B, C, T_IN, V = 4, 64, 128, 64
D = 64
PATCH, STRIDE = 16, 8
NPATCH = T_IN // STRIDE
NF = PATCH // 2 + 1
RF = 2 * NF
Q4 = STRIDE // 2
L = V * NPATCH
P = 128
NT, NV = 4, 2
SLOTS = NT * NV
HID = 128
LAYERS, EXPERTS = 2, 16
GROUPS = 64
GPB = GROUPS // B
GTOK = B * L // GROUPS
NS = 32
DT = 0.1
NFFT = 1536
RADIX = NFFT // P
NX = RADIX
SETS = RADIX // 2
NBLK = 2 + 4 * (SETS - 1)
SHIFT = (L - 1) // 2
COS30 = math.sqrt(0.75)
MOE, TOPW = 8, 2
PAIRS = MOE // 2
EPS = 1e-5
POOL_GROUPS = 5
ROUND = 1.5 * 2.0 ** 23
TURN = 6.2831850
NTAB = 2 * L // P + L // P
NCOL = NTAB + 1


def patch_dft():
    a = 2 * np.pi * np.arange(NF)[:, None] * np.arange(PATCH)[None, :] / PATCH
    return np.concatenate([np.cos(a), -np.sin(a)]) / math.sqrt(PATCH)


def forward_blocks():
    p = np.arange(P)[:, None]
    out = np.zeros((P, NBLK, P))
    g = np.arange(64)[None, :]
    for half, r in ((0, 0), (1, 6)):
        a = 2 * np.pi * (RADIX * g + r) * p / NFFT
        c, s = np.cos(a), -np.sin(a)
        if r == 0:
            s[:, 0] = np.cos(np.pi * p[:, 0])
        out[:, 0, half * 64:half * 64 + 64] = c
        out[:, 1, half * 64:half * 64 + 64] = s
    g = np.arange(P)[None, :]
    for r in range(1, SETS):
        a = 2 * np.pi * (RADIX * g + r) * p / NFFT
        fold = -1.0 if r % 2 else -COS30
        k = 4 * r - 2
        out[:, k + 0] = np.cos(a)
        out[:, k + 1] = fold * np.sin(a)
        out[:, k + 2] = -np.sin(a)
        out[:, k + 3] = fold * np.cos(a)
    return out


def inverse_blocks():
    p = np.arange(P)[None, :]
    out = np.zeros((P, NBLK, P))
    g = np.arange(64)[:, None]
    for half, r in ((0, 0), (1, 6)):
        a = 2 * np.pi * (RADIX * g + r) * p / NFFT
        c, s = 2 * np.cos(a) / NFFT, -2 * np.sin(a) / NFFT
        if r == 0:
            c[0] /= 2
            s[0] = np.cos(np.pi * p[0]) / NFFT
        out[half * 64:half * 64 + 64, 0] = c
        out[half * 64:half * 64 + 64, 1] = s
    g = np.arange(P)[:, None]
    for r in range(1, SETS):
        a = 2 * np.pi * (RADIX * g + r) * p / NFFT
        c, s = 2 * np.cos(a) / NFFT, 2 * np.sin(a) / NFFT
        fold = 1.0 if r % 2 else COS30
        k = 4 * r - 2
        out[:, k + 0], out[:, k + 1] = c, -s
        out[:, k + 2], out[:, k + 3] = fold * s, fold * c
    return out


def phase_tables():
    f = np.zeros((P, SETS))
    f[:64, 0] = RADIX * np.arange(64)
    f[64:, 0] = RADIX * np.arange(64) + 6
    for r in range(1, SETS):
        f[:, r] = RADIX * np.arange(P) + r
    a = 2 * np.pi * f * SHIFT / NFFT
    c, s = np.cos(a), np.sin(a)
    cb, sb, cd, sd = c.copy(), s.copy(), c.copy(), s.copy()
    cb[0, 0] = sb[0, 0] = 0.0
    cd[0, 0], sd[0, 0] = 0.0, 1.0
    return np.stack([c, -s, -sb, -cb, cd, -sd], 1)


def hilbert_band():
    m = (np.arange(3 * L)[None, :] - (2 * L - P)) - np.arange(P)[:, None]
    odd = m % 2 != 0
    h = np.zeros(m.shape)
    h[odd] = -1.0 / (L * np.tan(np.pi * m[odd] / (2 * L)))
    return h


def turn_offsets():
    im = (np.arange(P) // NS) % 2
    off = np.zeros((P, 2, NCOL))
    shift = np.zeros((P, NCOL))
    shift[:, :2 * L // P] = np.where(im[:, None] == 1, -0.25, 0.0)
    shift[:, 2 * L // P:NTAB] = np.where(im[:, None] == 1, 0.0, 0.25)
    off[:, 0] = shift + 0.25
    off[:, 1] = shift
    return off


def constants():
    f = np.float32
    im = ((np.arange(P) // NS) % 2).astype(f)
    cols = np.concatenate([P * np.arange(2 * L // P), P * np.arange(L // P), [2 * L]])
    sel = np.zeros((3 * MOE, PAIRS, P), f)
    for i in range(3):
        for e in range(MOE):
            sel[i * MOE + e, e // 2, (e % 2) * 64:(e % 2) * 64 + 64] = 1
    return {
        "c_ident": np.eye(P, dtype=f),
        "c_dft": patch_dft().astype(f),
        "c_fwd": forward_blocks().astype(f),
        "c_inv": inverse_blocks().astype(f),
        "c_phase": phase_tables().astype(f),
        "c_hilb": hilbert_band().astype(f),
        "c_ramp": np.broadcast_to(np.arange(P, dtype=f), (P, P)).copy(),
        "c_cols": np.broadcast_to(cols.astype(f), (P, NCOL)).copy(),
        "c_off": turn_offsets().astype(f),
        "c_quarter": (0.25 * im)[:, None].astype(f),
        "c_first": np.broadcast_to(MOE - np.arange(MOE, dtype=f), (P, MOE)).copy(),
        "c_sel": sel,
    }


class Steps:

    def __init__(self, engine, sem):
        self.engine, self.sem, self.base, self.n = engine, sem, 0, 0

    def done(self, instruction):
        instruction.then_inc(self.sem, 1)
        self.n += 1

    def wait(self):
        self.engine.wait_ge(self.sem, self.base + self.n)

    def seq(self, instruction):
        self.done(instruction)
        self.wait()

    def trip(self, index, per_trip):
        self.first = self.base + self.n
        self.per = per_trip
        self.base, self.n = index * per_trip + self.first, 0

    def leave(self, trips):
        assert self.n == self.per, (self.n, self.per)
        self.base, self.n = self.first + trips * self.per, 0


def seq_of(ap, b):
    return ap[:, ds(b, 1)].rearrange("p x s d -> p (x s) d")


def small_of(ap, b):
    return ap[:, ds(b, 1)].rearrange("p x s -> p (x s)")


def over_last(ap, n):
    return ap.unsqueeze(2).to_broadcast([ap.shape[0], ap.shape[1], n])


def build_tower(nc, x, tok_w, q_w, route, wi, bi, wr, br, ws, bs, wo, bo, a_re, a_im, c_re, c_im, dvec,
                router_w, w1, b1, w2, b2, c_ident, c_dft, c_fwd, c_inv, c_phase, c_hilb, c_ramp, c_cols,
                c_off, c_quarter, c_first, c_sel, out, **taps):
    with ExitStack() as ctx:
        def sb(name, shape, dt=F32):
            return ctx.enter_context(nc.sbuf_tensor(name, shape, dt))

        def region(name, floats):
            return sb(name, [P, floats])

        def part(area, first, shape, dt=F32):
            floats = math.prod(shape[1:]) * mybir.dt.size(dt) // 4
            ap = area[0:shape[0], first:first + floats]
            if dt != F32:
                ap = ap.bitcast(dt)
            if len(shape) == 2:
                return ap
            names = ["x%d" % i for i in range(len(shape) - 1)]
            return ap.rearrange("p (%s) -> p %s" % (" ".join(names), " ".join(names)),
                                **dict(zip(names[1:], shape[2:])))

        def sem(name):
            return ctx.enter_context(nc.semaphore(name))

        ident = sb("ident", [P, P])
        ident_b = sb("ident_b", [P, P], BF16)
        dft = sb("dft", [RF, PATCH])
        weff = sb("weff", [P, Q4, 2, D])
        wq = sb("wq", [P, 2, D])
        wq_s = sb("wq_s", [P, 3, 2 * D], BF16)
        wi_f = sb("wi_f", [P, HID])
        wi_s = sb("wi_s", [P, 3, HID], BF16)
        w1_f = sb("w1_f", [P, MOE, D])
        rw_f = sb("rw_f", [P, MOE])
        rw_s = sb("rw_s", [P, 3, MOE], BF16)
        w1_s = sb("w1_s", [P, 3, MOE * D], BF16)
        alpha = sb("alpha", [P, NS, 2, NTAB])
        wi_raw = sb("wi_raw", [HID, 2, D])
        ws_raw = sb("ws_raw", [HID, LAYERS, HID])
        base_t = sb("base_t", [HID, LAYERS, HID])
        b_raw = sb("b_raw", [LAYERS * (EXPERTS + 2), HID])
        b_t = sb("b_t", [HID, LAYERS * (EXPERTS + 2)])
        bi_c = sb("bi_c", [HID, 1])
        wo_raw = sb("wo_raw", [D, HID])
        wo_t = sb("wo_t", [HID, D])
        bo_b = sb("bo_b", [P, D])
        route_i = sb("route_i", [1, GROUPS], I32)
        route_f = sb("route_f", [1, GROUPS])
        route_ok = sb("route_ok", [1, GROUPS])
        route_lo = sb("route_lo", [1, GROUPS])
        route_x = sb("route_x", [1, GROUPS])
        route_e = sb("route_e", [1, GROUPS], I32)
        dvec_b = sb("dvec_b", [P, D])
        phase = sb("phase", [P, 6, SETS])
        ramp = sb("ramp", [P, P])
        cols = sb("cols", [P, NCOL])
        off = sb("off", [P, 2, NCOL])
        quarter = sb("quarter", [P, 1])
        rw_raw = sb("rw_raw", [MOE, 2, D])
        b1_raw = sb("b1_raw", [PAIRS, P])
        b1_t = sb("b1_t", [P, PAIRS])
        w2_s = sb("w2_s", [P, PAIRS, D])
        b2_f = sb("b2_f", [3 * MOE, D])
        b2_r = sb("b2_r", [3 * MOE, 2, D])
        b2_s = sb("b2_s", [3 * MOE, 3, D], BF16)
        first_w = sb("first_w", [P, MOE])
        sel_f = sb("sel_f", [3 * MOE, PAIRS, P])
        sel = sb("sel", [3 * MOE, PAIRS, P], BF16)
        minus_half = sb("minus_half", [P, SLOTS])

        area = region("area_x", 2 * (NPATCH + 1) * Q4 * V)
        x_one = (NPATCH + 1) * Q4 * V
        xs = [part(area, i * x_one, [P, NPATCH + 1, Q4, V]) for i in range(2)]
        hilb = part(area, 0, [P, 3 * L])
        fwd = part(area, 3 * L, [P, NBLK, P])
        inv = part(area, 3 * L + NBLK * P, [P, NBLK, P])

        area = region("area_w", 4096)
        tokw = part(area, 0, [RF, D, C])
        wr_raw = part(area, 0, [HID, LAYERS * EXPERTS, HID])
        k_spec = part(area, 0, [P, SETS, 2, D])
        k_mul = [part(area, (2 + i) * SETS * D, [P, SETS, D]) for i in range(2)]
        k_abd = part(area, 4 * SETS * D, [P, SETS, 3, D])
        even = part(area, 0, [P, SETS, B * D])
        odd = part(area, SETS * B * D, [P, SETS, B * D])
        result = [part(area, i * 512, [P, SLOTS, D]) for i in range(2)]
        gate_t = [part(area, 3072 + i * L // 2, [3 * MOE, L], BF16) for i in range(2)]

        area = region("area_t", LAYERS * (EXPERTS + 1) * (HID + 1))
        table = part(area, 0, [HID, LAYERS, EXPERTS + 1, HID + 1])
        u = part(area, 0, [P, L // P, B, D])
        gelu = [part(area, i * L, [P, L]) for i in range(2)]
        gated = [part(area, (2 + i) * L, [P, L]) for i in range(2)]

        area = region("area_a", 4096)
        row_y = part(area, 0, [P, NS, P])
        row_e = part(area, 0, [P, NS, P])
        att = [part(area, i * L, [P, L]) for i in range(4)]
        fly = part(area, 0, [P, 16, B * D])

        area = region("area_b", 4096)
        row_z = part(area, 0, [P, NS, P])
        beta = part(area, 0, [P, NS, P])
        hid = [part(area, i * L, [HID, L]) for i in range(2)]
        hid_in = [part(area, (2 + i) * L, [HID, L]) for i in range(2)]
        y_spec = part(area, 0, [P, SETS, 2, B * D])

        area = region("area_s", 6 * NS * NCOL)
        col_y = part(area, 0, [P, NS, NCOL])
        col_e = part(area, NS * NCOL, [P, NS, NCOL])
        col_tab = part(area, 2 * NS * NCOL, [P, 2, NS, NCOL])
        col_z = part(area, 4 * NS * NCOL, [P, 2, NS, NCOL])
        q_s = [part(area, i * 3 * L // 2, [P, 3, L], BF16) for i in range(2)]
        q_rest = part(area, 3 * L, [P, L])
        staged = [part(area, i * GPB * (HID + 1), [HID, GPB, HID + 1]) for i in range(2)]
        z = part(area, 0, [P, SETS, 2, B * D])
        sm_d, sm_p, sm_key, sm_c, *sm_one = [
            part(area, i * 2 * SLOTS * MOE, [P, 2 * SLOTS, MOE]) for i in range(6)]

        area = region("area_q", 2 * L)
        s_im = part(area, 0, [P, 2 * L // P, D])
        s_re = part(area, L, [P, L // P, D])
        k_fm = part(area, L + L // 2, [P, NT * P])
        parts = [part(area, i * L, [P, SLOTS, 2, 2, D], BF16) for i in range(2)]
        prod_a = [part(area, i * 512, [P, 2, B * D]) for i in range(2)]
        prod_b = [part(area, (2 + i) * 512, [P, 2, B * D]) for i in range(2)]

        area = region("area_f", 2 * NT * P)
        tok_fm = [part(area, i * NT * P, [P, NT * P]) for i in range(2)]
        pv_fm = [part(area, i * NT * P, [P, NT * P]) for i in range(2)]
        moe_fm = [part(area, i * NT * P, [P, NT * P]) for i in range(2)]
        xr = sb("xr", [P, NX, B * D])

        h = sb("h", [P, B, SLOTS, D])
        mean = sb("mean", [P, B, SLOTS])
        var = sb("var", [P, B, SLOTS])
        rstd = sb("rstd", [P, B, SLOTS])
        stat = sb("stat", [P, SLOTS, 6])
        st = [sb(f"st{i}", [P, SLOTS]) for i in range(5)]
        centred = sb("centred", [P, SLOTS, D])
        ln_t = sb("ln", [P, B, SLOTS, D])
        ln = [ln_t[:, i] for i in range(B)]
        ln_rest = sb("ln_rest", [P, SLOTS, D])
        fm = [sb(f"fm{i}", [P, 2, L], BF16) for i in range(2)]

        par_raw = sb("par_raw", [D, 4, 4, NS])
        par_t = sb("par_t", [P, 4, NS])
        lam = sb("lam", [P, NS])
        turns = sb("turns", [P, NS])
        small = [sb(f"small{i}", [P, NS]) for i in range(6)]
        k_time = sb("k_time", [P, L // P, 1, D])
        sm_r = [sb(f"sm_r{i}", [P, 2 * SLOTS]) for i in range(5)]
        split = sb("split", [P, 2 * SLOTS, 3 * MOE], BF16)

        wide_t = ctx.enter_context(nc.psum_tensor("wide", [P, 2, 2 * 512], F32))
        wide = [wide_t[:, i] for i in range(2)]
        turn_t = ctx.enter_context(nc.psum_tensor("turn", [P, 2, 512], F32))
        turn = [turn_t[:, i] for i in range(2)]
        turn_b = [turn_t[:, i].bitcast(BF16) for i in range(2)]
        turn_all = turn_t[:].rearrange("p x k -> p (x k)")
        acc_t = ctx.enter_context(nc.psum_tensor("acc", [P, 2, 512], F32))
        acc = [acc_t[:, i] for i in range(2)]

        ld_tok, ld_attn, ld_ffn, ld_ssm, ld_conv, ld_moe = (
            sem(n) for n in ("ld_tok", "ld_attn", "ld_ffn", "ld_ssm", "ld_conv", "ld_moe"))
        x_in = [sem(f"x_in{i}") for i in range(2)]
        ve, ae, pe_s, ge = sem("dve_step"), sem("act_step"), sem("pe_step"), sem("pool_step")
        s = {n: sem(n) for n in (
            "weff_mm", "weff_ready", "tok_mm", "tok_copied", "tok_turned", "h_ready", "stats_ready",
            "ln_ready", "top_ready", "parts_ready", "ln_turned", "fm_a_ready", "fm_b_ready", "weights_split",
            "ident_ready", "q_top",
            "q_mm", "q_ready", "score_mm", "att_ready", "pv_step", "pv_mm", "pv_copied", "pv_turned",
            "wgt_turned", "wgt_ready", "begun", "route_ready", "staged_ready", "bo_added",
            "hid_mm", "hid_relu", "bias_added", "ffn_mm", "staged_used",
            "par_turned", "tab_mul", "tab_ready", "exp_in", "exp_out", "sin_in", "sin_out",
            "s_mm", "s_ready", "hil_mm", "hil_copied", "k_turned", "k_ready", "k_fly", "k_dft",
            "k_spec_ready", "k_mul_ready", "u_ready", "u_fly", "u_dft", "u_prod", "y_ready", "z_mm",
            "z_copied", "even_ready", "route_mm", "sm_in", "sm_exp", "split_ready", "gate_turned",
            "gate_ready", "up_mm", "gelu_ready", "gate_mm", "gated_ready", "down_mm", "moe_copied",
            "moe_turned", "res_ready", "res_stored", "beta_ready", "alpha_ready", "small_turned",
            "moe_bias_ready", "gate_step", "passed", "staged_more")}
        block = ctx.enter_context(nc.Block())

        def stand_apart(engine):
            engine.sem_inc(s["passed"], 1)

        @block.sync
        def _(sp):
            sp.dma_start(ident[:], c_ident).then_inc(ld_tok, 16)
            sp.dma_start(dft[:], c_dft).then_inc(ld_tok, 16)
            sp.dma_start(tokw[:], tok_w.rearrange("o (r c) -> r o c", c=C)).then_inc(ld_tok, 16)

            def load_x(b, par):
                src = x[b].rearrange("c (n h q) v -> h c n (q v)", h=2, q=Q4)
                edge = x[b, :, T_IN - 1:T_IN, :]
                for hh in range(2):
                    half = xs[par][hh * C:(hh + 1) * C]
                    sp.dma_start(half[:, 0:NPATCH].rearrange("c n q v -> c n (q v)"),
                                 src[hh]).then_inc(x_in[par], 16)
                    sp.dma_start(half[:, NPATCH], edge.to_broadcast([C, Q4, V])).then_inc(x_in[par], 16)

            for i, a in enumerate((a_re, a_im, c_re, c_im)):
                sp.dma_start(par_raw[:, i], a.unsqueeze(1).to_broadcast([D, 4, NS])).then_inc(ld_ssm, 16)
            for dst, src in ((ramp, c_ramp), (cols, c_cols), (off, c_off), (quarter, c_quarter)):
                sp.dma_start(dst[:], src).then_inc(ld_ssm, 16)
            load_x(0, 0)
            load_x(1, 1)
            for i in range(2):
                sp.dma_start(wq[i * D:(i + 1) * D], q_w.unsqueeze(1).to_broadcast([D, 2, D])).then_inc(ld_attn, 16)
            sp.wait_ge(s["tok_mm"], 1)
            load_x(2, 0)
            sp.wait_ge(s["tok_mm"], 2)
            load_x(3, 1)
            sp.wait_ge(s["weff_mm"], 1)
            sp.dma_start(wr_raw[:], wr.rearrange("l e h d -> h (l e) d")).then_inc(ld_ffn, 16)
            sp.dma_start(ws_raw[:], ws.rearrange("l s h d -> h (l s) d")).then_inc(ld_ffn, 16)
            for i in range(2):
                sp.dma_start(wi_raw[:, i], wi).then_inc(ld_ffn, 16)
            sp.dma_start(b_raw[0:LAYERS * EXPERTS], br.rearrange("l e h -> (l e) h")).then_inc(ld_ffn, 16)
            sp.dma_start(b_raw[LAYERS * EXPERTS:LAYERS * (EXPERTS + 1)],
                         bs.rearrange("l s h -> (l s) h")).then_inc(ld_ffn, 16)
            sp.dma_start(bi_c[:], bi.unsqueeze(1)).then_inc(ld_ffn, 16)
            sp.dma_start(wo_raw[:], wo).then_inc(ld_ffn, 16)
            sp.dma_start(bo_b[:], bo.unsqueeze(0).to_broadcast([P, D])).then_inc(ld_ffn, 16)
            sp.dma_start(route_i[:], route.unsqueeze(0)).then_inc(ld_ffn, 16)
            sp.wait_ge(s["tok_mm"], B)
            for dst, src in ((hilb, c_hilb), (fwd, c_fwd), (inv, c_inv), (phase, c_phase)):
                sp.dma_start(dst[:], src).then_inc(ld_conv, 16)
            sp.dma_start(dvec_b[:], dvec.unsqueeze(0).to_broadcast([P, D])).then_inc(ld_conv, 16)
            for i in range(2):
                sp.dma_start(rw_raw[:, i], router_w).then_inc(ld_moe, 16)
                sp.dma_start(w1_f[i * D:(i + 1) * D], w1.rearrange("e d f -> d e f")).then_inc(ld_moe, 16)
            sp.dma_start(b1_raw[:], b1.rearrange("(q e) f -> q (e f)", e=2)).then_inc(ld_moe, 16)
            sp.dma_start(w2_s[:], w2.rearrange("(q e) f o -> (e f) q o", e=2)).then_inc(ld_moe, 16)
            for i in range(3):
                sp.dma_start(b2_f[i * MOE:(i + 1) * MOE], b2).then_inc(ld_moe, 16)
            sp.dma_start(first_w[:], c_first).then_inc(ld_moe, 16)
            sp.dma_start(sel_f[:], c_sel).then_inc(ld_moe, 16)
            sp.sem_inc(s["res_stored"], 16)
            for b in range(B):
                sp.wait_ge(s["res_ready"], b + 3)
                dst = out[b].rearrange("(v t p) d -> p t v d", v=NV, t=NT)
                res = result[b % 2].rearrange("p (t v) d -> p t v d", v=NV)
                for v in range(NV):
                    sp.dma_start(dst[:, :, v], res[:, :, v]).then_inc(s["res_stored"], 16)
            sp.wait_ge(s["res_stored"], 16 * NV * B + 16)

        @block.tensor
        def _(pe):
            def transposes(dst, src):
                for t in range(NT):
                    last = pe.transpose(dst[:, t * P:(t + 1) * P], src[:, t * P:(t + 1) * P], ident[:])
                return last

            def stack_tokens(n, par):
                pe.wait_ge(s["parts_ready"], n + 1)
                if not isinstance(n, int) or n > 0:
                    pe.wait_ge(s["fm_a_ready"], n)
                    pe.wait_ge(s["fm_b_ready"], n)
                for m in range(SLOTS):
                    t, v = m // NV, m % NV
                    for i in range(2):
                        last = pe.transpose(turn_b[i][:, (v * NT + t) * P:(v * NT + t + 1) * P],
                                            parts[par][:, m, i].rearrange("p k d -> p (k d)"), ident_b[:])
                last.then_inc(s["ln_turned"], 1)

            def stacks_ready(n):
                pe.wait_ge(s["fm_a_ready"], n + 1)
                pe.wait_ge(s["fm_b_ready"], n + 1)

            def in_parts(dst, weight, tokens, swap=False):
                for i in range(3):
                    w, x = weight(i), tokens(i)
                    last = pe.matmul(dst, x if swap else w, w if swap else x, start=(i == 0), stop=(i == 2))
                return last

            def spectrum(out_of, src, n, copied=None):
                for half, i in ((0, 0), (1, 1)):
                    for part in range(2):
                        pe.matmul(out_of(0, part)[half * 64:(half + 1) * 64], fwd[:, part, half * 64:(half + 1) * 64],
                                  src[:, i, 0:n], start=True, stop=True)
                for r in range(1, SETS):
                    for part in range(2):
                        for k in range(2):
                            last = pe.matmul(out_of(r, part), fwd[:, 4 * r - 2 + 2 * part + k],
                                             src[:, 2 * r + k, 0:n], start=(k == 0), stop=(k == 1))
                return last

            pe.wait_ge(ld_tok, 16 * 3)
            for o in range(D):
                last = pe.matmul(wide[0][0:C, o * PATCH:(o + 1) * PATCH], tokw[:, o, :], dft[:],
                                 start=True, stop=True)
            last.then_inc(s["weff_mm"], 1)

            pe.wait_ge(ld_ssm, 16 * 8)
            for i in range(4):
                last = pe.transpose(wide[1][:, i * D:(i + 1) * D], par_raw[:, i].rearrange("d r n -> d (r n)"),
                                    ident[0:D, 0:D])
            last.then_inc(s["par_turned"], 1)
            pe.wait_ge(s["weff_ready"], 2)

            with pe.Fori(0, B // 2) as pair:
                for par in range(2):
                    b = pair * 2 + par
                    pe.wait_ge(x_in[par], pair * 64 + 64)
                    pe.wait_ge(s["tok_copied"], b + 1)
                    for k in range(2 * Q4):
                        q, lohi = k // 2, k % 2
                        for v in range(NV):
                            last = pe.matmul(acc[par][v * D:(v + 1) * D], weff[:, q, lohi, :],
                                             xs[par][:, lohi:lohi + NPATCH, q, v * 32:(v + 1) * 32],
                                             start=(k == 0), stop=(k == 2 * Q4 - 1))
                    last.then_inc(s["tok_mm"], 1)
                for par in range(2):
                    b = pair * 2 + par
                    pe.wait_ge(s["tok_copied"], b + 3)
                    pe.wait_ge(s["h_ready"], b + 1)
                    transposes(turn[par], tok_fm[par]).then_inc(s["tok_turned"], 1)

            pe.wait_ge(ld_ffn, 16 * 10)
            pe.wait_ge(s["h_ready"], B + 2)
            for i in range(LAYERS):
                last = pe.transpose(turn[0][:, i * HID:(i + 1) * HID], ws_raw[:, i], ident[:])
            pe.transpose(turn[0][:, 256:256 + HID], wi_raw[:].rearrange("h c d -> h (c d)"), ident[:])
            pe.transpose(turn[0][:, 384:384 + D], wo_raw[:], ident[0:D, 0:D])
            nb = LAYERS * (EXPERTS + 1)
            pe.transpose(turn[1][:, 0:nb], b_raw[0:nb], ident[0:nb, 0:nb]).then_inc(s["wgt_turned"], 1)
            for g in range(LAYERS * EXPERTS // 8):
                if g == 1:
                    pe.wait_ge(s["small_turned"], 1)
                if g >= 2:
                    pe.wait_ge(s["wgt_ready"], g)
                for i in range(8):
                    last = pe.transpose(wide[g % 2][:, i * HID:(i + 1) * HID], wr_raw[:, g * 8 + i], ident[:])
                last.then_inc(s["wgt_turned"], 1)

            pe.wait_ge(s["beta_ready"], 1)
            pe.wait_ge(s["alpha_ready"], 1)
            pe.wait_ge(s["wgt_ready"], LAYERS * EXPERTS // 8 + 1)
            for dd in range(NS):
                o0 = (dd % 8) * 2 * NTAB
                last = pe.matmul(wide_t[:, dd // 16, (dd // 8 % 2) * 512 + o0:(dd // 8 % 2) * 512 + o0 + 2 * NTAB],
                                 beta[:, dd, :], alpha[:, dd].rearrange("p x j -> p (x j)"), start=True, stop=True)
            last.then_inc(s["s_mm"], 1)

            pe.wait_ge(s["s_ready"], 2)
            pe.wait_ge(ld_conv, 16 * 5)
            pe.wait_ge(s["tok_copied"], B + 2)
            for j in range(2 * L // P):
                for th in range(2):
                    x0 = 2 * L - P - j * P + th * 512
                    last = pe.matmul(acc[0][th * D:(th + 1) * D], s_im[:, j, :], hilb[:, x0:x0 + 512],
                                     start=(j == 0), stop=(j == 2 * L // P - 1))
            last.then_inc(s["hil_mm"], 1)
            pe.wait_ge(s["hil_copied"], 1)
            pe.wait_ge(s["wgt_ready"], 1)
            transposes(turn[0], k_fm).then_inc(s["k_turned"], 1)
            pe.wait_ge(s["k_fly"], 2)
            spectrum(lambda r, part: wide[0][:, r * P + part * D:r * P + (part + 1) * D], xr, D).then_inc(s["k_dft"], 1)

            pe.wait_ge(ld_moe, 16 * 11)
            pe.transpose(acc[1][:, 0:MOE], rw_raw[:].rearrange("e c d -> e (c d)"), ident[0:MOE, 0:MOE])
            pe.transpose(acc[1][:, 16:16 + PAIRS], b1_raw[:], ident[0:PAIRS, 0:PAIRS]).then_inc(s["wgt_turned"], 1)

            pe.wait_ge(s["wgt_ready"], LAYERS * EXPERTS // 8 + 2)
            pe.wait_ge(s["k_spec_ready"], 1)
            pe.wait_ge(s["k_ready"], 1)

            def query(b):
                par = b % 2
                stacks_ready(b)
                for c in range(2):
                    last = in_parts(turn[c], lambda i: wq_s[:, i], lambda i: fm[par][:, i // 2, c * 512:(c + 1) * 512])
                last.then_inc(s["q_mm"], 1)

            def scores(b, m):
                par, k0 = b % 2, (m % NV * NT + m // NV) * P
                pe.wait_ge(s["att_ready"], b * 8 + m + 1)
                for c in range(2):
                    last = in_parts(wide[m % 2][:, c * 512:(c + 1) * 512], lambda i: fm[par][:, i // 2, k0:k0 + P],
                                    lambda i: q_s[par][:, i, c * 512:(c + 1) * 512])
                last.then_inc(s["score_mm"], 1)

            def attention_back(b):
                pe.wait_ge(s["pv_copied"], b + 3)
                transposes(acc[b % 2], pv_fm[b % 2]).then_inc(s["pv_turned"], 1)

            pe.wait_ge(s["weights_split"], 1)
            stack_tokens(0, 0)
            query(0)
            for b in range(B):
                pe.wait_ge(s["q_ready"], b + 1)
                scores(b, 0)
                scores(b, 1)
                if b > 0:
                    attention_back(b - 1)
                if b >= 2:
                    pe.wait_ge(s["h_ready"], B + b + 1)
                for m in range(SLOTS):
                    pe.wait_ge(s["att_ready"], b * 8 + m + 3)
                    if m + 2 < SLOTS:
                        scores(b, m + 2)
                    for c in range(2):
                        last = pe.matmul(acc[b % 2][c * D:(c + 1) * D], ln[b][:, m, :],
                                         att[m % 4][:, c * 512:(c + 1) * 512],
                                         start=(m == 0), stop=(m == SLOTS - 1))
                    last.then_inc(s["pv_step"], 1)
                    if b + 1 < B and m == 2:
                        pe.wait_ge(s["q_ready"], b + 1)
                        stack_tokens(b + 1, (b + 1) % 2)
                    if b + 1 < B and m == 4:
                        query(b + 1)
            attention_back(B - 1)

            with pe.Fori(0, B // 2) as pair:
                for par in range(2):
                    b = pair * 2 + par
                    stack_tokens(b + B, par)
                    stacks_ready(b + B)
                    pe.wait_ge(s["bias_added"], pair * 4 + par + 1)
                    if par == 0:
                        pe.wait_ge(s["att_ready"], 8 * B + 2)
                    for v in range(NV):
                        last = in_parts(wide[par][:, v * 512:(v + 1) * 512], lambda i: wi_s[:, i],
                                        lambda i: fm[par][:, i // 2, v * 512:(v + 1) * 512])
                    last.then_inc(s["hid_mm"], 1)
                for layer in range(LAYERS):
                    for par in range(2):
                        pe.wait_ge(s["hid_relu"], pair * 6 + 2 * layer + par + 1)
                        pe.wait_ge(s["staged_ready"], pair * 4 + 2 * layer + par + 1)
                        pe.wait_ge(s["staged_more"], pair * 4 + 2 * layer + par + 1)
                        for g in range(GPB):
                            last = pe.matmul(wide[par][:, g * GTOK:(g + 1) * GTOK], staged[par][:, g, 0:HID],
                                             hid[par][:, g * GTOK:(g + 1) * GTOK], start=True, stop=True)
                        last.then_inc(s["hid_mm"], 1)
                for par in range(2):
                    b = pair * 2 + par
                    pe.wait_ge(s["hid_relu"], pair * 6 + 5 + par)
                    pe.wait_ge(s["h_ready"], b + 2 * B + 1)
                    for m in range(SLOTS):
                        t, v = m // NV, m % NV
                        last = pe.matmul(acc[par][:, m * D:(m + 1) * D], hid[par][:, v * 512 + t * P:v * 512 + (t + 1) * P],
                                         wo_t[:], start=True, stop=True)
                    last.then_inc(s["ffn_mm"], 1)

            pe.wait_ge(s["u_fly"], 2)
            pe.wait_ge(s["h_ready"], 3 * B + 2)
            banks = [wide_t[:, r // 2, (r % 2) * 512:(r % 2) * 512 + 512] for r in range(4)] + turn
            n = B * D
            spectrum(lambda r, part: banks[r][:, part * n:(part + 1) * n], xr, n).then_inc(s["u_dft"], 1)
            pe.wait_ge(s["y_ready"], 1)
            for half in range(2):
                rows = slice(half * 64, half * 64 + 64)
                for part in range(2):
                    last = pe.matmul((banks[0], acc[0])[half][:, 0:n], inv[rows, part], y_spec[rows, 0, part],
                                     start=(part == 0), stop=(part == 1))
            last.then_inc(s["z_mm"], 1)
            for r in range(1, SETS):
                pe.wait_ge(s["y_ready"], r + 1)
                for part in range(2):
                    for k in range(2):
                        last = pe.matmul(banks[r][:, part * n:(part + 1) * n], inv[:, 4 * r - 2 + 2 * part + k],
                                         y_spec[:, r, k], start=(k == 0), stop=(k == 1))
                last.then_inc(s["z_mm"], 1)

            def down(b, par, qd):
                pe.wait_ge(s["gated_ready"], b * PAIRS + qd + 3)
                for v in range(NV):
                    last = pe.matmul(acc[par][v * D:(v + 1) * D], w2_s[:, qd, :], gated[qd % 2][:, v * 512:(v + 1) * 512],
                                     start=(qd == 0), stop=False)
                if qd == PAIRS - 1:
                    for i in range(3):
                        for v in range(NV):
                            last = pe.matmul(acc[par][v * D:(v + 1) * D], b2_s[:, i, :], gate_t[par][:, v * 512:(v + 1) * 512],
                                             start=False, stop=(i == 2))
                last.then_inc(s["down_mm"], 1)

            pe.wait_ge(s["z_copied"], SETS)
            pe.wait_ge(s["moe_bias_ready"], 1)
            pe.wait_ge(s["weights_split"], 4)
            with pe.Fori(0, B // 2) as pair:
                for par in range(2):
                    b = pair * 2 + par
                    if par == 0:
                        pe.wait_ge(s["gate_ready"], b + 1)
                        pe.wait_ge(s["res_ready"], b + 2)
                    stack_tokens(b + 2 * B, par)
                    stacks_ready(b + 2 * B)
                    for m in range(SLOTS):
                        t, v = m // NV, m % NV
                        c0, k0 = (par * NT + t) * MOE, (v * NT + t) * P
                        last = in_parts(acc[v][:, c0:c0 + MOE], lambda i: rw_s[:, i], lambda i: fm[par][:, i // 2, k0:k0 + P],
                                        swap=True)
                last.then_inc(s["route_mm"], 1)
                pe.wait_ge(s["split_ready"], pair + 1)
                for par in range(2):
                    b = pair * 2 + par
                    narrow = turn_b[par]
                    if par == 0:
                        pe.wait_ge(s["fm_a_ready"], b + 2 * B + 2)
                        pe.wait_ge(s["fm_b_ready"], b + 2 * B + 2)
                    for m in range(SLOTS):
                        t, v = m // NV, m % NV
                        last = pe.transpose(narrow[0:3 * MOE, (v * NT + t) * P:(v * NT + t + 1) * P],
                                            split[:, (v * 2 + par) * NT + t, :], ident_b[:])
                    last.then_inc(s["gate_turned"], 1)
                for par in range(2):
                    b = pair * 2 + par
                    pe.wait_ge(s["gate_ready"], b + 2)
                    for qd in range(PAIRS):
                        pe.wait_ge(s["gelu_ready"], b * PAIRS + qd + 1)
                        for v in range(NV):
                            last = in_parts(wide[0][:, v * 512:(v + 1) * 512], lambda i: w1_s[:, i, qd * P:(qd + 1) * P],
                                            lambda i: fm[par][:, i // 2, v * 512:(v + 1) * 512])
                        last.then_inc(s["up_mm"], 1)
                        pe.wait_ge(s["gated_ready"], b * PAIRS + qd + 2)
                        for v in range(NV):
                            last = pe.matmul(wide[1][:, v * 512:(v + 1) * 512], sel[:, qd, :],
                                             gate_t[par][:, v * 512:(v + 1) * 512], start=True, stop=True)
                        last.then_inc(s["gate_mm"], 1)
                        if qd == 0:
                            pe.wait_ge(s["moe_copied"], b + 1)
                        else:
                            down(b, par, qd - 1)
                    down(b, par, PAIRS - 1)
                for par in range(2):
                    b = pair * 2 + par
                    pe.wait_ge(s["moe_copied"], b + 3)
                    transposes(acc[par], moe_fm[par]).then_inc(s["moe_turned"], 1)

        @block.scalar
        def _(act):
            step = Steps(act, ae)
            act.sem_inc(s["tok_copied"], 2)
            act.sem_inc(s["att_ready"], 2)
            act.sem_inc(s["gelu_ready"], 1)

            act.wait_ge(s["weff_mm"], 1)
            for hh in range(2):
                src = wide[0][0:C].rearrange("c (o k h q) -> c h q k o", k=2, h=2, q=Q4)
                act.copy(weff[hh * C:(hh + 1) * C], src[:, hh]).then_inc(s["weff_ready"], 1)
            act.wait_ge(s["small_turned"], 1)
            act.activation(small[5][:], par_t[:, 0], ACT.Exp).then_inc(s["exp_out"], 1)

            with act.Fori(0, B // 2) as pair:
                for par in range(2):
                    b = pair * 2 + par
                    act.wait_ge(s["tok_mm"], b + 1)
                    act.copy(tok_fm[par][:].rearrange("m (v n) -> m n v", n=NPATCH),
                             acc[par].rearrange("m (n v) -> m n v", n=NPATCH)).then_inc(s["tok_copied"], 1)

            def top_parts(n, par, src, ready):
                act.wait_ge(s["ln_ready"], ready)
                if not isinstance(n, int) or n >= 2:
                    act.wait_ge(s["ln_turned"], n - 1)
                act.copy(parts[par][:, :, :, 0], src.unsqueeze(2).to_broadcast([P, SLOTS, 2, D])
                         ).then_inc(s["top_ready"], 1)

            def copy_b(n, par):
                act.wait_ge(s["ln_turned"], n + 1)
                act.copy(fm[par][:, 1], turn_b[1]).then_inc(s["fm_b_ready"], 1)

            def query_top(b):
                act.wait_ge(s["q_mm"], b + 1)
                act.copy(q_s[b % 2][:, 0], turn_all).then_inc(s["q_top"], 1)

            act.wait_ge(s["exp_in"], 1)
            act.activation(row_e[:], row_e[:], ACT.Exp).then_inc(s["exp_out"], 1)
            act.wait_ge(s["tab_mul"], 2)
            act.activation(col_e[:], col_e[:], ACT.Exp).then_inc(s["exp_out"], 1)
            act.wait_ge(s["sin_in"], 1)
            act.activation(row_z[:], row_z[:], ACT.Sin, scale=-TURN).then_inc(s["sin_out"], 1)
            act.wait_ge(s["sin_in"], 2)
            act.activation(col_tab[:], col_z[:], ACT.Sin, scale=-TURN).then_inc(s["sin_out"], 1)

            act.wait_ge(s["s_mm"], 1)
            n_im = 2 * L // P
            src = wide_t[:].rearrange("p x (y k) -> p (x y) k", k=512)[:, :, 0:16 * NTAB].rearrange(
                "p z (d e j) -> p e z d j", e=2, j=NTAB)
            for dst, j0, j1 in ((s_im, 0, n_im), (s_re, n_im, NTAB)):
                for dh in range(2):
                    to = dst.rearrange("p j (e z d) -> p e z d j", e=2, z=4)[:, dh]
                    last = act.copy(to, src[:, dh, :, :, j0:j1])
                last.then_inc(s["s_ready"], 1)
            act.wait_ge(s["hil_mm"], 1)
            act.copy(k_fm[:], acc[0]).then_inc(s["hil_copied"], 1)
            act.wait_ge(s["k_dft"], 1)
            act.copy(k_spec[:].rearrange("p r c d -> p (r c d)"), wide[0][:, 0:SETS * 2 * D]).then_inc(s["k_spec_ready"], 1)

            act.wait_ge(s["k_ready"], 1)
            top_parts(0, 0, ln[0], 2)
            copy_b(0, 0)
            query_top(0)
            for b in range(B):
                for m in range(SLOTS):
                    act.wait_ge(s["score_mm"], b * 8 + m + 1)
                    act.wait_ge(s["pv_step"], b * 8 + m + 1)
                    act.activation(att[m % 4][:], wide[m % 2], ACT.Sigmoid).then_inc(s["att_ready"], 1)
                    if b + 1 < B:
                        if m == 0:
                            top_parts(b + 1, (b + 1) % 2, ln[b + 1], b + 3)
                        if m == 3:
                            copy_b(b + 1, (b + 1) % 2)
                        if m == 5:
                            query_top(b + 1)

            act.wait_ge(ld_ffn, 16 * 10)
            with act.Fori(0, B // 2) as pair:
                for par in range(2):
                    top_parts(pair * 2 + par + B, par, ln[par], pair * 2 + par + B + 2)
                for par in range(2):
                    copy_b(pair * 2 + par + B, par)
                for par in range(2):
                    act.wait_ge(s["hid_mm"], pair * 6 + par + 1)
                    act.activation(hid[par][:], wide[par], ACT.Relu, bias=bi_c[:, 0:1]).then_inc(s["hid_relu"], 1)
                for layer in range(LAYERS):
                    for par in range(2):
                        act.wait_ge(s["bias_added"], pair * 4 + 2 * layer + par + 3)
                        act.activation(hid[par][:], hid_in[par][:], ACT.Relu).then_inc(s["hid_relu"], 1)

            act.wait_ge(s["z_mm"], 1)
            act.copy(z[:, 0, 0], wide_t[:, 0, 0:B * D])
            act.copy(z[:, 0, 1], acc[0][:, 0:B * D]).then_inc(s["z_copied"], 1)
            for r in range(1, SETS):
                act.wait_ge(s["z_mm"], r + 1)
                src = wide_t[:, r // 2, (r % 2) * 512:(r % 2) * 512 + 512] if r < 4 else turn[r - 4]
                act.copy(z[:, r].rearrange("p c n -> p (c n)"), src).then_inc(s["z_copied"], 1)

            with act.Fori(0, B // 2) as pair:
                for par in range(2):
                    top_parts(pair * 2 + par + 2 * B, par, ln[par], pair * 2 + par + 3 * B + 2)
                for par in range(2):
                    copy_b(pair * 2 + par + 2 * B, par)
                act.wait_ge(s["sm_in"], pair + 1)
                act.activation(sm_p[:], sm_d[:], ACT.Exp).then_inc(s["sm_exp"], 1)
                for par in range(2):
                    b = pair * 2 + par
                    for qd in range(PAIRS):
                        act.wait_ge(s["up_mm"], b * PAIRS + qd + 1)
                        act.wait_ge(s["gated_ready"], b * PAIRS + qd + 1)
                        act.activation(gelu[qd % 2][:], wide[0], ACT.Gelu, bias=b1_t[:, qd:qd + 1]).then_inc(s["gelu_ready"], 1)

        @block.vector
        def _(dve):
            step = Steps(dve, ve)
            dve.sem_inc(s["h_ready"], 2)
            dve.sem_inc(s["gate_ready"], 1)
            dve.sem_inc(s["pv_copied"], 2)
            dve.sem_inc(s["bias_added"], 2)
            dve.sem_inc(s["gated_ready"], 2)
            dve.sem_inc(s["stats_ready"], 1)
            dve.sem_inc(s["moe_copied"], 2)
            dve.sem_inc(s["res_ready"], 2)

            def stats(b, hb, stage):
                dve.wait_ge(s["stats_ready"], b + stage * B + 1)
                stand_apart(dve)
                for m in range(SLOTS):
                    last = dve.bn_stats(stat[:, m, :], hb[:, m, :])
                step.seq(last)
                dve.tensor_tensor(st[0][:], stat[:, :, 1], stat[:, :, 4], ALU.add)
                dve.tensor_tensor(st[1][:], stat[:, :, 1], stat[:, :, 4], ALU.subtract)
                step.seq(dve.tensor_tensor(st[2][:], stat[:, :, 2], stat[:, :, 5], ALU.add))
                dve.tensor_scalar(small_of(mean, b), st[0][:], 0.5, None, ALU.mult)
                step.seq(dve.tensor_tensor(st[3][:], st[1][:], st[1][:], ALU.mult))
                step.seq(dve.scalar_tensor_tensor(st[4][:], st[3][:], D / 4.0, st[2][:], ALU.mult, ALU.add))
                dve.tensor_scalar(small_of(var, b), st[4][:], 1.0 / D, EPS, ALU.mult, ALU.add).then_inc(s["stats_ready"], 1)

            STATS, PARTS = 4, 2

            def odd_fly(src, dst, n):
                f = [fly[:, i, 0:n] for i in range(8)]
                o = [dst[:, i, 0:n] for i in range(NX)]
                tt, sst = dve.tensor_tensor, dve.scalar_tensor_tensor
                tt(f[0], src(0), src(6), ALU.subtract)
                tt(f[1], src(1), src(7), ALU.subtract)
                tt(f[4], src(2), src(4), ALU.subtract)
                step.seq(tt(f[5], src(2), src(4), ALU.add))
                tt(f[2], f[1], src(5), ALU.subtract)
                step.seq(tt(f[3], f[1], src(5), ALU.add))
                sst(f[6], f[4], 0.5, f[0], ALU.mult, ALU.add)
                tt(o[6], f[0], f[4], ALU.subtract)
                tt(o[7], f[3], src(3), ALU.subtract)
                step.seq(sst(f[7], f[3], 0.5, src(3), ALU.mult, ALU.add))
                sst(o[2], f[2], COS30, f[6], ALU.mult, ALU.add)
                sst(o[3], f[5], COS30, f[7], ALU.mult, ALU.add)
                sst(o[10], f[2], -COS30, f[6], ALU.mult, ALU.add)
                return sst(o[11], f[5], -COS30, f[7], ALU.mult, ALU.add)

            dve.wait_ge(s["par_turned"], 1)
            for dh in range(2):
                rows = slice(dh * 64, dh * 64 + 64)
                last = dve.tensor_copy(par_t[rows], wide[1][rows, 0:4 * D].rearrange(
                    "p (i x d) -> p i x d", i=4, x=2)[:, :, dh])
            last.then_inc(s["small_turned"], 1)
            dve.wait_ge(s["small_turned"], 1)
            step.seq(dve.tensor_scalar(small[0][:], par_t[:, 1], DT / (2 * math.pi), None, ALU.mult))
            step.seq(dve.tensor_scalar(small[1][:], small[0][:], ROUND, -ROUND, ALU.add, ALU.add))
            step.seq(dve.tensor_tensor(turns[:], small[0][:], small[1][:], ALU.subtract))
            dve.wait_ge(s["exp_out"], 1)
            dve.tensor_scalar(lam[:], small[5][:], -DT, None, ALU.mult).then_inc(s["tab_mul"], 1)
            step.seq(dve.tensor_tensor(row_y[:], ramp[:].unsqueeze(1).to_broadcast([P, NS, P]),
                                       over_last(turns[:], P), ALU.mult))
            step.seq(dve.tensor_scalar(row_y[:], row_y[:], quarter[:, 0:1], None, ALU.add))
            step.seq(dve.tensor_scalar(row_z[:], row_y[:], ROUND, -ROUND, ALU.add, ALU.add))
            dve.tensor_tensor(row_z[:], row_z[:], row_y[:], ALU.subtract).then_inc(s["sin_in"], 1)

            with dve.Fori(0, B // 2) as pair:
                step.trip(pair, 2 * STATS)
                for par in range(2):
                    b = pair * 2 + par
                    dve.wait_ge(s["tok_turned"], b + 1)
                    hb = seq_of(h, b)
                    dve.tensor_copy(hb, turn[par].rearrange("p (s d) -> p s d", d=D)).then_inc(s["h_ready"], 1)
                    dve.wait_ge(s["h_ready"], b + 3)
                    stats(b, hb, 0)
            step.leave(B // 2)

            def by_col(i):
                return cols[:].unsqueeze(1).to_broadcast([P, NS, NCOL])
            dve.tensor_tensor(col_y[:], by_col(0), over_last(turns[:], NCOL), ALU.mult)
            step.seq(dve.tensor_tensor(col_e[:], by_col(0), over_last(lam[:], NCOL), ALU.mult))
            dve.sem_inc(s["tab_mul"], 1)
            for i in range(2):
                last = dve.tensor_tensor(col_tab[:, i], col_y[:], off[:, i].unsqueeze(1).to_broadcast([P, NS, NCOL]), ALU.add)
            step.seq(last)
            step.seq(dve.tensor_scalar(col_z[:], col_tab[:], ROUND, -ROUND, ALU.add, ALU.add))
            dve.tensor_tensor(col_z[:], col_z[:], col_tab[:], ALU.subtract).then_inc(s["sin_in"], 1)
            dve.wait_ge(s["sin_out"], 2)
            dve.wait_ge(s["exp_out"], 3)
            c_r, c_i = par_t[:, 2], par_t[:, 3]
            d_r, d_i, z_r, q_r, q_i, w = (t[:] for t in small)
            e_last = col_e[:, :, NTAB]
            tt = dve.tensor_tensor
            tt(d_r, col_tab[:, 0, :, NTAB], e_last, ALU.mult)
            step.seq(tt(d_i, col_tab[:, 1, :, NTAB], e_last, ALU.mult))
            step.seq(dve.tensor_scalar(z_r, d_r, -1.0, 1.0, ALU.mult, ALU.add))
            tt(q_r, z_r, z_r, ALU.mult)
            step.seq(tt(q_i, d_i, d_i, ALU.mult))
            step.seq(tt(w, q_r, q_i, ALU.add))
            tt(q_r, c_r, z_r, ALU.mult)
            tt(q_i, c_i, d_i, ALU.mult)
            step.seq(dve.reciprocal(d_r, w))
            step.seq(tt(q_r, q_r, q_i, ALU.subtract))
            tt(q_i, c_r, d_i, ALU.mult)
            step.seq(tt(z_r, c_i, z_r, ALU.mult))
            step.seq(tt(q_i, q_i, z_r, ALU.add))
            tt(q_r, q_r, d_r, ALU.mult)
            step.seq(tt(q_i, q_i, d_r, ALU.mult))
            tt(col_z[:, 0, :, 0:NTAB], col_tab[:, 0, :, 0:NTAB], over_last(q_r, NTAB), ALU.mult)
            step.seq(tt(col_z[:, 1, :, 0:NTAB], col_tab[:, 1, :, 0:NTAB], over_last(q_i, NTAB), ALU.mult))
            step.seq(tt(col_y[:, :, 0:NTAB], col_z[:, 0, :, 0:NTAB], col_z[:, 1, :, 0:NTAB], ALU.subtract))
            dve.wait_ge(s["ident_ready"], 1)
            for dh in range(2):
                rows = slice(dh * 64, dh * 64 + 64)
                last = tt(alpha[rows, :, dh], col_y[rows, :, 0:NTAB], col_e[rows, :, 0:NTAB], ALU.mult)
            last.then_inc(s["alpha_ready"], 1)

            dve.wait_ge(ld_ffn, 16 * 10)
            dve.wait_ge(s["wgt_turned"], 1)
            dve.tensor_tensor(base_t[:], turn[0][:, 0:2 * HID].rearrange("d (l h) -> d l h", l=LAYERS),
                              ident[:].unsqueeze(1).to_broadcast([P, LAYERS, P]), ALU.add)
            dve.tensor_copy(wi_f[:], turn[0][:, 256:256 + HID])
            dve.tensor_copy(wo_t[:], turn[0][:, 384:384 + D])
            dve.tensor_copy(b_t[:, 0:LAYERS * (EXPERTS + 1)], turn[1][:, 0:LAYERS * (EXPERTS + 1)]).then_inc(s["wgt_ready"], 1)
            dve.wait_ge(s["wgt_ready"], 1)
            for layer in range(LAYERS):
                shared = b_t[:, LAYERS * EXPERTS + layer:LAYERS * EXPERTS + layer + 1]
                dve.tensor_scalar(table[:, layer, 0:EXPERTS, HID], b_t[:, layer * EXPERTS:(layer + 1) * EXPERTS],
                                  shared, None, ALU.add)
                dve.tensor_copy(table[:, layer, EXPERTS, HID:HID + 1], shared)
                dve.tensor_copy(table[:, layer, EXPERTS, 0:HID], base_t[:, layer])
            step.seq(dve.tensor_copy(route_f[:], route_i[:]))
            dve.tensor_scalar(route_ok[:], route_f[:], 0.0, None, ALU.is_ge)
            dve.tensor_scalar(route_lo[:], route_f[:], float(EXPERTS - 1), None, ALU.is_le)
            step.seq(dve.tensor_scalar(route_x[:], route_f[:], float(-EXPERTS), None, ALU.add))
            step.seq(dve.tensor_tensor(route_ok[:], route_ok[:], route_lo[:], ALU.mult))
            step.seq(dve.tensor_tensor(route_x[:], route_x[:], route_ok[:], ALU.mult))
            dve.tensor_scalar(route_e[:], route_x[:], float(EXPERTS), None, ALU.add).then_inc(s["route_ready"], 1)
            for g in range(LAYERS * EXPERTS // 8):
                layer, e0 = g // 2, (g % 2) * 8
                dve.wait_ge(s["wgt_turned"], g + 2)
                dve.tensor_tensor(table[:, layer, e0:e0 + 8, 0:HID], wide[g % 2].rearrange("d (e h) -> d e h", e=8),
                                  base_t[:, layer].unsqueeze(1).to_broadcast([P, 8, HID]), ALU.add).then_inc(s["wgt_ready"], 1)

            dve.wait_ge(s["k_turned"], 1)
            dve.wait_ge(s["s_ready"], 2)
            dve.tensor_tensor(k_time[:].rearrange("p (v t) x d -> p t v (x d)", v=NV),
                              turn[0].rearrange("p (t v d) -> p t v d", t=NT, v=NV),
                              s_re[:].rearrange("p (v t) d -> p t v d", v=NV), ALU.add).then_inc(s["k_ready"], 1)
            dve.wait_ge(s["k_ready"], 1)
            odd_fly(lambda j: k_time[:, j].rearrange("p x d -> p (x d)"), xr, D).then_inc(s["k_fly"], 1)

            dve.wait_ge(s["wgt_turned"], LAYERS * EXPERTS // 8 + 2)
            dve.tensor_copy(rw_f[:], acc[1][:, 0:MOE])
            dve.tensor_copy(b1_t[:], acc[1][:, 16:16 + PAIRS]).then_inc(s["wgt_ready"], 1)

            def lower_parts(n, par, src, ready):
                dve.wait_ge(s["ln_ready"], ready)
                dve.wait_ge(s["top_ready"], n + 1)
                if not isinstance(n, int) or n > 0:
                    dve.wait_ge(s["parts_ready"], n)
                step.seq(dve.tensor_tensor(ln_rest[:], src, parts[par][:, :, 0, 0], ALU.subtract))
                step.seq(dve.tensor_copy(parts[par][:, :, 0, 1], ln_rest[:]))
                dve.tensor_tensor(parts[par][:, :, 1, 1], ln_rest[:], parts[par][:, :, 0, 1],
                                  ALU.subtract).then_inc(s["parts_ready"], 1)

            def copy_a(n, par):
                dve.wait_ge(s["ln_turned"], n + 1)
                dve.tensor_copy(fm[par][:, 0], turn_b[0]).then_inc(s["fm_a_ready"], 1)

            def query_parts(b):
                q = q_s[b % 2]
                low, high = slice(0, D), slice(D, P)
                dve.wait_ge(s["q_top"], b + 1)
                if b > 0:
                    dve.wait_ge(s["q_ready"], b)
                step.seq(dve.tensor_tensor(q_rest, turn_all, q[:, 0], ALU.subtract))
                dve.tensor_copy(q[high, 2], q[high, 0])
                step.seq(dve.tensor_copy(q[:, 1], q_rest))
                dve.tensor_tensor(q[low, 2], q_rest[low], q[low, 1], ALU.subtract).then_inc(s["q_ready"], 1)

            def weighted(b):
                dve.wait_ge(s["pv_step"], b * 8 + 12)
                dve.tensor_copy(pv_fm[b % 2][:], acc[b % 2]).then_inc(s["pv_copied"], 1)

            def residual(b):
                dve.wait_ge(s["pv_turned"], b + 1)
                hb = h[:, b]
                dve.tensor_tensor(hb, acc[b % 2].rearrange("p (s d) -> p s d", d=D), hb, ALU.add).then_inc(s["h_ready"], 1)
                dve.wait_ge(s["h_ready"], b + B + 3)
                stats(b, hb, 1)

            lower_parts(0, 0, ln[0], 2)
            copy_a(0, 0)
            query_parts(0)
            for b in range(B):
                if b + 1 < B:
                    lower_parts(b + 1, (b + 1) % 2, ln[b + 1], b + 3)
                    copy_a(b + 1, (b + 1) % 2)
                    query_parts(b + 1)
                weighted(b)
                residual(b)

            def stage_experts(pair, layer, par):
                stand_apart(dve)
                for g in range(POOL_GROUPS, GPB):
                    e = dve.value_load(route_e[0:1, ds((pair * 2 + par) * GPB + g, 1)], min_val=0, max_val=EXPERTS)
                    last = dve.tensor_copy(staged[par][:, g, :], table[:, layer, ds(e, 1), :].rearrange(
                        "d x h -> d (x h)"))
                last.then_inc(s["staged_more"], 1)

            dve.wait_ge(s["route_ready"], 1)
            with dve.Fori(0, B // 2) as pair:
                step.trip(pair, 2 * STATS + 2 * PARTS)
                for par in range(2):
                    n = pair * 2 + par + B
                    lower_parts(n, par, ln[par], n + 2)
                    copy_a(n, par)
                for par in range(2):
                    stage_experts(pair, 0, par)
                for layer in range(LAYERS):
                    for par in range(2):
                        dve.wait_ge(s["hid_mm"], pair * 6 + 2 * (layer + 1) + par + 1)
                        dve.wait_ge(s["staged_ready"], pair * 4 + 2 * layer + par + 1)
                        dve.tensor_tensor(hid_in[par][:].rearrange("h (g t) -> h g t", g=GPB),
                                          wide[par].rearrange("h (g t) -> h g t", g=GPB),
                                          over_last(staged[par][:, :, HID], GTOK), ALU.add).then_inc(s["bias_added"], 1)
                        if layer + 1 < LAYERS:
                            dve.wait_ge(s["bias_added"], pair * 4 + 2 * layer + par + 3)
                            stage_experts(pair, layer + 1, par)
                for par in range(2):
                    b = pair * 2 + par
                    dve.wait_ge(s["ffn_mm"], b + 1)
                    dve.wait_ge(s["bo_added"], b + 1)
                    hb = seq_of(h, b)
                    dve.tensor_tensor(hb, acc[par].rearrange("p (s d) -> p s d", d=D), hb, ALU.add).then_inc(s["h_ready"], 1)
                    dve.wait_ge(s["h_ready"], b + 2 * B + 3)
                    stats(b, hb, 2)
            step.leave(B // 2)

            n = B * D
            dve.wait_ge(s["ln_ready"], 3 * B + 1)
            odd_fly(lambda j: u[:, j].rearrange("p b d -> p (b d)"), xr, n).then_inc(s["u_fly"], 1)
            dve.wait_ge(s["u_dft"], 1)
            dve.wait_ge(s["k_mul_ready"], 1)
            for r in range(SETS):
                src = (wide_t[:, r // 2, (r % 2) * 512:(r % 2) * 512 + 512] if r < 4 else turn[r - 4])
                if r >= 2:
                    dve.wait_ge(s["y_ready"], r - 1)
                four = "p (c b d) -> p c b d"
                for part in range(2):
                    src_p = src.rearrange(four, c=2, b=B)[:, part]
                    dve.tensor_tensor(prod_a[r % 2][:, part].rearrange("p (b d) -> p b d", b=B), src_p,
                                      k_abd[:, r, part].unsqueeze(1).to_broadcast([P, B, D]), ALU.mult)
                last = dve.tensor_tensor(prod_b[r % 2][:].rearrange("p c (b d) -> p (c b) d", b=B),
                                         src.rearrange("p (c b d) -> p (c b) d", c=2, b=B),
                                         k_abd[:, r, 2].unsqueeze(1).to_broadcast([P, 2 * B, D]), ALU.mult)
                last.then_inc(s["u_prod"], 1)
            dve.wait_ge(s["z_copied"], SETS)
            zr = [z[:, r, 0] for r in range(SETS)]
            zi = [z[:, r, 1] for r in range(SETS)]
            f = [fly[:, i] for i in range(8)]
            tt, sst = dve.tensor_tensor, dve.scalar_tensor_tensor
            tt(f[0], zr[1], zr[5], ALU.add)
            tt(f[1], zr[1], zr[5], ALU.subtract)
            tt(f[2], zi[1], zi[5], ALU.add)
            step.seq(tt(f[3], zi[1], zi[5], ALU.subtract))
            sst(f[4], f[2], 0.5, zi[3], ALU.mult, ALU.add)
            step.seq(sst(f[5], f[0], 0.5, zr[3], ALU.mult, ALU.subtract))
            tt(odd[:, 0], f[0], zr[3], ALU.add)
            sst(odd[:, 1], f[1], COS30, f[4], ALU.mult, ALU.subtract)
            sst(odd[:, 2], f[3], -COS30, f[5], ALU.mult, ALU.add)
            tt(odd[:, 3], zi[3], f[2], ALU.subtract)
            sst(odd[:, 4], f[3], -COS30, f[5], ALU.mult, ALU.subtract)
            step.seq(sst(odd[:, 5], f[1], -COS30, f[4], ALU.mult, ALU.subtract))
            dve.wait_ge(s["even_ready"], 1)
            tt(fly[:, 8:14], even[:], odd[:], ALU.add)
            step.seq(tt(fly[:, 14:16], even[:, 0:2], odd[:, 0:2], ALU.subtract))
            with dve.Fori(0, B) as b:
                step.trip(b, STATS)
                y = fly[:, 8:16].rearrange("p (v t) (b d) -> p t v b d", v=NV, b=B)[:, :, :, ds(b, 1)].rearrange(
                    "p t v x d -> p t v (x d)")
                hb = seq_of(h, b)
                h4 = hb.rearrange("p (t v) d -> p t v d", v=NV)
                dve.wait_ge(s["bo_added"], 2 * B)
                dve.tensor_tensor(h4, h4, y, ALU.add).then_inc(s["h_ready"], 1)
                dve.wait_ge(s["h_ready"], b + 3 * B + 3)
                stats(b, hb, 3)
            step.leave(B)

            dve.wait_ge(ld_moe, 16 * 11)
            SOFTMAX = 17
            with dve.Fori(0, B // 2) as pair:
                step.trip(pair, SOFTMAX + 2 * PARTS)
                for par in range(2):
                    n = pair * 2 + par + 2 * B
                    lower_parts(n, par, ln[par], n + B + 2)
                    copy_a(n, par)
                dve.wait_ge(s["route_mm"], pair + 1)
                logits = acc_t[:, :, 0:SLOTS * MOE].rearrange("p v (s e) -> p v s e", e=MOE)
                m1, m2, k1, tot, rec = (t[:] for t in sm_r)
                by_half = "p (v s) e -> p v s e"
                step.seq(dve.tensor_reduce(m1.rearrange("p (v s) -> p v s", v=NV), logits, AX.X, ALU.max))
                dve.tensor_tensor(sm_d[:].rearrange(by_half, v=NV), logits,
                                  over_last(m1, MOE).rearrange(by_half, v=NV), ALU.subtract).then_inc(s["sm_in"], 1)
                dve.wait_ge(s["sm_exp"], pair + 1)
                step.seq(dve.tensor_reduce(tot, sm_p[:], AX.X, ALU.add))
                step.seq(dve.reciprocal(rec, tot))
                step.seq(dve.tensor_tensor(sm_p[:], sm_p[:], over_last(rec, MOE), ALU.mult))
                weight = first_w[:].unsqueeze(1).to_broadcast([P, 2 * SLOTS, MOE])

                def largest(src, top, one):
                    step.seq(dve.tensor_reduce(top, src, AX.X, ALU.max))
                    step.seq(dve.tensor_tensor(sm_key[:], src, over_last(top, MOE), ALU.is_equal))
                    step.seq(dve.tensor_tensor(sm_key[:], sm_key[:], weight, ALU.mult))
                    step.seq(dve.tensor_reduce(k1, sm_key[:], AX.X, ALU.max))
                    step.seq(dve.tensor_tensor(one, sm_key[:], over_last(k1, MOE), ALU.is_equal))

                largest(sm_p[:], m1, sm_one[0][:])
                step.seq(dve.scalar_tensor_tensor(sm_d[:], sm_one[0][:], -2.0, sm_p[:], ALU.mult, ALU.add))
                largest(sm_d[:], m2, sm_one[1][:])
                dve.tensor_tensor(sm_one[0][:], sm_one[0][:], sm_one[1][:], ALU.add)
                step.seq(dve.tensor_tensor(tot, m1, m2, ALU.add))
                step.seq(dve.tensor_scalar(tot, tot, 1e-12, None, ALU.max))
                dve.tensor_tensor(sm_c[:], sm_one[0][:], sm_p[:], ALU.mult)
                dve.reciprocal(rec, tot).then_inc(s["gate_step"], 1)
                dve.wait_ge(s["gate_step"], pair * 5 + 1)
                dve.tensor_tensor(sm_c[:], sm_c[:], over_last(rec, MOE), ALU.mult).then_inc(s["gate_step"], 1)
                dve.wait_ge(s["gate_step"], pair * 5 + 2)
                dve.tensor_copy(split[:, :, 0:MOE], sm_c[:]).then_inc(s["gate_step"], 1)
                dve.wait_ge(s["gate_step"], pair * 5 + 3)
                dve.tensor_tensor(sm_key[:], sm_c[:], split[:, :, 0:MOE], ALU.subtract).then_inc(s["gate_step"], 1)
                dve.wait_ge(s["gate_step"], pair * 5 + 4)
                dve.tensor_copy(split[:, :, MOE:2 * MOE], sm_key[:]).then_inc(s["gate_step"], 1)
                dve.wait_ge(s["gate_step"], pair * 5 + 5)
                dve.tensor_tensor(split[:, :, 2 * MOE:3 * MOE], sm_key[:], split[:, :, MOE:2 * MOE],
                                  ALU.subtract).then_inc(s["split_ready"], 1)
                for par in range(2):
                    b = pair * 2 + par
                    dve.wait_ge(s["gate_turned"], b + 1)
                    dve.tensor_copy(gate_t[par][:], turn_b[par][0:3 * MOE]).then_inc(s["gate_ready"], 1)
                for par in range(2):
                    b = pair * 2 + par
                    for qd in range(PAIRS):
                        dve.wait_ge(s["gelu_ready"], b * PAIRS + qd + 2)
                        dve.wait_ge(s["gate_mm"], b * PAIRS + qd + 1)
                        dve.wait_ge(s["down_mm"], b * PAIRS + qd + 1)
                        dve.tensor_tensor(gated[qd % 2][:], gelu[qd % 2][:], wide[1], ALU.mult).then_inc(s["gated_ready"], 1)
                    dve.wait_ge(s["down_mm"], b * PAIRS + PAIRS + 2)
                    dve.tensor_copy(moe_fm[par][:], acc[par]).then_inc(s["moe_copied"], 1)
                for par in range(2):
                    b = pair * 2 + par
                    dve.wait_ge(s["moe_turned"], b + 1)
                    dve.wait_ge(s["bo_added"], b + 2 * B + 1)
                    if par == 0:
                        dve.wait_ge(s["res_stored"], pair * (16 * NV * 2) + 16)
                    dve.tensor_tensor(result[par][:], acc[par].rearrange("p (s d) -> p s d", d=D), seq_of(h, b),
                                      ALU.add).then_inc(s["res_ready"], 1)
            step.leave(B // 2)

        @block.gpsimd
        def _(pool):
            step = Steps(pool, ge)
            pool.sem_inc(s["pv_step"], 4)
            pool.sem_inc(s["down_mm"], 2)
            pool.sem_inc(s["ln_ready"], 1)
            tt = pool.tensor_tensor
            pool.memset(minus_half[:], -0.5).then_inc(s["begun"], 1)
            pool.wait_ge(s["begun"], 1)

            def normalise(index, b, dst, waits):
                pool.wait_ge(s["stats_ready"], index + 2)
                stand_apart(pool)
                tt(small_of(rstd, b), small_of(var, b), minus_half[:], ALU.pow)
                pool.wait_ge(s["ln_ready"], index + 1)
                stand_apart(pool)
                step.seq(tt(centred[:], seq_of(h, b), over_last(small_of(mean, b), D), ALU.subtract))
                waits()
                stand_apart(pool)
                return tt(dst, centred[:], over_last(small_of(rstd, b), D), ALU.mult)

            def even_fly(src, dst, n):
                f = [fly[:, 8 + i, 0:n] for i in range(8)]
                o = [dst[:, i, 0:n] for i in range(NX)]
                tt(f[0], src(0), src(6), ALU.add)
                step.seq(tt(f[1], src(1), src(7), ALU.add))
                tt(f[2], f[0], src(3), ALU.add)
                tt(f[3], f[1], src(4), ALU.add)
                tt(f[4], src(2), src(5), ALU.add)
                tt(f[5], f[0], src(3), ALU.subtract)
                tt(f[6], f[1], src(4), ALU.subtract)
                step.seq(tt(f[7], src(2), src(5), ALU.subtract))
                tt(f[0], f[3], f[4], ALU.add)
                tt(o[9], f[3], f[4], ALU.subtract)
                tt(o[5], f[6], f[7], ALU.add)
                step.seq(tt(f[1], f[6], f[7], ALU.subtract))
                tt(o[0], f[2], f[0], ALU.add)
                tt(o[1], f[5], f[1], ALU.subtract)
                pool.tensor_scalar(f[3], f[0], -0.5, 0.0, ALU.mult, ALU.add)
                step.seq(pool.tensor_scalar(f[4], f[1], 0.5, 0.0, ALU.mult, ALU.add))
                tt(o[8], f[3], f[2], ALU.add)
                return tt(o[4], f[4], f[5], ALU.add)

            def split_weight(src, dst, count):
                low, high = slice(0, D), slice(D, P)
                step.seq(pool.tensor_copy(dst[:, 0], src))
                step.seq(pool.tensor_copy(dst[high, 2], dst[high, 0]))
                step.seq(tt(src, src, dst[:, 0], ALU.subtract))
                step.seq(pool.tensor_copy(dst[:, 1], src))
                tt(dst[low, 2], src[low], dst[low, 1], ALU.subtract).then_inc(s["weights_split"], 1)
                pool.wait_ge(s["weights_split"], count)

            pool.memset(alpha[:], 0.0).then_inc(s["ident_ready"], 1)
            pool.wait_ge(ld_tok, 16 * 3)
            pool.tensor_copy(ident_b[:], ident[:])
            pool.wait_ge(ld_attn, 16 * 2)
            split_weight(wq[:].rearrange("p c e -> p (c e)"), wq_s, 1)

            pool.wait_ge(s["tab_mul"], 1)
            pool.wait_ge(s["sin_in"], 1)
            tt(row_e[:], ramp[:].unsqueeze(1).to_broadcast([P, NS, P]), over_last(lam[:], P), ALU.mult).then_inc(s["exp_in"], 1)
            with pool.Fori(0, B) as b:
                step.trip(b, 1)
                normalise(b, b, seq_of(ln_t, b), lambda: None).then_inc(s["ln_ready"], 1)
            step.leave(B)

            pool.wait_ge(s["exp_out"], 2)
            pool.wait_ge(s["sin_out"], 1)
            tt(beta[:], row_z[:], row_e[:], ALU.mult).then_inc(s["beta_ready"], 1)

            pool.wait_ge(s["k_ready"], 1)
            even_fly(lambda j: k_time[:, j].rearrange("p x d -> p (x d)"), xr, D).then_inc(s["k_fly"], 1)
            pool.wait_ge(s["k_spec_ready"], 1)
            for i, dst in enumerate((0, 2, 1)):
                step.wait()
                tt(k_mul[0][:], k_spec[:, :, 0], over_last(phase[:, 2 * i], D), ALU.mult)
                step.seq(tt(k_mul[1][:], k_spec[:, :, 1], over_last(phase[:, 2 * i + 1], D), ALU.mult))
                step.done(tt(k_abd[:, :, dst], k_mul[0][:], k_mul[1][:], ALU.add))
            step.wait()
            pool.sem_inc(s["k_mul_ready"], 1)

            pool.wait_ge(s["wgt_ready"], LAYERS * EXPERTS // 8 + 2)
            split_weight(wi_f[:], wi_s, 2)
            split_weight(rw_f[:], rw_s, 3)
            split_weight(w1_f[:].rearrange("p e f -> p (e f)"), w1_s, 4)
            pool.tensor_copy(sel[:], sel_f[:])
            step.seq(pool.tensor_copy(b2_s[:, 0], b2_f[:]))
            step.seq(tt(b2_r[:, 0], b2_f[:], b2_s[:, 0], ALU.subtract))
            step.seq(pool.tensor_copy(b2_s[:, 1], b2_r[:, 0]))
            step.seq(tt(b2_r[:, 1], b2_r[:, 0], b2_s[:, 1], ALU.subtract))
            pool.tensor_copy(b2_s[:, 2], b2_r[:, 1]).then_inc(s["moe_bias_ready"], 1)

            pool.wait_ge(s["route_ready"], 1)
            pool.wait_ge(s["wgt_ready"], 1 + LAYERS * EXPERTS // 8)
            pool.wait_ge(s["pv_copied"], B + 2)
            with pool.Fori(0, B // 2) as pair:
                step.trip(pair, 2)
                for par in range(2):
                    b = pair * 2 + par
                    normalise(b + B, b, ln[par][:], lambda: pool.wait_ge(s["ln_turned"], b + 3)).then_inc(s["ln_ready"], 1)
                for layer in range(LAYERS):
                    for par in range(2):
                        b = pair * 2 + par
                        pool.wait_ge(s["bias_added"], pair * 4 + 2 * layer + par + 1)
                        stand_apart(pool)
                        for g in range(POOL_GROUPS):
                            e = pool.value_load(route_e[0:1, ds(b * GPB + g, 1)], min_val=0, max_val=EXPERTS)
                            last = pool.tensor_copy(staged[par][:, g, :], table[:, layer, ds(e, 1), :].rearrange(
                                "d x h -> d (x h)"))
                        last.then_inc(s["staged_ready"], 1)
                    if layer == 0:
                        stand_apart(pool)
                        for par in range(2):
                            hb = seq_of(h, pair * 2 + par)
                            tt(hb, hb, bo_b[:].unsqueeze(1).to_broadcast([P, SLOTS, D]), ALU.add).then_inc(s["bo_added"], 1)
            step.leave(B // 2)

            pool.wait_ge(ld_conv, 16 * 5)
            with pool.Fori(0, B) as b:
                step.trip(b, 1)
                pool.wait_ge(s["stats_ready"], b + 2 * B + 2)
                stand_apart(pool)
                tt(small_of(rstd, b), small_of(var, b), minus_half[:], ALU.pow)
                pool.wait_ge(s["ln_ready"], b + 2 * B + 1)
                step.done(tt(centred[:], seq_of(h, b), over_last(small_of(mean, b), D), ALU.subtract))
                hb = seq_of(h, b)
                tt(hb, hb, dvec_b[:].unsqueeze(1).to_broadcast([P, SLOTS, D]), ALU.add).then_inc(s["bo_added"], 1)
                ub = u[:, :, ds(b, 1)].rearrange("p (v t) x d -> p v t (x d)", v=NV)
                r4 = small_of(rstd, b).rearrange("p (t v) -> p v t", v=NV).unsqueeze(3).to_broadcast([P, NV, NT, D])
                step.wait()
                stand_apart(pool)
                tt(ub, centred[:].rearrange("p (t v) d -> p v t d", v=NV), r4, ALU.mult).then_inc(s["ln_ready"], 1)
            step.leave(B)
            pool.wait_ge(s["ln_ready"], 3 * B + 1)
            even_fly(lambda j: u[:, j].rearrange("p b d -> p (b d)"), xr, B * D).then_inc(s["u_fly"], 1)
            for r in range(SETS):
                pool.wait_ge(s["u_prod"], r + 1)
                a_, b_ = prod_a[r % 2], prod_b[r % 2]
                tt(y_spec[:, r, 0], a_[:, 0], b_[:, 1], ALU.subtract)
                tt(y_spec[:, r, 1], b_[:, 0], a_[:, 1], ALU.add).then_inc(s["y_ready"], 1)
            pool.wait_ge(s["z_copied"], SETS)
            z0, z6 = z[:, 0, 0], z[:, 0, 1]
            z2r, z2i, z4r, z4i = z[:, 2, 0], z[:, 2, 1], z[:, 4, 0], z[:, 4, 1]
            f = [fly[:, 8 + i] for i in range(8)]
            tt(f[0], z0, z4r, ALU.add)
            tt(f[3], z2r, z6, ALU.add)
            pool.tensor_scalar(f[1], z4r, -0.5, 0.0, ALU.mult, ALU.add)
            step.seq(pool.tensor_scalar(f[4], z2r, 0.5, 0.0, ALU.mult, ALU.add))
            tt(f[2], f[1], z0, ALU.add)
            step.seq(tt(f[5], f[4], z6, ALU.subtract))
            tt(f[1], f[2], z4i, ALU.subtract)
            tt(f[6], f[2], z4i, ALU.add)
            tt(f[4], f[5], z2i, ALU.subtract)
            step.seq(tt(f[7], f[5], z2i, ALU.add))
            tt(even[:, 0], f[0], f[3], ALU.add)
            tt(even[:, 3], f[0], f[3], ALU.subtract)
            tt(even[:, 1], f[1], f[4], ALU.add)
            tt(even[:, 4], f[1], f[4], ALU.subtract)
            tt(even[:, 2], f[6], f[7], ALU.subtract)
            tt(even[:, 5], f[6], f[7], ALU.add).then_inc(s["even_ready"], 1)

            with pool.Fori(0, B // 2) as pair:
                step.trip(pair, 2)
                for par in range(2):
                    b = pair * 2 + par
                    normalise(b + 3 * B, b, ln[par][:], lambda: pool.wait_ge(s["ln_turned"], b + 2 * B - 1)).then_inc(s["ln_ready"], 1)
                for par in range(2):
                    b = pair * 2 + par
                    pool.wait_ge(s["ln_ready"], b + 3 * B + 2)
                    stand_apart(pool)
                    hb = seq_of(h, b)
                    tt(hb, hb, ln[par][:], ALU.add).then_inc(s["bo_added"], 1)
            step.leave(B // 2)


_INS = {
    "x": "x", "L0_tok_W": "tok_w", "L0_attn_q_weight": "q_w", "L0_ffn_route_id": "route", "L0_ffn_Wi": "wi",
    "L0_ffn_bi": "bi", "L0_ffn_Wr": "wr", "L0_ffn_br": "br", "L0_ffn_Ws": "ws", "L0_ffn_bs": "bs",
    "L0_ffn_Wo": "wo", "L0_ffn_bo": "bo", "L1_attn_A_real": "a_re", "L1_attn_A_imag": "a_im",
    "L1_attn_C_real": "c_re", "L1_attn_C_imag": "c_im", "L1_attn_D": "dvec", "L1_ffn_router_w": "router_w",
    "L1_ffn_w1": "w1", "L1_ffn_b1": "b1", "L1_ffn_w2": "w2", "L1_ffn_b2": "b2",
}


def kernel(**inputs):
    from concourse import bacc
    from concourse.bass_utils import run_bass_kernel_spmd

    nc = bacc.Bacc("TRN2", target_bir_lowering=False, num_devices=1)
    arrays, args = {}, {}
    for name, short in _INS.items():
        arrays["in_" + short] = np.ascontiguousarray(inputs[name])
    for name, a in constants().items():
        arrays["in_" + name] = np.ascontiguousarray(a)
    for name, a in arrays.items():
        args[name[3:]] = nc.dram_tensor(name, a.shape, mybir.dt.from_np(a.dtype), kind="ExternalInput").ap()
    args["out"] = nc.dram_tensor("out_0", (B, L, D), F32, kind="ExternalOutput").ap()
    build_tower(nc, **args)
    r = run_bass_kernel_spmd(nc, [arrays], core_ids=[0])
    return r.results[0]["out_0"]
```

```python
from contextlib import ExitStack
import math

import numpy as np

import concourse.bass as bass
from concourse import mybir

ALU = mybir.AluOpType
ACT = mybir.ActivationFunctionType
AX = mybir.AxisListType
F32 = mybir.dt.float32
BF16 = mybir.dt.bfloat16
I32 = mybir.dt.int32
ds = bass.ds

B, C, T_IN, V = 4, 64, 128, 64
D = 64
PATCH, STRIDE = 16, 8
NPATCH = T_IN // STRIDE
NF = PATCH // 2 + 1
RF = 2 * NF
OSTACK = 4
Q4 = STRIDE // 2
L = V * NPATCH
P = 128
NT, NV = 4, 2
SLOTS = NT * NV
HID = 128
LAYERS, EXPERTS = 2, 16
GROUPS = 64
GPB = GROUPS // B
GTOK = B * L // GROUPS
NS = 32
DT = 0.1
NFFT = 1536
RADIX = NFFT // P
NX = RADIX
SETS = RADIX // 2
NBLK = 2 + 4 * (SETS - 1)
SHIFT = (L - 1) // 2
COS30 = math.sqrt(0.75)
MOE, TOPW = 8, 2
PAIRS = MOE // 2
PC = 2 * D
POOL_G, VEC_G = 2, 9
LAST_VEC = 6
EPS = 1e-5
ROUTE_BITS, PACK = 5, 4
ROUND = 1.5 * 2.0 ** 23
TURN = 6.2831850
NTAB = 2 * L // P + L // P
NCOL = NTAB + 1


def patch_dft():
    a = 2 * np.pi * np.arange(NF)[:, None] * np.arange(PATCH)[None, :] / PATCH
    return np.concatenate([np.cos(a), -np.sin(a)]) / math.sqrt(PATCH)


def forward_blocks():
    p = np.arange(P)[:, None]
    out = np.zeros((P, NBLK, P))
    g = np.arange(64)[None, :]
    for half, r in ((0, 0), (1, 6)):
        a = 2 * np.pi * (RADIX * g + r) * p / NFFT
        c, s = np.cos(a), -np.sin(a)
        if r == 0:
            s[:, 0] = np.cos(np.pi * p[:, 0])
        out[:, 0, half * 64:half * 64 + 64] = c
        out[:, 1, half * 64:half * 64 + 64] = s
    g = np.arange(P)[None, :]
    for r in range(1, SETS):
        a = 2 * np.pi * (RADIX * g + r) * p / NFFT
        fold = -1.0 if r % 2 else -COS30
        k = 4 * r - 2
        out[:, k + 0] = np.cos(a)
        out[:, k + 1] = fold * np.sin(a)
        out[:, k + 2] = -np.sin(a)
        out[:, k + 3] = fold * np.cos(a)
    return out


def inverse_blocks():
    p = np.arange(P)[None, :]
    out = np.zeros((P, NBLK, P))
    g = np.arange(64)[:, None]
    for half, r in ((0, 0), (1, 6)):
        a = 2 * np.pi * (RADIX * g + r) * p / NFFT
        c, s = 2 * np.cos(a) / NFFT, -2 * np.sin(a) / NFFT
        if r == 0:
            c[0] /= 2
            s[0] = np.cos(np.pi * p[0]) / NFFT
        out[half * 64:half * 64 + 64, 0] = c
        out[half * 64:half * 64 + 64, 1] = s
    g = np.arange(P)[:, None]
    for r in range(1, SETS):
        a = 2 * np.pi * (RADIX * g + r) * p / NFFT
        c, s = 2 * np.cos(a) / NFFT, 2 * np.sin(a) / NFFT
        fold = 1.0 if r % 2 else COS30
        k = 4 * r - 2
        out[:, k + 0], out[:, k + 1] = c, -s
        out[:, k + 2], out[:, k + 3] = fold * s, fold * c
    return out


def phase_tables():
    f = np.zeros((P, SETS))
    f[:64, 0] = RADIX * np.arange(64)
    f[64:, 0] = RADIX * np.arange(64) + 6
    for r in range(1, SETS):
        f[:, r] = RADIX * np.arange(P) + r
    a = 2 * np.pi * f * SHIFT / NFFT
    c, s = np.cos(a), np.sin(a)
    cb, sb, cd, sd = c.copy(), s.copy(), c.copy(), s.copy()
    cb[0, 0] = sb[0, 0] = 0.0
    cd[0, 0], sd[0, 0] = 0.0, 1.0
    return np.stack([c, -s, -sb, -cb, cd, -sd], 1)


def hilbert_band():
    m = (np.arange(3 * L)[None, :] - (2 * L - P)) - np.arange(P)[:, None]
    odd = m % 2 != 0
    h = np.zeros(m.shape)
    h[odd] = -1.0 / (L * np.tan(np.pi * m[odd] / (2 * L)))
    return h


def turn_offsets():
    im = (np.arange(P) // NS) % 2
    off = np.zeros((P, 2, NCOL))
    shift = np.zeros((P, NCOL))
    shift[:, :2 * L // P] = np.where(im[:, None] == 1, -0.25, 0.0)
    shift[:, 2 * L // P:NTAB] = np.where(im[:, None] == 1, 0.0, 0.25)
    off[:, 0] = shift + 0.25
    off[:, 1] = shift
    return off


def constants():
    f = np.float32
    im = ((np.arange(P) // NS) % 2).astype(f)
    cols = np.concatenate([P * np.arange(2 * L // P), P * np.arange(L // P), [2 * L]])
    sel = np.zeros((3 * MOE, PAIRS, P), f)
    for i in range(3):
        for e in range(MOE):
            sel[i * MOE + e, e // 2, (e % 2) * 64:(e % 2) * 64 + 64] = 1
    return {
        "c_ident": np.eye(P, dtype=f),
        "c_dft": np.kron(np.eye(OSTACK), patch_dft()).astype(f),
        "c_fwd": forward_blocks().astype(f),
        "c_inv": inverse_blocks().astype(f),
        "c_phase": phase_tables().astype(f),
        "c_hilb": hilbert_band().astype(f),
        "c_ramp": np.broadcast_to(np.arange(P, dtype=f), (P, P)).copy(),
        "c_cols": np.broadcast_to(cols.astype(f), (P, NCOL)).copy(),
        "c_off": turn_offsets().astype(f),
        "c_quarter": (0.25 * im)[:, None].astype(f),
        "c_first": np.broadcast_to(MOE - np.arange(MOE, dtype=f), (P, MOE)).copy(),
        "c_sel": sel,
        "c_third": np.kron(np.eye(3), np.ones((3 * MOE, 1))).astype(f),
    }


class Steps:

    def __init__(self, engine, sem):
        self.engine, self.sem, self.n = engine, sem, 0

    def done(self, instruction):
        instruction.then_inc(self.sem, 1)
        self.n += 1

    def wait(self):
        self.engine.wait_ge(self.sem, self.n)

    def seq(self, instruction):
        self.done(instruction)
        self.wait()


def over_last(ap, n):
    return ap.unsqueeze(2).to_broadcast([ap.shape[0], ap.shape[1], n])


def build_tower(nc, x, tok_w, q_w, route, wi, bi, wr, br, ws, bs, wo, bo, a_re, a_im, c_re, c_im, dvec,
                router_w, w1, b1, w2, b2, c_ident, c_dft, c_fwd, c_inv, c_phase, c_hilb, c_ramp, c_cols,
                c_off, c_quarter, c_first, c_sel, c_third, out):
    with ExitStack() as ctx:
        def sb(name, shape, dt=F32):
            return ctx.enter_context(nc.sbuf_tensor(name, shape, dt))

        def region(name, floats):
            return sb(name, [P, floats])

        def part(area, first, shape, dt=F32):
            floats = math.prod(shape[1:]) * mybir.dt.size(dt) // 4
            ap = area[0:shape[0], first:first + floats]
            if dt != F32:
                ap = ap.bitcast(dt)
            if len(shape) == 2:
                return ap
            names = ["x%d" % i for i in range(len(shape) - 1)]
            return ap.rearrange("p (%s) -> p %s" % (" ".join(names), " ".join(names)),
                                **dict(zip(names[1:], shape[2:])))

        def sem(name):
            return ctx.enter_context(nc.semaphore(name))

        ident = sb("ident", [P, P])
        ident_b = sb("ident_b", [P, P], BF16)
        dft = sb("dft", [OSTACK * RF, OSTACK * PATCH])
        weff = sb("weff", [P, Q4, 2, D])
        wq = sb("wq", [P, 2, D])
        wq_s = sb("wq_s", [P, 3, 2 * D], BF16)
        wi_f = sb("wi_f", [P, HID])
        wi_s = sb("wi_s", [P, 3, HID], BF16)
        rw_f = sb("rw_f", [P, MOE])
        rw_s = sb("rw_s", [P, 3, MOE], BF16)
        w1_s = sb("w1_s", [P, 3, MOE * D], BF16)
        alpha = sb("alpha", [P, NS, 2, NTAB])
        wi_raw = sb("wi_raw", [HID, 2, D])
        ws_raw = sb("ws_raw", [HID, LAYERS, HID])
        base_t = sb("base_t", [HID, LAYERS, HID])
        b_raw = sb("b_raw", [LAYERS * (EXPERTS + 2), HID])
        b_t = sb("b_t", [HID, LAYERS * (EXPERTS + 2)])
        bi_c = sb("bi_c", [HID, 1])
        wo_raw = sb("wo_raw", [D, HID])
        wo_t = sb("wo_t", [HID, D])
        bo_b = sb("bo_b", [P, D])
        route_i = sb("route_i", [1, GROUPS], I32)
        route_f = sb("route_f", [1, GROUPS])
        route_ok = sb("route_ok", [1, GROUPS])
        route_lo = sb("route_lo", [1, GROUPS])
        route_x = sb("route_x", [1, GROUPS])
        route_e = sb("route_e", [1, GROUPS // PACK], I32)
        phase = sb("phase", [P, 6, SETS])
        ramp = sb("ramp", [P, P])
        cols = sb("cols", [P, NCOL])
        off = sb("off", [P, 2, NCOL])
        quarter = sb("quarter", [P, 1])
        rw_raw = sb("rw_raw", [MOE, 2, D])
        b1_raw = sb("b1_raw", [PAIRS, P])
        b1_t = sb("b1_t", [P, PAIRS])
        w2_s = sb("w2_s", [P, PAIRS, D])
        b2_r = sb("b2_r", [9 * MOE, 3, D])
        b2_s = sb("b2_s", [9 * MOE, D], BF16)
        third = sb("third", [9 * MOE, 3])
        first_w = sb("first_w", [P, MOE])
        sel = sb("sel", [3 * MOE, PAIRS, P], BF16)

        area = region("area_x", 2 * (NPATCH + 1) * Q4 * V)
        xs = [part(area, i * (NPATCH + 1) * Q4 * V, [P, NPATCH + 1, Q4, V]) for i in range(2)]
        hilb = part(area, 0, [P, 3 * L])
        fwd = part(area, 3 * L, [P, NBLK, P])
        inv = part(area, 3 * L + NBLK * P, [P, NBLK, P])

        staged_odd = part(area, 0, [HID, GPB, HID + 1])

        area = region("area_g", GPB * (HID + 1))
        w1_f = part(area, 0, [P, MOE, D])
        sel_f = part(area, MOE * D, [3 * MOE, PAIRS, P])
        staged = [part(area, 0, [HID, GPB, HID + 1]), staged_odd]
        gate_t = [part(area, i * L // 2, [9 * MOE, L], BF16) for i in range(2)]
        split = part(area, L, [P, 2 * SLOTS, 9 * MOE], BF16)

        area = region("area_w", 4096)
        tokw = part(area, 0, [OSTACK * RF, D // OSTACK, C])
        wr_raw = part(area, 0, [HID, LAYERS * EXPERTS, HID])
        k_spec = part(area, 0, [P, SETS, 2, D])
        k_mul = [part(area, (2 + i) * SETS * D, [P, SETS, D]) for i in range(2)]
        even = part(area, 0, [P, SETS, PC])
        odd = part(area, SETS * PC, [P, SETS, PC])
        prod_a = [part(area, 7 * SETS * D + i * 2 * PC, [P, 2, PC]) for i in range(2)]
        prod_b = [part(area, 7 * SETS * D + (2 + i) * 2 * PC, [P, 2, PC]) for i in range(2)]
        k_abd = part(area, 4 * SETS * D, [P, SETS, 3, D])
        result = [part(area, i * 512, [P, SLOTS, D]) for i in range(2)]

        area = region("area_t", LAYERS * (EXPERTS + 1) * (HID + 1))
        row_e = part(area, 0, [P, NS, P])
        table = part(area, 0, [HID, LAYERS, EXPERTS + 1, HID + 1])
        gelu = [part(area, i * L, [P, L]) for i in range(2)]
        gated = [part(area, (2 + i) * L, [P, L]) for i in range(2)]

        area = region("area_a", 4096)
        row_y = part(area, 0, [P, NS, P])
        att = [part(area, i * L, [P, L]) for i in range(4)]
        fly = part(area, 0, [P, 16, PC])
        xr = part(area, 16 * PC, [P, NX, PC])
        k_time = part(area, 28 * PC, [P, L // P, 1, D])

        area = region("area_b", 4096)
        par_raw = part(area, 0, [D, 4, 4, NS])
        row_z = part(area, 0, [P, NS, P])
        beta = part(area, 0, [P, NS, P])
        hid = [part(area, i * L, [HID, L]) for i in range(2)]
        hid_in = [part(area, (2 + i) * L, [HID, L]) for i in range(2)]
        vec_centred = part(area, L, [P, SLOTS, D])
        y_time = part(area, 0, [P, L // P, PC])

        area = region("area_s", 32 * PC + 6 * 2 * SLOTS * MOE)
        col_y = part(area, 0, [P, NS, NCOL])
        col_e = part(area, NS * NCOL, [P, NS, NCOL])
        col_tab = part(area, 2 * NS * NCOL, [P, 2, NS, NCOL])
        col_z = part(area, 4 * NS * NCOL, [P, 2, NS, NCOL])
        q_s = [part(area, i * 3 * L // 2, [P, 3, L], BF16) for i in range(2)]
        q_rest = part(area, 3 * L, [P, L])
        u = part(area, 0, [P, L // P, 2, D])
        y_spec = part(area, 8 * PC, [P, SETS, 2, PC])
        z = part(area, 20 * PC, [P, SETS, 2, PC])
        sm_d, sm_p, sm_key, sm_c, *sm_one = [
            part(area, 32 * PC + i * 2 * SLOTS * MOE, [P, 2 * SLOTS, MOE]) for i in range(6)]

        area = region("area_q", 2 * L)
        s_im = part(area, 0, [P, 2 * L // P, D])
        s_re = part(area, L, [P, L // P, D])
        k_fm = part(area, L + L // 2, [P, NT * P])
        parts = [part(area, i * L, [P, SLOTS, 2, 2, D], BF16) for i in range(2)]

        area = region("area_f", 2 * NT * P)
        tok_fm = [part(area, i * NT * P, [P, NT * P]) for i in range(2)]
        pv_fm = [part(area, i * NT * P, [P, NT * P]) for i in range(2)]
        moe_fm = [part(area, i * NT * P, [P, NT * P]) for i in range(2)]

        h = sb("h", [P, B, SLOTS, D])
        mean = sb("mean", [P, B, SLOTS])
        var = sb("var", [P, B, SLOTS])
        minus_half = sb("minus_half", [P, 2, SLOTS])
        rstd = sb("rstd", [P, B, SLOTS])
        stat = sb("stat", [P, SLOTS, 6])
        st = [sb(f"st{i}", [P, SLOTS]) for i in range(5)]
        fm = [sb(f"fm{i}", [P, 2, L], BF16) for i in range(B)]
        parts_first = sb("parts_first", [P, SLOTS, 2, 2, D], BF16)
        dc = sb("dc", [1, D])
        centred = sb("centred", [P, SLOTS, D])
        ln_t = sb("ln", [P, B, SLOTS, D])
        ln = [ln_t[:, i] for i in range(B)]
        ln_rest = sb("ln_rest", [P, SLOTS, D])

        par_t = sb("par_t", [P, 4, NS])
        lam = sb("lam", [P, NS])
        turns = sb("turns", [P, NS])
        small = [sb(f"small{i}", [P, NS]) for i in range(6)]
        sm_r = [sb(f"sm_r{i}", [P, 2 * SLOTS]) for i in range(5)]

        wide_t = ctx.enter_context(nc.psum_tensor("wide", [P, 2, 2 * 512], F32))
        wide = [wide_t[:, i] for i in range(2)]
        turn_t = ctx.enter_context(nc.psum_tensor("turn", [P, 2, 512], F32))
        turn = [turn_t[:, i] for i in range(2)]
        turn_b = [turn_t[:, i].bitcast(BF16) for i in range(2)]
        turn_all = turn_t[:].rearrange("p x k -> p (x k)")
        acc_t = ctx.enter_context(nc.psum_tensor("acc", [P, 2, 512], F32))
        acc = [acc_t[:, i] for i in range(2)]
        acc_b = [acc_t[:, i].bitcast(BF16) for i in range(2)]

        ld_tok, ld_attn, ld_ffn, ld_ssm, ld_conv, ld_moe = (
            sem(n) for n in ("ld_tok", "ld_attn", "ld_ffn", "ld_ssm", "ld_conv", "ld_moe"))
        res_stored = [sem(f"res_stored{i}") for i in range(2)]
        x_in = [sem(f"x_in{i}") for i in range(2)]
        ve, ae, ge = sem("dve_step"), sem("act_step"), sem("pool_step")
        s = {n: sem(n) for n in (
            "weff_mm", "weff_ready", "tok_mm", "tok_copied", "tok_turned", "h_ready", "stats_ready",
            "ln_ready", "top_ready", "parts_ready", "ln_turned", "fm_a_ready", "fm_b_ready", "weights_split",
            "ident_ready", "q_top",
            "q_mm", "q_ready", "score_mm", "att_ready", "pv_step", "pv_copied", "pv_turned",
            "wgt_turned", "wgt_ready", "route_ready", "staged_ready", "bo_added",
            "hid_mm", "hid_relu", "bias_added", "ffn_mm",
            "par_turned", "tab_mul", "exp_in", "exp_out", "sin_in", "sin_out",
            "s_mm", "s_ready", "hil_mm", "hil_copied", "k_turned", "k_ready", "k_fly", "k_dft",
            "k_spec_ready", "k_mul_ready", "u_odd", "u_even", "u_dft", "u_prod", "y_ready", "z_mm",
            "z_copied", "even_ready", "route_mm", "sm_in", "sm_exp", "split_ready", "gate_turned",
            "gate_ready", "up_mm", "gelu_ready", "gate_mm", "gated_ready", "down_mm", "moe_copied",
            "moe_turned", "res_ready", "beta_ready", "alpha_ready", "small_turned",
            "moe_bias_ready", "staged_more", "staged_act", "first_mm", "moe_ln", "rstd_ready",
            "u_tokens", "y_time_ready", "odd_added")}
        block = ctx.enter_context(nc.Block())
        WGT_TILES = LAYERS * EXPERTS // 8

        def route_words(engine, b, first, end):
            return {w: engine.value_load(route_e[0:1, b * (GPB // PACK) + w:b * (GPB // PACK) + w + 1], min_val=0,
                                         max_val=2 ** (ROUTE_BITS * PACK) - 1)
                    for w in range(first // PACK, (end - 1) // PACK + 1)}

        def stage_experts(copy, words, b, layer, first, end):
            for g in range(first, end):
                e = (words[g // PACK] >> (ROUTE_BITS * (g % PACK))) & (2 ** ROUTE_BITS - 1)
                e = nc.s_assert_within(e, 0, EXPERTS, skip_runtime_bounds_check_because=
                                       "VectorE puts every route outside the experts to EXPERTS before it packs them")
                last = copy(staged[b % 2][:, g, :], table[:, layer, ds(e, 1), :].rearrange("d x h -> d (x h)"))
            return last

        UNITS = [(2 * q + par, layer) for q in range(2) for layer in range(LAYERS) for par in range(2)]

        def unit_staged(engine, unit):
            engine.wait_ge(s["staged_ready"], unit + 1)
            if unit >= 2:
                engine.wait_ge(s["staged_act"], unit - 1)
            if 2 <= unit < LAST_VEC:
                engine.wait_ge(s["staged_more"], unit - 1)

        wide_banks = [wide_t[:, r // 4, (r // 2 % 2) * 512 + (r % 2) * 256:(r // 2 % 2) * 512 + (r % 2) * 256 + 256]
                      for r in range(SETS)] + [wide_t[:, 1, 512:512 + 256]]
        turn_banks = [turn_t[:, r // 2, (r % 2) * 256:(r % 2) * 256 + 256] for r in range(4)] + wide_banks[2:4]
        fwd_banks = [turn_banks, wide_banks]

        @block.sync
        def _(sp):
            sp.dma_start(ident[:], c_ident).then_inc(ld_tok, 16)
            sp.dma_start(dft[:], c_dft).then_inc(ld_tok, 16)
            sp.dma_start(tokw[:], tok_w.rearrange("(k o) (r c) -> (o r) k c", o=OSTACK, c=C)).then_inc(ld_tok, 16)

            def load_x(b, par):
                src = x[b].rearrange("c (n h q) v -> h c n (q v)", h=2, q=Q4)
                edge = x[b, :, T_IN - 1:T_IN, :]
                for hh in range(2):
                    half = xs[par][hh * C:(hh + 1) * C]
                    sp.dma_start(half[:, 0:NPATCH].rearrange("c n q v -> c n (q v)"),
                                 src[hh]).then_inc(x_in[par], 16)
                    sp.dma_start(half[:, NPATCH], edge.to_broadcast([C, Q4, V])).then_inc(x_in[par], 16)

            for i, a in enumerate((a_re, a_im, c_re, c_im)):
                sp.dma_start(par_raw[:, i], a.unsqueeze(1).to_broadcast([D, 4, NS])).then_inc(ld_ssm, 16)
            for dst, src in ((ramp, c_ramp), (cols, c_cols), (off, c_off), (quarter, c_quarter)):
                sp.dma_start(dst[:], src).then_inc(ld_ssm, 16)
            load_x(0, 0)
            load_x(1, 1)
            for i in range(2):
                sp.dma_start(wq[i * D:(i + 1) * D], q_w.unsqueeze(1).to_broadcast([D, 2, D])).then_inc(ld_attn, 16)
            sp.wait_ge(s["tok_mm"], 1)
            load_x(2, 0)
            sp.wait_ge(s["tok_mm"], 2)
            load_x(3, 1)
            sp.wait_ge(s["weff_mm"], 1)
            sp.dma_start(wr_raw[:], wr.rearrange("l e h d -> h (l e) d")).then_inc(ld_ffn, 16)
            sp.dma_start(ws_raw[:], ws.rearrange("l s h d -> h (l s) d")).then_inc(ld_ffn, 16)
            for i in range(2):
                sp.dma_start(wi_raw[:, i], wi).then_inc(ld_ffn, 16)
            sp.dma_start(b_raw[0:LAYERS * EXPERTS], br.rearrange("l e h -> (l e) h")).then_inc(ld_ffn, 16)
            sp.dma_start(b_raw[LAYERS * EXPERTS:LAYERS * (EXPERTS + 1)],
                         bs.rearrange("l s h -> (l s) h")).then_inc(ld_ffn, 16)
            sp.dma_start(bi_c[:], bi.unsqueeze(1)).then_inc(ld_ffn, 16)
            sp.dma_start(wo_raw[:], wo).then_inc(ld_ffn, 16)
            sp.dma_start(bo_b[:], bo.unsqueeze(0).to_broadcast([P, D])).then_inc(ld_ffn, 16)
            sp.dma_start(route_i[:], route.unsqueeze(0)).then_inc(ld_ffn, 16)
            sp.wait_ge(s["tok_mm"], B)
            for dst, src in ((hilb, c_hilb), (fwd, c_fwd), (inv, c_inv), (phase, c_phase)):
                sp.dma_start(dst[:], src).then_inc(ld_conv, 16)
            sp.dma_start(dc[:], dvec.unsqueeze(0)).then_inc(ld_conv, 16)
            for i in range(2):
                sp.dma_start(rw_raw[:, i], router_w).then_inc(ld_moe, 16)
                sp.dma_start(w1_f[i * D:(i + 1) * D], w1.rearrange("e d f -> d e f")).then_inc(ld_moe, 16)
            sp.dma_start(b1_raw[:], b1.rearrange("(q e) f -> q (e f)", e=2)).then_inc(ld_moe, 16)
            sp.dma_start(w2_s[:], w2.rearrange("(q e) f o -> (e f) q o", e=2)).then_inc(ld_moe, 16)
            for i in range(9):
                sp.dma_start(b2_r[i * MOE:(i + 1) * MOE, 0], b2).then_inc(ld_moe, 16)
            sp.dma_start(first_w[:], c_first).then_inc(ld_moe, 16)
            sp.dma_start(sel_f[:], c_sel).then_inc(ld_moe, 16)
            sp.dma_start(third[:], c_third).then_inc(ld_moe, 16)
            for b in range(B):
                sp.wait_ge(s["res_ready"], b + 3)
                dst = out[b].rearrange("(v t p) d -> p t v d", v=NV, t=NT)
                res = result[b % 2].rearrange("p (t v) d -> p t v d", v=NV)
                for v in range(NV):
                    sp.dma_start(dst[:, :, v], res[:, :, v]).then_inc(res_stored[b % 2], 16)
            for par in range(2):
                sp.wait_ge(res_stored[par], 16 * NV * B // 2)

        @block.tensor
        def _(pe):
            def transposes(dst, src):
                for t in range(NT):
                    last = pe.transpose(dst[:, t * P:(t + 1) * P], src[:, t * P:(t + 1) * P], ident[:])
                return last

            def stack_tokens(n, par, own=None):
                pe.wait_ge(s["parts_ready"], n + 1)
                if n > 0 and own is None:
                    pe.wait_ge(s["fm_a_ready"], n)
                    pe.wait_ge(s["fm_b_ready"], n)
                tiles, src = own or turn_b, parts[par] if n else parts_first
                for m in range(SLOTS):
                    t, v = m // NV, m % NV
                    for i in range(2):
                        last = pe.transpose(tiles[i][:, (v * NT + t) * P:(v * NT + t + 1) * P],
                                            src[:, m, i].rearrange("p k d -> p (k d)"), ident_b[:])
                last.then_inc(s["ln_turned"], 1)

            def stacks_ready(n):
                pe.wait_ge(s["fm_a_ready"], n + 1)
                pe.wait_ge(s["fm_b_ready"], n + 1)

            def in_parts(dst, weight, tokens, swap=False):
                for i in range(3):
                    w, x = weight(i), tokens(i)
                    last = pe.matmul(dst, x if swap else w, w if swap else x, start=(i == 0), stop=(i == 2))
                return last

            def spectrum(out_of, src, n, done, residues=range(SETS)):
                for r in residues:
                    if r == 0:
                        for half in range(2):
                            cols_ = slice(half * 64, half * 64 + 64)
                            for part in range(2):
                                pe.matmul(out_of(0, part)[cols_], fwd[:, part, cols_], src[:, half, 0:n],
                                          start=True, stop=True)
                        continue
                    for part in range(2):
                        for k in range(2):
                            last = pe.matmul(out_of(r, part), fwd[:, 4 * r - 2 + 2 * part + k],
                                             src[:, 2 * r + k, 0:n], start=(k == 0), stop=(k == 1))
                    if r % 2:
                        last.then_inc(s[done], 1)

            pe.wait_ge(ld_tok, 16 * 3)
            width = OSTACK * PATCH
            for k in range(D // OSTACK):
                last = pe.matmul(wide[0][0:C, k * width:(k + 1) * width], tokw[:, k, :], dft[:], start=True, stop=True)
            last.then_inc(s["weff_mm"], 1)

            pe.wait_ge(ld_ssm, 16 * 8)
            for i in range(4):
                last = pe.transpose(wide[1][:, i * D:(i + 1) * D], par_raw[:, i].rearrange("d r n -> d (r n)"),
                                    ident[0:D, 0:D])
            last.then_inc(s["par_turned"], 1)
            pe.wait_ge(s["weff_ready"], 2)

            def embed(b):
                par = b % 2
                pe.wait_ge(x_in[par], 64 * (b // 2 + 1))
                pe.wait_ge(s["tok_copied"], b + 1)
                for k in range(2 * Q4):
                    q, lohi = k // 2, k % 2
                    for v in range(NV):
                        last = pe.matmul(acc[par][v * D:(v + 1) * D], weff[:, q, lohi, :],
                                         xs[par][:, lohi:lohi + NPATCH, q, v * 32:(v + 1) * 32],
                                         start=(k == 0), stop=(k == 2 * Q4 - 1))
                last.then_inc(s["tok_mm"], 1)

            def embedded_back(b):
                pe.wait_ge(s["tok_copied"], b + 3)
                pe.wait_ge(s["h_ready"], b + 1)
                transposes(turn[b % 2], tok_fm[b % 2]).then_inc(s["tok_turned"], 1)

            embed(0)
            embed(1)
            embedded_back(0)
            embedded_back(1)
            embed(2)
            embed(3)
            embedded_back(2)
            embedded_back(3)

            pe.wait_ge(s["beta_ready"], 1)
            pe.wait_ge(s["alpha_ready"], 1)
            for dd in range(NS):
                if dd == NS // 2:
                    pe.wait_ge(s["beta_ready"], 2)
                o0 = (dd % 8) * 2 * NTAB
                last = pe.matmul(wide_t[:, dd // 16, (dd // 8 % 2) * 512 + o0:(dd // 8 % 2) * 512 + o0 + 2 * NTAB],
                                 beta[:, dd, :], alpha[:, dd].rearrange("p x j -> p (x j)"), start=True, stop=True)
            last.then_inc(s["s_mm"], 1)

            pe.wait_ge(ld_ffn, 16 * 10)
            pe.wait_ge(s["h_ready"], B + 2)
            for i in range(LAYERS):
                last = pe.transpose(turn[0][:, i * HID:(i + 1) * HID], ws_raw[:, i], ident[:])
            pe.transpose(turn[0][:, 256:256 + HID], wi_raw[:].rearrange("h c d -> h (c d)"), ident[:])
            pe.transpose(turn[0][:, 384:384 + D], wo_raw[:], ident[0:D, 0:D])
            nb = LAYERS * (EXPERTS + 1)
            pe.transpose(turn[1][:, 0:nb], b_raw[0:nb], ident[0:nb, 0:nb]).then_inc(s["wgt_turned"], 1)

            def expert_weights(g):
                if g >= 2:
                    pe.wait_ge(s["wgt_ready"], g)
                for i in range(8):
                    last = pe.transpose(wide[g % 2][:, i * HID:(i + 1) * HID], wr_raw[:, g * 8 + i], ident[:])
                last.then_inc(s["wgt_turned"], 1)

            pe.wait_ge(s["s_ready"], 2)
            for g in range(WGT_TILES - 1):
                expert_weights(g)

            pe.wait_ge(s["s_ready"], 2)
            pe.wait_ge(ld_conv, 16 * 5)
            pe.wait_ge(s["tok_copied"], B + 2)
            for j in range(2 * L // P):
                for th in range(2):
                    x0 = 2 * L - P - j * P + th * 512
                    last = pe.matmul(acc[0][th * D:(th + 1) * D], s_im[:, j, :], hilb[:, x0:x0 + 512],
                                     start=(j == 0), stop=(j == 2 * L // P - 1))
            last.then_inc(s["hil_mm"], 1)
            pe.wait_ge(s["weights_split"], 1)
            pe.wait_ge(s["wgt_ready"], 1)
            stack_tokens(0, 0)
            pe.wait_ge(s["hil_copied"], 1)
            transposes(acc[1], k_fm).then_inc(s["k_turned"], 1)
            def query(b):
                par = b % 2
                stacks_ready(b)
                for c in range(2):
                    last = in_parts(turn[c], lambda i: wq_s[:, i], lambda i: fm[par][:, i // 2, c * 512:(c + 1) * 512])
                last.then_inc(s["q_mm"], 1)

            query(0)
            expert_weights(WGT_TILES - 1)
            pe.wait_ge(s["k_fly"], 2)
            spectrum(lambda r, part: wide[0][:, r * P + part * D:r * P + (part + 1) * D], xr, D, "k_dft")

            pe.wait_ge(ld_moe, 16 * 18)
            pe.wait_ge(s["k_ready"], 1)
            pe.transpose(acc[1][:, 0:MOE], rw_raw[:].rearrange("e c d -> e (c d)"), ident[0:MOE, 0:MOE])
            pe.transpose(acc[1][:, 16:16 + PAIRS], b1_raw[:], ident[0:PAIRS, 0:PAIRS]).then_inc(s["wgt_turned"], 1)

            pe.wait_ge(s["wgt_ready"], WGT_TILES + 2)
            pe.wait_ge(s["k_spec_ready"], 1)

            def scores(b, m):
                par, k0 = b % 2, (m % NV * NT + m // NV) * P
                pe.wait_ge(s["att_ready"], b * 8 + m + 1)
                for c in range(2):
                    last = in_parts(wide[m % 2][:, c * 512:(c + 1) * 512], lambda i: fm[par][:, i // 2, k0:k0 + P],
                                    lambda i: q_s[par][:, i, c * 512:(c + 1) * 512])
                last.then_inc(s["score_mm"], 1)

            def first_hidden(b):
                stacks_ready(b + B)
                for v in range(NV):
                    last = in_parts(turn[v], lambda i: wi_s[:, i], lambda i: fm[b % 2][:, i // 2, v * 512:(v + 1) * 512])
                last.then_inc(s["first_mm"], 1)

            def attention_back(b):
                pe.wait_ge(s["pv_copied"], b + 3)
                transposes(acc[b % 2], pv_fm[b % 2]).then_inc(s["pv_turned"], 1)

            for b in range(B):
                pe.wait_ge(s["q_ready"], b + 1)
                scores(b, 0)
                scores(b, 1)
                if b > 0:
                    attention_back(b - 1)
                if b >= 2:
                    pe.wait_ge(s["h_ready"], B + b + 1)
                for m in range(SLOTS):
                    pe.wait_ge(s["att_ready"], b * 8 + m + 3)
                    if m + 2 < SLOTS:
                        scores(b, m + 2)
                    for c in range(2):
                        last = pe.matmul(acc[b % 2][c * D:(c + 1) * D], ln[b][:, m, :],
                                         att[m % 4][:, c * 512:(c + 1) * 512],
                                         start=(m == 0), stop=(m == SLOTS - 1))
                    last.then_inc(s["pv_step"], 1)
                    if b + 1 < B and m == 2:
                        pe.wait_ge(s["q_ready"], b + 1)
                        stack_tokens(b + 1, (b + 1) % 2)
                    if b + 1 < B and m == 4:
                        query(b + 1)
                    if b + 1 == B and m == 2:
                        pe.wait_ge(s["q_ready"], B)
                        stack_tokens(B, 0)
                    if b + 1 == B and m == 4:
                        pe.wait_ge(s["weights_split"], 2)
                        first_hidden(0)
                    if b + 1 == B and m == 6:
                        pe.wait_ge(s["hid_relu"], 1)
                        stack_tokens(B + 1, 1)
            first_hidden(1)
            attention_back(B - 1)

            def hidden(unit, relus):
                b, par = UNITS[unit][0], UNITS[unit][0] % 2
                pe.wait_ge(s["hid_relu"], relus)
                unit_staged(pe, unit)
                if unit < 2:
                    pe.wait_ge(s["att_ready"], 8 * B + 2)
                else:
                    pe.wait_ge(s["bias_added"], unit + 1)
                for g in range(GPB):
                    last = pe.matmul(wide[par][:, g * GTOK:(g + 1) * GTOK], staged[par][:, g, 0:HID],
                                     hid[par][:, g * GTOK:(g + 1) * GTOK], start=True, stop=True)
                last.then_inc(s["hid_mm"], 1)

            def ffn_out(b, relus):
                par = b % 2
                pe.wait_ge(s["hid_relu"], relus)
                for m in range(SLOTS):
                    k0 = (m % NV * NT + m // NV) * P
                    last = pe.matmul(acc[par][:, m * D:(m + 1) * D], hid[par][:, k0:k0 + P], wo_t[:], start=True, stop=True)
                last.then_inc(s["ffn_mm"], 1)

            def forward(q, residues=range(SETS)):
                pe.wait_ge(s["u_odd"], q + 1)
                pe.wait_ge(s["u_even"], q + 1)
                spectrum(lambda r, part_: fwd_banks[q][r][:, part_ * PC:(part_ + 1) * PC], xr, PC, "u_dft", residues)

            def inverse(q):
                pe.wait_ge(s["y_ready"], q * SETS + 2)
                for half in range(2):
                    rows = slice(half * 64, half * 64 + 64)
                    for part_ in range(2):
                        last = pe.matmul(wide_banks[half * SETS][:, 0:PC], inv[rows, part_], y_spec[rows, 0, part_],
                                         start=(part_ == 0), stop=(part_ == 1))
                last.then_inc(s["z_mm"], 1)
                if q == 0:
                    pe.wait_ge(s["u_prod"], SETS)
                for r in range(1, SETS):
                    if r % 2 == 0:
                        pe.wait_ge(s["y_ready"], q * SETS + r + 2)
                    for part_ in range(2):
                        for k in range(2):
                            last = pe.matmul(wide_banks[r][:, part_ * PC:(part_ + 1) * PC], inv[:, 4 * r - 2 + 2 * part_ + k],
                                             y_spec[:, r, k], start=(k == 0), stop=(k == 1))
                    last.then_inc(s["z_mm"], 1)

            def route(q):
                stacks_ready(2 * q + 1 + 2 * B)
                for b in (2 * q, 2 * q + 1):
                    for k in range(SLOTS):
                        c0 = (b % 2 * SLOTS + k) * MOE
                        last = in_parts(turn[0][:, c0:c0 + MOE], lambda i: rw_s[:, i],
                                        lambda i: fm[b][:, i // 2, k * P:(k + 1) * P], swap=True)
                last.then_inc(s["route_mm"], 1)

            def gates_back(q):
                pe.wait_ge(s["split_ready"], q + 1)
                for par in range(2):
                    for k in range(SLOTS):
                        last = pe.transpose(turn_b[par][0:9 * MOE, k * P:(k + 1) * P],
                                            split[:, par * SLOTS + k, :], ident_b[:])
                    last.then_inc(s["gate_turned"], 1)

            def down(b, qd):
                par = b % 2
                pe.wait_ge(s["gated_ready"], b * PAIRS + qd + 3)
                for v in range(NV):
                    last = pe.matmul(acc[par][v * D:(v + 1) * D], w2_s[:, qd, :], gated[qd % 2][:, v * 512:(v + 1) * 512],
                                     start=(qd == 0), stop=False)
                if qd == PAIRS - 1:
                    for v in range(NV):
                        last = pe.matmul(acc[par][v * D:(v + 1) * D], b2_s[:], gate_t[par][:, v * 512:(v + 1) * 512],
                                         start=False, stop=True)
                last.then_inc(s["down_mm"], 1)

            def mixture_back(b):
                pe.wait_ge(s["moe_copied"], b + 1)
                transposes(acc[b % 2], moe_fm[b % 2]).then_inc(s["moe_turned"], 1)

            def mixture(b):
                par = b % 2
                for qd in range(PAIRS):
                    pe.wait_ge(s["gelu_ready"], b * PAIRS + qd + 1)
                    for v in range(NV):
                        last = in_parts(wide[0][:, v * 512:(v + 1) * 512], lambda i: w1_s[:, i, qd * P:(qd + 1) * P],
                                        lambda i: fm[b][:, i // 2, v * 512:(v + 1) * 512])
                    last.then_inc(s["up_mm"], 1)
                    if (b, qd) == (1, 2):
                        route(1)
                    if qd == 0:
                        if b > 0:
                            down(b - 1, PAIRS - 1)
                        if b == 2:
                            gates_back(1)
                        pe.wait_ge(s["gate_ready"], b + 1)
                    pe.wait_ge(s["gated_ready"], b * PAIRS + qd + 2)
                    for v in range(NV):
                        last = pe.matmul(wide[1][:, v * 512:(v + 1) * 512], sel[:, qd, :],
                                         gate_t[par][0:3 * MOE, v * 512:(v + 1) * 512], start=True, stop=True)
                    last.then_inc(s["gate_mm"], 1)
                    if qd == 0:
                        pe.wait_ge(s["res_ready"], b + 1)
                    else:
                        down(b, qd - 1)
                    if qd == 1 and b > 0:
                        mixture_back(b - 1)
                    if (b, qd) == (1, 0):
                        stack_tokens(2 * B + 2, 0)
                    if (b, qd) == (1, 1):
                        stack_tokens(2 * B + 3, 1)

            hidden(0, 1)
            hidden(1, 2)
            pe.wait_ge(s["hid_relu"], 2)
            stack_tokens(B + 2, 0)
            hidden(2, 3)
            hidden(3, 4)
            pe.wait_ge(s["h_ready"], 2 * B + 1)
            ffn_out(0, 5)
            first_hidden(2)
            pe.wait_ge(s["h_ready"], 2 * B + 2)
            ffn_out(1, 6)
            pe.wait_ge(s["hid_relu"], 7)
            stack_tokens(B + 3, 1)
            first_hidden(3)
            hidden(4, 7)
            hidden(5, 8)
            hidden(6, 9)
            forward(0, range(4))
            hidden(7, 10)
            pe.wait_ge(s["h_ready"], 2 * B + 3)
            ffn_out(2, 11)
            pe.wait_ge(s["bias_added"], 2 * B + 1)
            forward(0, range(4, SETS))
            pe.wait_ge(s["h_ready"], 2 * B + 4)
            ffn_out(3, 12)
            pe.wait_ge(s["bias_added"], 2 * B + 2)
            inverse(0)
            pe.wait_ge(s["z_copied"], SETS)
            forward(1)
            pe.wait_ge(s["weights_split"], 4)
            stack_tokens(2 * B, 0)
            stack_tokens(2 * B + 1, 1, acc_b)
            route(0)
            inverse(1)
            gates_back(0)
            pe.wait_ge(s["z_copied"], 2 * SETS)
            pe.wait_ge(s["moe_bias_ready"], 1)
            for b in range(B):
                mixture(b)
            down(B - 1, PAIRS - 1)
            mixture_back(3)

        @block.scalar
        def _(act):
            step = Steps(act, ae)
            act.sem_inc(s["tok_copied"], 2)
            act.sem_inc(s["att_ready"], 2)
            act.sem_inc(s["gelu_ready"], 1)

            act.wait_ge(s["weff_mm"], 1)
            for hh in range(2):
                src = wide[0][0:C].rearrange("c (o k h q) -> c h q k o", k=2, h=2, q=Q4)
                act.copy(weff[hh * C:(hh + 1) * C], src[:, hh]).then_inc(s["weff_ready"], 1)
            act.wait_ge(s["small_turned"], 1)
            act.activation(small[5][:], par_t[:, 0], ACT.Exp).then_inc(s["exp_out"], 1)

            def embedded_copy(b):
                act.wait_ge(s["tok_mm"], b + 1)
                act.copy(tok_fm[b % 2][:].rearrange("m (v n) -> m n v", n=NPATCH),
                         acc[b % 2].rearrange("m (n v) -> m n v", n=NPATCH)).then_inc(s["tok_copied"], 1)

            embedded_copy(0)
            embedded_copy(1)
            act.wait_ge(s["exp_in"], 1)
            act.activation(row_e[:], row_e[:], ACT.Exp).then_inc(s["exp_out"], 1)
            act.wait_ge(s["tab_mul"], 2)
            act.activation(col_e[:], col_e[:], ACT.Exp).then_inc(s["exp_out"], 1)
            act.wait_ge(s["sin_in"], 1)
            act.activation(row_z[:], row_z[:], ACT.Sin, scale=-TURN).then_inc(s["sin_out"], 1)
            act.wait_ge(s["sin_in"], 2)
            act.activation(col_tab[:], col_z[:], ACT.Sin, scale=-TURN).then_inc(s["sin_out"], 1)
            embedded_copy(2)
            embedded_copy(3)

            def top_parts(n, par, src, ready, of="ln_ready"):
                act.wait_ge(s[of], ready)
                if n >= 2:
                    act.wait_ge(s["ln_turned"], n - 1)
                dst = parts[par] if n else parts_first
                act.copy(dst[:, :, :, 0], src.unsqueeze(2).to_broadcast([P, SLOTS, 2, D])
                         ).then_inc(s["top_ready"], 1)

            top_parts(0, 0, ln[0], 2)

            def first_relu(b):
                act.wait_ge(s["first_mm"], b + 1)
                act.activation(hid[b % 2][:], turn_all, ACT.Relu, bias=bi_c[:, 0:1]).then_inc(s["hid_relu"], 1)

            def copy_b(n, par, to=None, tiles=turn_b):
                act.wait_ge(s["ln_turned"], n + 1)
                act.copy(fm[par if to is None else to][:, 1], tiles[1]).then_inc(s["fm_b_ready"], 1)

            def query_top(b):
                act.wait_ge(s["q_mm"], b + 1)
                act.copy(q_s[b % 2][:, 0], turn_all).then_inc(s["q_top"], 1)

            act.wait_ge(s["s_mm"], 1)
            n_im = 2 * L // P
            src = wide_t[:].rearrange("p x (y k) -> p (x y) k", k=512)[:, :, 0:16 * NTAB].rearrange(
                "p z (d e j) -> p e z d j", e=2, j=NTAB)
            for dst, j0, j1 in ((s_im, 0, n_im), (s_re, n_im, NTAB)):
                for dh in range(2):
                    to = dst.rearrange("p j (e z d) -> p e z d j", e=2, z=4)[:, dh]
                    last = act.copy(to, src[:, dh, :, :, j0:j1])
                last.then_inc(s["s_ready"], 1)
            act.wait_ge(s["hil_mm"], 1)
            act.copy(k_fm[:], acc[0]).then_inc(s["hil_copied"], 1)
            copy_b(0, 0)
            query_top(0)
            act.wait_ge(s["k_ready"], 1)
            act.wait_ge(s["k_dft"], SETS // 2)
            act.copy(k_spec[:].rearrange("p r c d -> p (r c d)"), wide[0][:, 0:SETS * 2 * D]).then_inc(s["k_spec_ready"], 1)
            for b in range(B):
                for m in range(SLOTS):
                    act.wait_ge(s["score_mm"], b * 8 + m + 1)
                    act.wait_ge(s["pv_step"], b * 8 + m + 1)
                    act.activation(att[m % 4][:], wide[m % 2], ACT.Sigmoid).then_inc(s["att_ready"], 1)
                    if b + 1 < B:
                        if m == 0:
                            top_parts(b + 1, (b + 1) % 2, ln[b + 1], b + 3)
                        if m == 3:
                            copy_b(b + 1, (b + 1) % 2)
                        if m == 5:
                            query_top(b + 1)
                    else:
                        if m == 0:
                            top_parts(B, 0, ln[0], B + 2)
                        if m == 1:
                            top_parts(B + 1, 1, ln[1], B + 3)
                        if m == 3:
                            copy_b(B, 0)
                        if m == 5:
                            first_relu(0)

            def next_relu(unit):
                act.wait_ge(s["bias_added"], unit + 3)
                par = unit % 2
                act.activation(hid[par][:], hid_in[par][:], ACT.Relu).then_inc(s["hid_relu"], 1)

            def relu_and_stage(unit):
                b, layer = UNITS[unit + 2]
                first = VEC_G if unit + 2 < LAST_VEC else POOL_G
                words = route_words(act, b, first, GPB)
                next_relu(unit)
                stage_experts(act.copy, words, b, layer, first, GPB).then_inc(s["staged_act"], 1)

            def copy_z(q):
                act.wait_ge(s["z_mm"], q * SETS + 2)
                act.copy(z[:, 0, 0], wide_banks[0][:, 0:PC])
                act.copy(z[:, 0, 1], wide_banks[SETS][:, 0:PC]).then_inc(s["z_copied"], 1)
                for r in range(1, SETS):
                    if r % 2 == 0:
                        act.wait_ge(s["z_mm"], q * SETS + r + 2)
                    act.copy(z[:, r].rearrange("p c n -> p (c n)"), wide_banks[r]).then_inc(s["z_copied"], 1)

            def gelus(b):
                for qd in range(PAIRS):
                    j = b * PAIRS + qd
                    act.wait_ge(s["up_mm"], j + 1)
                    act.wait_ge(s["gated_ready"], j + 1)
                    act.activation(gelu[qd % 2][:], wide[0], ACT.Gelu, bias=b1_t[:, qd:qd + 1]).then_inc(s["gelu_ready"], 1)
                    if (b, qd) == (0, 3):
                        top_parts(2 * B + 2, 0, ln[2], 3, "moe_ln")
                    if (b, qd) == (1, 0):
                        top_parts(2 * B + 3, 1, ln[3], 4, "moe_ln")
                        copy_b(2 * B + 2, 0, 2)
                    if (b, qd) == (1, 1):
                        copy_b(2 * B + 3, 1, 3)
                    if (b, qd) == (1, 2):
                        act.wait_ge(s["sm_in"], 2)
                        act.activation(sm_p, sm_d, ACT.Exp).then_inc(s["sm_exp"], 1)

            act.wait_ge(s["score_mm"], 8 * B)
            copy_b(B + 1, 1)
            first_relu(1)
            top_parts(B + 2, 0, ln[2], B + 4)
            relu_and_stage(0)
            relu_and_stage(1)
            copy_b(B + 2, 0)
            top_parts(B + 3, 1, ln[3], B + 5)
            relu_and_stage(2)
            relu_and_stage(3)
            first_relu(2)
            copy_b(B + 3, 1)
            first_relu(3)
            relu_and_stage(4)
            relu_and_stage(5)
            next_relu(6)
            next_relu(7)
            copy_z(0)
            for par in range(2):
                top_parts(2 * B + par, par, ln[par], par + 1, "moe_ln")
            copy_b(2 * B, 0, 0)
            copy_b(2 * B + 1, 1, 1, acc_b)
            act.wait_ge(s["sm_in"], 1)
            act.activation(sm_p, sm_d, ACT.Exp).then_inc(s["sm_exp"], 1)
            copy_z(1)
            gelus(0)
            gelus(1)
            gelus(2)
            gelus(3)

        @block.vector
        def _(dve):
            step = Steps(dve, ve)
            dve.sem_inc(s["h_ready"], 2)
            dve.sem_inc(s["pv_copied"], 2)
            dve.sem_inc(s["bias_added"], 2)
            dve.sem_inc(s["gated_ready"], 2)
            dve.sem_inc(s["stats_ready"], 1)
            dve.sem_inc(s["res_ready"], 2)

            def stats(b, hb, stage):
                dve.wait_ge(s["stats_ready"], b + stage * B + 1)
                for m in range(SLOTS):
                    last = dve.bn_stats(stat[:, m, :], hb[:, m, :])
                step.seq(last)
                dve.tensor_tensor(st[0][:], stat[:, :, 1], stat[:, :, 4], ALU.add)
                dve.tensor_tensor(st[1][:], stat[:, :, 1], stat[:, :, 4], ALU.subtract)
                step.seq(dve.tensor_tensor(st[2][:], stat[:, :, 2], stat[:, :, 5], ALU.add))
                dve.tensor_scalar(mean[:, b], st[0][:], 0.5, None, ALU.mult)
                step.seq(dve.tensor_tensor(st[3][:], st[1][:], st[1][:], ALU.mult))
                step.seq(dve.scalar_tensor_tensor(st[4][:], st[3][:], D / 4.0, st[2][:], ALU.mult, ALU.add))
                dve.tensor_scalar(var[:, b], st[4][:], 1.0 / D, EPS, ALU.mult, ALU.add).then_inc(s["stats_ready"], 1)

            def odd_fly(src, dst, n):
                f = [fly[:, i, 0:n] for i in range(11)]
                o = [dst[:, i, 0:n] for i in range(NX)]
                tt, sst = dve.tensor_tensor, dve.scalar_tensor_tensor
                tt(f[0], src(0), src(6), ALU.subtract)
                tt(f[1], src(1), src(7), ALU.subtract)
                tt(f[4], src(2), src(4), ALU.subtract)
                step.seq(tt(f[5], src(2), src(4), ALU.add))
                tt(f[2], f[1], src(5), ALU.subtract)
                step.seq(tt(f[3], f[1], src(5), ALU.add))
                sst(f[6], f[4], 0.5, f[0], ALU.mult, ALU.add)
                tt(o[6], f[0], f[4], ALU.subtract)
                tt(o[7], f[3], src(3), ALU.subtract)
                step.seq(sst(f[7], f[3], 0.5, src(3), ALU.mult, ALU.add))
                tt(f[8], src(0), src(6), ALU.add)
                tt(f[9], src(1), src(7), ALU.add)
                step.seq(tt(f[10], src(2), src(5), ALU.subtract))
                tt(f[8], f[8], src(3), ALU.subtract)
                step.seq(tt(f[9], f[9], src(4), ALU.subtract))
                tt(o[5], f[9], f[10], ALU.add)
                step.seq(tt(f[10], f[9], f[10], ALU.subtract))
                tt(o[1], f[8], f[10], ALU.subtract)
                sst(o[4], f[10], 0.5, f[8], ALU.mult, ALU.add)
                sst(o[2], f[2], COS30, f[6], ALU.mult, ALU.add)
                sst(o[3], f[5], COS30, f[7], ALU.mult, ALU.add)
                sst(o[10], f[2], -COS30, f[6], ALU.mult, ALU.add)
                return sst(o[11], f[5], -COS30, f[7], ALU.mult, ALU.add)

            dve.wait_ge(s["par_turned"], 1)
            for dh in range(2):
                rows = slice(dh * 64, dh * 64 + 64)
                last = dve.tensor_copy(par_t[rows], wide[1][rows, 0:4 * D].rearrange(
                    "p (i x d) -> p i x d", i=4, x=2)[:, :, dh])
            last.then_inc(s["small_turned"], 1)
            dve.wait_ge(s["small_turned"], 1)
            step.seq(dve.tensor_scalar(small[0][:], par_t[:, 1], DT / (2 * math.pi), None, ALU.mult))
            step.seq(dve.tensor_scalar(small[1][:], small[0][:], ROUND, -ROUND, ALU.add, ALU.add))
            step.seq(dve.tensor_tensor(turns[:], small[0][:], small[1][:], ALU.subtract))
            dve.wait_ge(s["exp_out"], 1)
            dve.tensor_scalar(lam[:], small[5][:], -DT, None, ALU.mult).then_inc(s["tab_mul"], 1)
            step.seq(dve.tensor_tensor(row_y[:], ramp[:].unsqueeze(1).to_broadcast([P, NS, P]),
                                       over_last(turns[:], P), ALU.mult))
            step.seq(dve.tensor_scalar(row_y[:], row_y[:], quarter[:, 0:1], None, ALU.add))
            step.seq(dve.tensor_scalar(row_z[:], row_y[:], ROUND, -ROUND, ALU.add, ALU.add))
            dve.tensor_tensor(row_z[:], row_z[:], row_y[:], ALU.subtract).then_inc(s["sin_in"], 1)

            def by_col(i):
                return cols[:].unsqueeze(1).to_broadcast([P, NS, NCOL])
            dve.tensor_tensor(col_y[:], by_col(0), over_last(turns[:], NCOL), ALU.mult)
            step.seq(dve.tensor_tensor(col_e[:], by_col(0), over_last(lam[:], NCOL), ALU.mult))
            dve.sem_inc(s["tab_mul"], 1)
            for i in range(2):
                last = dve.tensor_tensor(col_tab[:, i], col_y[:], off[:, i].unsqueeze(1).to_broadcast([P, NS, NCOL]), ALU.add)
            step.seq(last)
            step.seq(dve.tensor_scalar(col_z[:], col_tab[:], ROUND, -ROUND, ALU.add, ALU.add))
            dve.tensor_tensor(col_z[:], col_z[:], col_tab[:], ALU.subtract).then_inc(s["sin_in"], 1)
            def embedded(b):
                dve.wait_ge(s["tok_turned"], b + 1)
                dve.tensor_copy(h[:, b], turn[b % 2].rearrange("p (s d) -> p s d", d=D)).then_inc(s["h_ready"], 1)
                dve.wait_ge(s["h_ready"], b + 3)
                stats(b, h[:, b], 0)

            embedded(0)
            embedded(1)
            dve.wait_ge(s["sin_out"], 2)
            dve.wait_ge(s["exp_out"], 3)
            c_r, c_i = par_t[:, 2], par_t[:, 3]
            d_r, d_i, z_r, q_r, q_i, w = (t[:] for t in small)
            e_last = col_e[:, :, NTAB]
            tt = dve.tensor_tensor
            tt(d_r, col_tab[:, 0, :, NTAB], e_last, ALU.mult)
            step.seq(tt(d_i, col_tab[:, 1, :, NTAB], e_last, ALU.mult))
            step.seq(dve.tensor_scalar(z_r, d_r, -1.0, 1.0, ALU.mult, ALU.add))
            tt(q_r, z_r, z_r, ALU.mult)
            step.seq(tt(q_i, d_i, d_i, ALU.mult))
            step.seq(tt(w, q_r, q_i, ALU.add))
            tt(q_r, c_r, z_r, ALU.mult)
            tt(q_i, c_i, d_i, ALU.mult)
            step.seq(dve.reciprocal(d_r, w))
            step.seq(tt(q_r, q_r, q_i, ALU.subtract))
            tt(q_i, c_r, d_i, ALU.mult)
            step.seq(tt(z_r, c_i, z_r, ALU.mult))
            step.seq(tt(q_i, q_i, z_r, ALU.add))
            tt(q_r, q_r, d_r, ALU.mult)
            step.seq(tt(q_i, q_i, d_r, ALU.mult))
            tt(col_z[:, 0, :, 0:NTAB], col_tab[:, 0, :, 0:NTAB], over_last(q_r, NTAB), ALU.mult)
            step.seq(tt(col_z[:, 1, :, 0:NTAB], col_tab[:, 1, :, 0:NTAB], over_last(q_i, NTAB), ALU.mult))
            step.seq(tt(col_y[:, :, 0:NTAB], col_z[:, 0, :, 0:NTAB], col_z[:, 1, :, 0:NTAB], ALU.subtract))
            dve.wait_ge(s["ident_ready"], 1)
            for dh in range(2):
                rows = slice(dh * 64, dh * 64 + 64)
                last = tt(alpha[rows, :, dh], col_y[rows, :, 0:NTAB], col_e[rows, :, 0:NTAB], ALU.mult)
            last.then_inc(s["alpha_ready"], 1)

            embedded(2)
            embedded(3)

            dve.wait_ge(ld_ffn, 16 * 10)
            dve.wait_ge(s["wgt_turned"], 1)
            dve.tensor_tensor(base_t[:], turn[0][:, 0:2 * HID].rearrange("d (l h) -> d l h", l=LAYERS),
                              ident[:].unsqueeze(1).to_broadcast([P, LAYERS, P]), ALU.add)
            dve.tensor_copy(wi_f[:], turn[0][:, 256:256 + HID])
            dve.tensor_copy(wo_t[:], turn[0][:, 384:384 + D])
            dve.tensor_copy(b_t[:, 0:LAYERS * (EXPERTS + 1)], turn[1][:, 0:LAYERS * (EXPERTS + 1)]).then_inc(s["wgt_ready"], 1)
            dve.wait_ge(s["wgt_ready"], 1)
            dve.wait_ge(s["beta_ready"], 2)
            for layer in range(LAYERS):
                shared = b_t[:, LAYERS * EXPERTS + layer:LAYERS * EXPERTS + layer + 1]
                dve.tensor_scalar(table[:, layer, 0:EXPERTS, HID], b_t[:, layer * EXPERTS:(layer + 1) * EXPERTS],
                                  shared, None, ALU.add)
                dve.tensor_copy(table[:, layer, EXPERTS, HID:HID + 1], shared)
                dve.tensor_copy(table[:, layer, EXPERTS, 0:HID], base_t[:, layer])
            step.seq(dve.tensor_copy(route_f[:], route_i[:]))
            dve.tensor_scalar(route_ok[:], route_f[:], 0.0, None, ALU.is_ge)
            dve.tensor_scalar(route_lo[:], route_f[:], float(EXPERTS - 1), None, ALU.is_le)
            step.seq(dve.tensor_scalar(route_x[:], route_f[:], float(-EXPERTS), None, ALU.add))
            step.seq(dve.tensor_tensor(route_ok[:], route_ok[:], route_lo[:], ALU.mult))
            step.seq(dve.tensor_tensor(route_x[:], route_x[:], route_ok[:], ALU.mult))
            step.seq(dve.tensor_scalar(route_x[:], route_x[:], float(EXPERTS), None, ALU.add))
            packed = route_x[:].rearrange("x (w k) -> x k w", k=PACK)
            word = route_lo[:, 0:GROUPS // PACK]
            step.seq(dve.tensor_copy(word, packed[:, PACK - 1]))
            for k in range(PACK - 2, -1, -1):
                step.seq(dve.scalar_tensor_tensor(word, word, float(2 ** ROUTE_BITS), packed[:, k], ALU.mult, ALU.add))
            dve.tensor_copy(route_e[:], word).then_inc(s["route_ready"], 1)
            def expert_table(g):
                layer, e0 = g // 2, (g % 2) * 8
                dve.wait_ge(s["wgt_turned"], g + 2)
                dve.tensor_tensor(table[:, layer, e0:e0 + 8, 0:HID], wide[g % 2].rearrange("d (e h) -> d e h", e=8),
                                  base_t[:, layer].unsqueeze(1).to_broadcast([P, 8, HID]), ALU.add).then_inc(s["wgt_ready"], 1)

            for g in range(WGT_TILES - 1):
                expert_table(g)

            def lower_parts(n, par, src, ready, of="ln_ready"):
                dve.wait_ge(s[of], ready)
                dve.wait_ge(s["top_ready"], n + 1)
                if n > 0:
                    dve.wait_ge(s["parts_ready"], n)
                dst = parts[par] if n else parts_first
                step.seq(dve.tensor_tensor(ln_rest[:], src, dst[:, :, 0, 0], ALU.subtract))
                step.seq(dve.tensor_copy(dst[:, :, 0, 1], ln_rest[:]))
                dve.tensor_tensor(dst[:, :, 1, 1], ln_rest[:], dst[:, :, 0, 1],
                                  ALU.subtract).then_inc(s["parts_ready"], 1)

            def copy_a(n, par, to=None, tiles=turn_b):
                dve.wait_ge(s["ln_turned"], n + 1)
                dve.tensor_copy(fm[par if to is None else to][:, 0], tiles[0]).then_inc(s["fm_a_ready"], 1)

            lower_parts(0, 0, ln[0], 2)

            copy_a(0, 0)
            dve.wait_ge(s["k_turned"], 1)
            dve.wait_ge(s["s_ready"], 2)
            dve.tensor_tensor(k_time[:].rearrange("p (v t) x d -> p t v (x d)", v=NV),
                              acc[1].rearrange("p (t v d) -> p t v d", t=NT, v=NV),
                              s_re[:].rearrange("p (v t) d -> p t v d", v=NV), ALU.add).then_inc(s["k_ready"], 1)
            dve.wait_ge(s["k_ready"], 1)
            def query_parts(b):
                q = q_s[b % 2]
                low, high = slice(0, D), slice(D, P)
                dve.wait_ge(s["q_top"], b + 1)
                if b > 0:
                    dve.wait_ge(s["q_ready"], b)
                step.seq(dve.tensor_tensor(q_rest, turn_all, q[:, 0], ALU.subtract))
                dve.tensor_copy(q[high, 2], q[high, 0])
                step.seq(dve.tensor_copy(q[:, 1], q_rest))
                dve.tensor_tensor(q[low, 2], q_rest[low], q[low, 1], ALU.subtract).then_inc(s["q_ready"], 1)

            def weighted(b):
                dve.wait_ge(s["pv_step"], b * 8 + 12)
                dve.tensor_copy(pv_fm[b % 2][:], acc[b % 2]).then_inc(s["pv_copied"], 1)

            def residual(b):
                dve.wait_ge(s["pv_turned"], b + 1)
                hb = h[:, b]
                dve.tensor_tensor(hb, acc[b % 2].rearrange("p (s d) -> p s d", d=D), hb, ALU.add).then_inc(s["h_ready"], 1)
                dve.wait_ge(s["h_ready"], b + B + 3)
                stats(b, hb, 1)

            odd_fly(lambda j: k_time[:, j].rearrange("p x d -> p (x d)"), xr, D).then_inc(s["k_fly"], 1)
            expert_table(WGT_TILES - 1)
            query_parts(0)
            dve.wait_ge(s["wgt_turned"], WGT_TILES + 2)
            dve.tensor_copy(rw_f[:], acc[1][:, 0:MOE])
            dve.tensor_copy(b1_t[:], acc[1][:, 16:16 + PAIRS]).then_inc(s["wgt_ready"], 1)

            for b in range(B):
                if b + 1 < B:
                    lower_parts(b + 1, (b + 1) % 2, ln[b + 1], b + 3)
                    copy_a(b + 1, (b + 1) % 2)
                    query_parts(b + 1)
                else:
                    lower_parts(B, 0, ln[0], B + 2)
                    copy_a(B, 0)
                    lower_parts(B + 1, 1, ln[1], B + 3)
                weighted(b)
                if b + 1 == B:
                    copy_a(B + 1, 1)
                residual(b)

            def add_bias(unit):
                par = unit % 2
                dve.wait_ge(s["hid_mm"], unit + 1)
                unit_staged(dve, unit)
                dve.tensor_tensor(hid_in[par][:].rearrange("h (g t) -> h g t", g=GPB),
                                  wide[par].rearrange("h (g t) -> h g t", g=GPB),
                                  over_last(staged[par][:, :, HID], GTOK), ALU.add).then_inc(s["bias_added"], 1)

            def bias_and_stage(unit):
                b, layer = UNITS[unit + 2]
                words = route_words(dve, b, POOL_G, VEC_G)
                add_bias(unit)
                dve.wait_ge(s["bias_added"], unit + 3)
                stage_experts(dve.tensor_copy, words, b, layer, POOL_G, VEC_G).then_inc(s["staged_more"], 1)

            def ffn_residual(b):
                dve.wait_ge(s["ffn_mm"], b + 1)
                dve.wait_ge(s["bo_added"], b + 1)
                hb = h[:, b]
                dve.tensor_tensor(hb, acc[b % 2].rearrange("p (s d) -> p s d", d=D), hb, ALU.add).then_inc(s["h_ready"], 1)
                dve.wait_ge(s["h_ready"], b + 2 * B + 3)
                stats(b, hb, 2)

            def forward_odd(q):
                if q == 0:
                    dve.wait_ge(s["ln_ready"], 2 * B + 3)
                else:
                    dve.wait_ge(s["u_tokens"], 2)
                    dve.wait_ge(s["u_dft"], SETS // 2)
                odd_fly(lambda j: u[:, j].rearrange("p b d -> p (b d)"), xr, PC).then_inc(s["u_odd"], 1)

            def products(q, residues):
                dve.wait_ge(s["k_mul_ready"], 1)
                for r in residues:
                    dve.wait_ge(s["u_dft"], q * SETS // 2 + r // 2 + 1)
                    if q * SETS + r >= 2:
                        dve.wait_ge(s["y_ready"], q * SETS + r - 1)
                    src = fwd_banks[q][r]
                    for part_ in range(2):
                        dve.tensor_tensor(prod_a[r % 2][:, part_].rearrange("p (b d) -> p b d", b=2),
                                          src[:, part_ * PC:(part_ + 1) * PC].rearrange("p (b d) -> p b d", b=2),
                                          k_abd[:, r, part_].unsqueeze(1).to_broadcast([P, 2, D]), ALU.mult)
                    dve.tensor_tensor(prod_b[r % 2][:].rearrange("p c (b d) -> p (c b) d", b=2),
                                      src.rearrange("p (c b d) -> p (c b) d", c=2, b=2),
                                      k_abd[:, r, 2].unsqueeze(1).to_broadcast([P, 4, D]), ALU.mult).then_inc(s["u_prod"], 1)

            def inverse_odd(q):
                dve.wait_ge(s["z_copied"], (q + 1) * SETS)
                dve.wait_ge(s["u_odd"], 2)
                zr = [z[:, r, 0] for r in range(SETS)]
                zi = [z[:, r, 1] for r in range(SETS)]
                f = [fly[:, i] for i in range(11)]
                tt, sst = dve.tensor_tensor, dve.scalar_tensor_tensor
                tt(f[0], zr[1], zr[5], ALU.add)
                tt(f[1], zr[1], zr[5], ALU.subtract)
                tt(f[2], zi[1], zi[5], ALU.add)
                step.seq(tt(f[3], zi[1], zi[5], ALU.subtract))
                sst(f[4], f[2], 0.5, zi[3], ALU.mult, ALU.add)
                step.seq(sst(f[5], f[0], 0.5, zr[3], ALU.mult, ALU.subtract))
                tt(odd[:, 0], f[0], zr[3], ALU.add)
                sst(odd[:, 1], f[1], COS30, f[4], ALU.mult, ALU.subtract)
                sst(odd[:, 2], f[3], -COS30, f[5], ALU.mult, ALU.add)
                tt(odd[:, 3], zi[3], f[2], ALU.subtract)
                sst(odd[:, 4], f[3], -COS30, f[5], ALU.mult, ALU.subtract)
                step.seq(sst(odd[:, 5], f[1], -COS30, f[4], ALU.mult, ALU.subtract))

            def conv_tokens(b):
                ub = u[:, :, b % 2].rearrange("p (v t) d -> p v t d", v=NV)
                if b == 2:
                    dve.wait_ge(s["u_even"], 1)
                    dve.wait_ge(s["rstd_ready"], 1)
                else:
                    dve.wait_ge(s["u_tokens"], 1)
                    dve.wait_ge(s["rstd_ready"], 2)
                step.seq(dve.tensor_tensor(vec_centred, h[:, b], over_last(mean[:, b], D), ALU.subtract))
                r4 = rstd[:, b].rearrange("p (t v) -> p v t", v=NV).unsqueeze(3).to_broadcast([P, NV, NT, D])
                dve.tensor_tensor(ub, vec_centred.rearrange("p (t v) d -> p v t d", v=NV), r4, ALU.mult
                                  ).then_inc(s["u_tokens"], 1)

            def moe_tokens(b):
                dve.wait_ge(s["stats_ready"], b + 3 * B + 2)
                if b > 0:
                    dve.wait_ge(s["moe_ln"], b)
                step.seq(dve.tensor_tensor(vec_centred, h[:, b], over_last(mean[:, b], D), ALU.subtract))
                dve.wait_ge(s["rstd_ready"], b + 3)
                dve.tensor_tensor(ln[b], vec_centred, over_last(rstd[:, b], D), ALU.mult).then_inc(s["moe_ln"], 1)

            def in_time(q):
                dve.wait_ge(s["even_ready"], q + 1)
                dve.tensor_tensor(y_time[:, 0:6], even, odd, ALU.add)
                dve.tensor_tensor(y_time[:, 6:8], even[:, 0:2], odd[:, 0:2], ALU.subtract).then_inc(s["y_time_ready"], 1)
                dve.wait_ge(s["y_time_ready"], q + 1)

            def conv_residual(b):
                if b % 2 == 0:
                    y = y_time.rearrange("p (v t) (b d) -> p t v b d", v=NV, b=2)[:, :, :, 0]
                    h4 = h[:, b].rearrange("p (t v) d -> p t v d", v=NV)
                    dve.tensor_tensor(h4, h4, y, ALU.add).then_inc(s["h_ready"], 1)
                    dve.wait_ge(s["h_ready"], b // 2 + 3 * B + 3)
                else:
                    dve.wait_ge(s["odd_added"], b // 2 + 1)
                stats(b, h[:, b], 3)

            m1, m2, k1, tot, rec = (x_[:] for x_ in sm_r)

            def largest(src, top, one):
                weight = first_w[:].unsqueeze(1).to_broadcast([P, 2 * SLOTS, MOE])
                step.seq(dve.tensor_reduce(top, src, AX.X, ALU.max))
                step.seq(dve.tensor_tensor(sm_key, src, over_last(top, MOE), ALU.is_equal))
                step.seq(dve.tensor_tensor(sm_key, sm_key, weight, ALU.mult))
                step.seq(dve.tensor_reduce(k1, sm_key, AX.X, ALU.max))
                step.seq(dve.tensor_tensor(one, sm_key, over_last(k1, MOE), ALU.is_equal))

            def logits_less_max(q):
                dve.wait_ge(s["route_mm"], q + 1)
                logits = turn[0][:, 0:2 * SLOTS * MOE].rearrange("p (s e) -> p s e", e=MOE)
                step.seq(dve.tensor_reduce(m1, logits, AX.X, ALU.max))
                dve.tensor_tensor(sm_d, logits, over_last(m1, MOE), ALU.subtract).then_inc(s["sm_in"], 1)

            def probabilities(q):
                dve.wait_ge(s["sm_exp"], q + 1)
                step.seq(dve.tensor_reduce(tot, sm_p, AX.X, ALU.add))
                step.seq(dve.reciprocal(rec, tot))
                step.seq(dve.tensor_tensor(sm_p, sm_p, over_last(rec, MOE), ALU.mult))

            def top_first():
                largest(sm_p, m1, sm_one[0])

            def top_second():
                step.seq(dve.scalar_tensor_tensor(sm_d, sm_one[0], -2.0, sm_p, ALU.mult, ALU.add))
                largest(sm_d, m2, sm_one[1])

            def gates():
                dve.tensor_tensor(sm_one[0], sm_one[0], sm_one[1], ALU.add)
                step.seq(dve.tensor_tensor(tot, m1, m2, ALU.add))
                step.seq(dve.tensor_scalar(tot, tot, 1e-12, None, ALU.max))
                dve.tensor_tensor(sm_c, sm_one[0], sm_p, ALU.mult)
                step.seq(dve.reciprocal(rec, tot))
                step.seq(dve.tensor_tensor(sm_c, sm_c, over_last(rec, MOE), ALU.mult))
                step.seq(dve.tensor_copy(split[:, :, 0:MOE], sm_c))
                step.seq(dve.tensor_tensor(sm_key, sm_c, split[:, :, 0:MOE], ALU.subtract))
                step.seq(dve.tensor_copy(split[:, :, MOE:2 * MOE], sm_key))
                step.seq(dve.tensor_tensor(split[:, :, 2 * MOE:3 * MOE], sm_key, split[:, :, MOE:2 * MOE],
                                           ALU.subtract))
                dve.tensor_copy(split[:, :, 3 * MOE:].rearrange("p s (k e) -> p s k e", k=2),
                                split[:, :, 0:3 * MOE].unsqueeze(2).to_broadcast([P, 2 * SLOTS, 2, 3 * MOE])
                                ).then_inc(s["split_ready"], 1)

            def gates_copied(b):
                dve.wait_ge(s["gate_turned"], b + 1)
                dve.tensor_copy(gate_t[b % 2], turn_b[b % 2][0:9 * MOE]).then_inc(s["gate_ready"], 1)

            def gate_hidden(b, qd):
                j = b * PAIRS + qd
                dve.wait_ge(s["gelu_ready"], j + 2)
                dve.wait_ge(s["gate_mm"], j + 1)
                dve.wait_ge(s["down_mm"], j + 1)
                dve.tensor_tensor(gated[qd % 2][:], gelu[qd % 2][:], wide[1], ALU.mult).then_inc(s["gated_ready"], 1)

            def mixture_copied(b):
                dve.wait_ge(s["down_mm"], (b + 1) * PAIRS + 2)
                dve.tensor_copy(moe_fm[b % 2], acc[b % 2]).then_inc(s["moe_copied"], 1)

            def result_of(b):
                dve.wait_ge(s["moe_turned"], b + 1)
                dve.wait_ge(s["bo_added"], b + B + 1)
                if b >= 2:
                    dve.wait_ge(res_stored[b % 2], 16 * NV * (b // 2))
                dve.tensor_tensor(result[b % 2][:], acc[b % 2].rearrange("p (s d) -> p s d", d=D), h[:, b],
                                  ALU.add).then_inc(s["res_ready"], 1)

            lower_parts(B + 2, 0, ln[2], B + 4)
            bias_and_stage(0)
            bias_and_stage(1)
            copy_a(B + 2, 0)
            lower_parts(B + 3, 1, ln[3], B + 5)
            bias_and_stage(2)
            bias_and_stage(3)
            ffn_residual(0)
            copy_a(B + 3, 1)
            ffn_residual(1)
            add_bias(4)
            forward_odd(0)
            add_bias(5)
            add_bias(6)
            products(0, range(4))
            add_bias(7)
            ffn_residual(2)
            products(0, range(4, SETS))
            ffn_residual(3)
            conv_tokens(2)
            conv_tokens(3)
            forward_odd(1)
            inverse_odd(0)
            products(1, range(2))
            in_time(0)
            conv_residual(0)
            conv_residual(1)
            moe_tokens(0)
            moe_tokens(1)
            for par in range(2):
                lower_parts(2 * B + par, par, ln[par], par + 1, "moe_ln")
            products(1, range(2, 3))
            copy_a(2 * B, 0, 0)
            products(1, range(3, 4))
            copy_a(2 * B + 1, 1, 1, acc_b)
            products(1, range(4, SETS))
            dve.wait_ge(ld_moe, 16 * 18)
            logits_less_max(0)
            probabilities(0)
            top_first()
            top_second()
            gates()
            gates_copied(0)
            gates_copied(1)
            inverse_odd(1)
            for b in range(B):
                for qd in range(PAIRS):
                    if (b, qd) == (1, 2):
                        logits_less_max(1)
                    gate_hidden(b, qd)
                    if b == 0 and qd == 0:
                        in_time(1)
                    if b == 0 and qd == 1:
                        conv_residual(2)
                    if b == 0 and qd == 2:
                        conv_residual(3)
                    if b == 0 and qd == 3:
                        lower_parts(2 * B + 2, 0, ln[2], 3, "moe_ln")
                    if b == 1 and qd == 0:
                        copy_a(2 * B + 2, 0, 2)
                        lower_parts(2 * B + 3, 1, ln[3], 4, "moe_ln")
                    if b == 1 and qd == 1:
                        copy_a(2 * B + 3, 1, 3)
                    if b == 1 and qd == 2:
                        probabilities(1)
                        top_first()
                    if b == 1 and qd == 3:
                        top_second()
                        gates()
                    if b > 0 and qd == 1:
                        result_of(b - 1)
                mixture_copied(b)
                if b == 1:
                    gates_copied(2)
                    gates_copied(3)
            result_of(B - 1)

        @block.gpsimd
        def _(pool):
            step = Steps(pool, ge)
            pool.sem_inc(s["pv_step"], 4)
            pool.sem_inc(s["down_mm"], 2)
            pool.sem_inc(s["ln_ready"], 1)
            tt = pool.tensor_tensor
            step.seq(pool.memset(minus_half[:], -0.5))

            def normalise(index, b, dst):
                pool.wait_ge(s["stats_ready"], index + 2)
                pool.wait_ge(s["ln_ready"], index + 1)
                tt(rstd[:, b], var[:, b], minus_half[:, 0], ALU.pow)
                step.seq(tt(centred[:], h[:, b], over_last(mean[:, b], D), ALU.subtract))
                return tt(dst, centred[:], over_last(rstd[:, b], D), ALU.mult)

            def even_fly(src, dst, n):
                f = [fly[:, 11 + i, 0:n] for i in range(5)]
                o = [dst[:, i, 0:n] for i in range(NX)]
                tt(f[0], src(0), src(6), ALU.add)
                step.seq(tt(f[1], src(1), src(7), ALU.add))
                tt(f[2], f[0], src(3), ALU.add)
                tt(f[3], f[1], src(4), ALU.add)
                step.seq(tt(f[4], src(2), src(5), ALU.add))
                step.seq(tt(f[0], f[3], f[4], ALU.add))
                tt(o[9], f[3], f[4], ALU.subtract)
                tt(o[0], f[2], f[0], ALU.add)
                step.seq(pool.tensor_scalar(f[1], f[0], -0.5, 0.0, ALU.mult, ALU.add))
                return tt(o[8], f[1], f[2], ALU.add)

            def split_weight(src, dst, count):
                low, high = slice(0, D), slice(D, P)
                step.seq(pool.tensor_copy(dst[:, 0], src))
                step.seq(pool.tensor_copy(dst[high, 2], dst[high, 0]))
                step.seq(tt(src, src, dst[:, 0], ALU.subtract))
                step.seq(pool.tensor_copy(dst[:, 1], src))
                tt(dst[low, 2], src[low], dst[low, 1], ALU.subtract).then_inc(s["weights_split"], 1)
                pool.wait_ge(s["weights_split"], count)

            pool.memset(alpha[:], 0.0).then_inc(s["ident_ready"], 1)
            pool.wait_ge(ld_tok, 16 * 3)
            pool.tensor_copy(ident_b[:], ident[:])
            pool.wait_ge(ld_attn, 16 * 2)
            split_weight(wq[:].rearrange("p c e -> p (c e)"), wq_s, 1)

            pool.wait_ge(s["tab_mul"], 1)
            tt(row_e[:], ramp[:].unsqueeze(1).to_broadcast([P, NS, P]), over_last(lam[:], P), ALU.mult).then_inc(s["exp_in"], 1)
            for b in range(2):
                normalise(b, b, ln[b]).then_inc(s["ln_ready"], 1)
            pool.wait_ge(s["exp_out"], 2)
            pool.wait_ge(s["sin_out"], 1)
            for half in (slice(0, NS // 2), slice(NS // 2, NS)):
                tt(beta[:, half], row_z[:, half], row_e[:, half], ALU.mult).then_inc(s["beta_ready"], 1)
            for b in range(2, B):
                normalise(b, b, ln[b]).then_inc(s["ln_ready"], 1)

            pool.wait_ge(s["k_ready"], 1)
            even_fly(lambda j: k_time[:, j].rearrange("p x d -> p (x d)"), xr, D).then_inc(s["k_fly"], 1)
            pool.wait_ge(s["k_spec_ready"], 1)
            for i, dst in enumerate((0, 2, 1)):
                step.wait()
                tt(k_mul[0][:], k_spec[:, :, 0], over_last(phase[:, 2 * i], D), ALU.mult)
                step.seq(tt(k_mul[1][:], k_spec[:, :, 1], over_last(phase[:, 2 * i + 1], D), ALU.mult))
                step.done(tt(k_abd[:, :, dst], k_mul[0][:], k_mul[1][:], ALU.add))
            step.wait()
            pool.sem_inc(s["k_mul_ready"], 1)

            pool.wait_ge(s["wgt_ready"], WGT_TILES + 2)
            split_weight(wi_f[:], wi_s, 2)
            split_weight(rw_f[:], rw_s, 3)
            split_weight(w1_f[:].rearrange("p e f -> p (e f)"), w1_s, 4)
            pool.tensor_copy(sel[:], sel_f[:])
            for i in range(2):
                step.seq(pool.tensor_copy(b2_s[:], b2_r[:, i]))
                step.seq(tt(b2_r[:, i + 1], b2_r[:, i], b2_s[:], ALU.subtract))
            step.seq(tt(b2_r[:], b2_r[:], over_last(third[:], D), ALU.mult))
            step.seq(tt(b2_r[:, 0], b2_r[:, 0], b2_r[:, 1], ALU.add))
            tt(b2_s[:], b2_r[:, 0], b2_r[:, 2], ALU.add).then_inc(s["moe_bias_ready"], 1)

            def stage(unit):
                b, layer = UNITS[unit]
                end = POOL_G if unit >= 2 else GPB
                words = route_words(pool, b, 0, end)
                if unit >= 2:
                    pool.wait_ge(s["bias_added"], unit + 1)
                stage_experts(pool.tensor_copy, words, b, layer, 0, end).then_inc(s["staged_ready"], 1)

            def ffn_tokens(b):
                pool.wait_ge(s["pv_copied"], b + 3)
                normalise(b + B, b, ln[b]).then_inc(s["ln_ready"], 1)
                tt(h[:, b], h[:, b], bo_b[:].unsqueeze(1).to_broadcast([P, SLOTS, D]), ALU.add).then_inc(s["bo_added"], 1)

            def conv_tokens(b):
                ub = u[:, :, b % 2].rearrange("p (v t) d -> p v t d", v=NV)
                pool.wait_ge(s["stats_ready"], b + 2 * B + 2)
                tt(rstd[:, b], var[:, b], minus_half[:, 0], ALU.pow)
                pool.wait_ge(s["ln_ready"], b + 2 * B + 1)
                step.seq(tt(centred[:], h[:, b], over_last(mean[:, b], D), ALU.subtract))
                r4 = rstd[:, b].rearrange("p (t v) -> p v t", v=NV).unsqueeze(3).to_broadcast([P, NV, NT, D])
                tt(ub, centred[:].rearrange("p (t v) d -> p v t d", v=NV), r4, ALU.mult).then_inc(s["ln_ready"], 1)

            def deviation(b, stage):
                pool.wait_ge(s["stats_ready"], b + stage * B + 2)
                tt(rstd[:, b], var[:, b], minus_half[:, 0], ALU.pow).then_inc(s["rstd_ready"], 1)

            def forward_even(q):
                if q == 0:
                    pool.wait_ge(s["ln_ready"], 2 * B + 3)
                else:
                    pool.wait_ge(s["u_tokens"], 2)
                    pool.wait_ge(s["u_dft"], SETS // 2)
                even_fly(lambda j: u[:, j].rearrange("p b d -> p (b d)"), xr, PC).then_inc(s["u_even"], 1)

            def spectrum_sums(q, residues):
                for r in residues:
                    pool.wait_ge(s["u_prod"], q * SETS + r + 1)
                    if q:
                        pool.wait_ge(s["z_mm"], SETS)
                    a_, b_ = prod_a[r % 2], prod_b[r % 2]
                    if r == 0:
                        step.seq(tt(y_spec[:, r, 0], a_[:, 0], b_[:, 1], ALU.subtract))
                        y0 = y_spec[0:1, 0, 0].rearrange("p (b d) -> p b d", b=2)
                        step.seq(tt(y0, y0, dc[:].unsqueeze(1).to_broadcast([1, 2, D]), ALU.add))
                    else:
                        tt(y_spec[:, r, 0], a_[:, 0], b_[:, 1], ALU.subtract)
                    tt(y_spec[:, r, 1], b_[:, 0], a_[:, 1], ALU.add).then_inc(s["y_ready"], 1)

            def inverse_even(q):
                pool.wait_ge(s["z_copied"], (q + 1) * SETS)
                pool.wait_ge(s["u_even"], 2)
                if q:
                    pool.wait_ge(s["even_ready"], q)
                    pool.wait_ge(s["h_ready"], 3 * B + 3)
                z0, z2, z4 = z[:, 0, 0], z[:, 2, 0], z[:, 4, 0]
                y0, y2, y4 = z[:, 0, 1], z[:, 2, 1], z[:, 4, 1]
                f = [fly[:, 11 + i] for i in range(4)]
                tt(f[0], z0, z4, ALU.add)
                tt(f[1], z2, y0, ALU.add)
                pool.tensor_scalar(f[2], z4, -0.5, 0.0, ALU.mult, ALU.add)
                step.seq(pool.tensor_scalar(f[3], z2, 0.5, 0.0, ALU.mult, ALU.add))
                tt(even[:, 0], f[0], f[1], ALU.add)
                tt(even[:, 3], f[0], f[1], ALU.subtract)
                tt(f[2], f[2], z0, ALU.add)
                step.seq(tt(f[3], f[3], y0, ALU.subtract))
                tt(f[0], f[2], y4, ALU.subtract)
                tt(f[1], f[3], y2, ALU.subtract)
                tt(f[2], f[2], y4, ALU.add)
                step.seq(tt(f[3], f[3], y2, ALU.add))
                tt(even[:, 1], f[0], f[1], ALU.add)
                tt(even[:, 4], f[0], f[1], ALU.subtract)
                tt(even[:, 2], f[2], f[3], ALU.subtract)
                tt(even[:, 5], f[2], f[3], ALU.add).then_inc(s["even_ready"], 1)

            def odd_residual(q):
                pool.wait_ge(s["y_time_ready"], q + 1)
                y = y_time.rearrange("p (v t) (b d) -> p t v b d", v=NV, b=2)[:, :, :, 1]
                h4 = h[:, 2 * q + 1].rearrange("p (t v) d -> p t v d", v=NV)
                tt(h4, h4, y, ALU.add).then_inc(s["odd_added"], 1)

            def moe_tokens(b):
                deviation(b, 3)
                pool.wait_ge(s["rstd_ready"], b + 3)
                if b > 2:
                    pool.wait_ge(s["moe_ln"], b)
                step.seq(tt(centred[:], h[:, b], over_last(mean[:, b], D), ALU.subtract))
                tt(ln[b], centred[:], over_last(rstd[:, b], D), ALU.mult).then_inc(s["moe_ln"], 1)

            def moe_residual(b):
                tt(h[:, b], h[:, b], ln[b], ALU.add).then_inc(s["bo_added"], 1)

            pool.wait_ge(ld_conv, 16 * 5)
            step.seq(pool.tensor_scalar(dc[:], dc[:], float(NFFT), 0.0, ALU.mult, ALU.add))
            pool.wait_ge(s["route_ready"], 1)
            stage(0)
            ffn_tokens(0)
            stage(1)
            for b in range(1, B):
                ffn_tokens(b)
            for unit in range(2, 6):
                stage(unit)
            conv_tokens(0)
            conv_tokens(1)
            stage(6)
            forward_even(0)
            stage(7)
            spectrum_sums(0, range(SETS))
            deviation(2, 2)
            deviation(3, 2)
            forward_even(1)
            inverse_even(0)
            spectrum_sums(1, range(2))
            odd_residual(0)
            deviation(0, 3)
            deviation(1, 3)
            spectrum_sums(1, range(2, SETS))
            pool.wait_ge(s["moe_ln"], 2)
            moe_residual(0)
            moe_residual(1)
            inverse_even(1)
            odd_residual(1)
            moe_tokens(2)
            moe_tokens(3)
            pool.wait_ge(s["moe_ln"], B)
            moe_residual(2)
            moe_residual(3)


_INS = {
    "x": "x", "L0_tok_W": "tok_w", "L0_attn_q_weight": "q_w", "L0_ffn_route_id": "route", "L0_ffn_Wi": "wi",
    "L0_ffn_bi": "bi", "L0_ffn_Wr": "wr", "L0_ffn_br": "br", "L0_ffn_Ws": "ws", "L0_ffn_bs": "bs",
    "L0_ffn_Wo": "wo", "L0_ffn_bo": "bo", "L1_attn_A_real": "a_re", "L1_attn_A_imag": "a_im",
    "L1_attn_C_real": "c_re", "L1_attn_C_imag": "c_im", "L1_attn_D": "dvec", "L1_ffn_router_w": "router_w",
    "L1_ffn_w1": "w1", "L1_ffn_b1": "b1", "L1_ffn_w2": "w2", "L1_ffn_b2": "b2",
}


def kernel(**inputs):
    from concourse import bacc
    from concourse.bass_utils import run_bass_kernel_spmd

    nc = bacc.Bacc("TRN2", target_bir_lowering=False, num_devices=1)
    arrays, args = {}, {}
    for name, short in _INS.items():
        arrays["in_" + short] = np.ascontiguousarray(inputs[name])
    for name, a in constants().items():
        arrays["in_" + name] = np.ascontiguousarray(a)
    for name, a in arrays.items():
        args[name[3:]] = nc.dram_tensor(name, a.shape, mybir.dt.from_np(a.dtype), kind="ExternalInput").ap()
    args["out"] = nc.dram_tensor("out_0", (B, L, D), F32, kind="ExternalOutput").ap()
    build_tower(nc, **args)
    r = run_bass_kernel_spmd(nc, [arrays], core_ids=[0])
    return r.results[0]["out_0"]
```
